# Optimizing a Trainium2 kernel written in Bass

```python
import numpy as np
import jax
import jax.numpy as jnp

def _softmax(x, axis=-1):
    return jax.nn.softmax(x, axis=axis)

def _gelu(x):
    return jax.nn.gelu(x, approximate=True)

def _silu(x):
    return jax.nn.silu(x)

def _sigmoid(x):
    return jax.nn.sigmoid(x)

def _layernorm(x, axis=-1, eps=1e-05):
    m = jnp.mean(x, axis=axis, keepdims=True)
    v = jnp.var(x, axis=axis, keepdims=True)
    return (x - m) / jnp.sqrt(v + eps)

def _scatter_add(tgt, idx, src, axis=0):
    return tgt.at[idx].add(src)

def _segment_sum(src, seg, n):
    return jax.ops.segment_sum(src, seg, n)
kernel_name = 'mk_xattn_seq_d4_seqx_r4_b829f0'

def setup_inputs(seed: int=0):
    np.random.seed(seed)
    _w = jnp.asarray

    def _rec_inputs():
        import jax
        import jax.numpy as jnp
        _rk = jax.random.key(seed)
        x = 7.22e-05 + 1 * jax.random.normal(jax.random.fold_in(_rk, 1), (8, 100, 512), jnp.float32)
        _lenS = 100 - jax.random.randint(jax.random.fold_in(_rk, 7), (8,), 0, max(1, 100 // 4) + 1, jnp.int32)
        _lenS2 = 361 - jax.random.randint(jax.random.fold_in(_rk, 8), (8,), 0, max(1, 361 // 4) + 1, jnp.int32)
        _ctx_2048P = jax.random.normal(jax.random.fold_in(_rk, 11), (8, 16, 512), jnp.float32)
        _ctx_2048c = jax.random.dirichlet(jax.random.fold_in(_rk, 511), 0.3 * jnp.ones((16,), jnp.float32), (8, 361))
        _ctx_2048t = jnp.einsum('bsk,bkd->bsd', _ctx_2048c, _ctx_2048P)
        _ctx_2048t = _ctx_2048t * jax.lax.rsqrt(jnp.mean(jnp.square(_ctx_2048t)) + 1e-12) * 0.953939
        ctx_2048 = 4.13588e-05 + 0.999923 * (_ctx_2048t + 0.3 * jax.random.normal(jax.random.fold_in(_rk, 611), (8, 361, 512), jnp.float32))
        _validS = jnp.arange(100)[None, :] < _lenS[:, None]
        _validS2 = jnp.arange(361)[None, :] < _lenS2[:, None]
        _causal = jnp.tril(jnp.ones((100, 100), dtype=bool))
        mask_Bx1xSxS2_ff0 = jnp.where(jnp.ones((8, 1, 100, 361), dtype=bool), 0.0, -1000000000.0).astype(jnp.float32)
        return (x, ctx_2048, mask_Bx1xSxS2_ff0)
    x, ctx_2048, mask_Bx1xSxS2_ff0 = _rec_inputs()

    def _L0_xattn_setup():
        import jax, jax.numpy as jnp
        import numpy as np
        H = 512
        NH = 32
        KVH = 8
        HD = H // NH
        GROUPS = NH // KVH
        EPS = 1e-06
        B, L, S = (4, 256, 256)

        def _gqa_forward(hidden_state, encoder_hidden_state, encoder_attention_mask, Wq, bq, Wk, bk, Wv, bv, Wo, bo, gamma, beta):
            b, l, _ = hidden_state.shape
            s = encoder_hidden_state.shape[1]
            q = hidden_state @ Wq + bq
            k = encoder_hidden_state @ Wk + bk
            v = encoder_hidden_state @ Wv + bv
            q = q.reshape(b, l, KVH, GROUPS, HD).transpose(0, 2, 3, 1, 4)
            k = k.reshape(b, s, KVH, HD).transpose(0, 2, 1, 3)
            v = v.reshape(b, s, KVH, HD).transpose(0, 2, 1, 3)
            scale = 1.0 / jnp.sqrt(jnp.asarray(HD, q.dtype))
            scores = jnp.einsum('bkgld,bksd->bkgls', q, k) * scale
            scores = scores + encoder_attention_mask[:, :, None, :, :]
            attn = jax.nn.softmax(scores, axis=-1)
            out = jnp.einsum('bkgls,bksd->bkgld', attn, v)
            out = out.transpose(0, 3, 1, 2, 4).reshape(b, l, H)
            out = out @ Wo + bo
            x = out + hidden_state
            mu = jnp.mean(x, axis=-1, keepdims=True)
            var = jnp.var(x, axis=-1, keepdims=True)
            return (x - mu) * jax.lax.rsqrt(var + EPS) * gamma + beta
        key = jax.random.key(seed)
        ks = jax.random.split(key, 12)
        sd = 0.02
        return {'hidden_state': jax.random.normal(ks[0], (B, L, H), jnp.float32), 'encoder_hidden_state': jax.random.normal(ks[1], (B, S, H), jnp.float32), 'encoder_attention_mask': jnp.zeros((B, 1, L, S), jnp.float32), 'Wq': jax.random.normal(ks[2], (H, H), jnp.float32) * sd, 'bq': jnp.zeros((H,), jnp.float32), 'Wk': jax.random.normal(ks[3], (H, KVH * HD), jnp.float32) * sd, 'bk': jnp.zeros((KVH * HD,), jnp.float32), 'Wv': jax.random.normal(ks[4], (H, KVH * HD), jnp.float32) * sd, 'bv': jnp.zeros((KVH * HD,), jnp.float32), 'Wo': jax.random.normal(ks[5], (H, H), jnp.float32) * sd, 'bo': jnp.zeros((H,), jnp.float32), 'gamma': jnp.ones((H,), jnp.float32), 'beta': jnp.zeros((H,), jnp.float32)}
    _L0_xattn_all = _L0_xattn_setup()
    _L0_xattn_in = {k: v for k, v in _L0_xattn_all.items() if k in ('Wq', 'bq', 'Wk', 'bk', 'Wv', 'bv', 'Wo', 'bo', 'gamma', 'beta')}
    del _L0_xattn_all

    def _L1_xattn_setup():
        import jax, jax.numpy as jnp
        import numpy as np
        N_HEAD = 32
        EPS = 1e-05

        def _ln(x, w, b):
            m = jnp.mean(x, axis=-1, keepdims=True)
            v = jnp.mean((x - m) ** 2, axis=-1, keepdims=True)
            return (x - m) * jax.lax.rsqrt(v + EPS) * w + b

        def _forward(x, state, i, ln1_w, ln1_b, ln2_w, ln2_b, maa_x, maa_w, maa_k, maa_v, maa_r, maa_g, maa_w1, maa_w2, time_decay, decay_w1, decay_w2, faaaa, Wr, Wk, Wv, Wg, Wo, gn_w, gn_b, fmaa_k, fmaa_r, fWk, fWr, fWv):
            B, L, C = x.shape
            H = N_HEAD
            S = C // H
            i0 = (2 + S) * i
            xa = _ln(x, ln1_w, ln1_b)
            sx = jnp.concatenate([state[:, i0 + 1][:, None], xa[:, :-1]], axis=1) - xa
            xxx = xa + sx * maa_x
            t = jnp.tanh(xxx @ maa_w1).reshape(B, L, 5, -1)
            m = jnp.einsum('blfd,fdc->blfc', t, maa_w2)
            mw, mk, mv, mr, mg = (m[:, :, j] for j in range(5))
            xw = xa + sx * (maa_w + mw)
            xk = xa + sx * (maa_k + mk)
            xv = xa + sx * (maa_v + mv)
            xr = xa + sx * (maa_r + mr)
            xg = xa + sx * (maa_g + mg)
            w = time_decay + jnp.tanh(xw @ decay_w1) @ decay_w2
            w = jnp.exp(-jnp.exp(w)).reshape(B, L, H, S)
            r = (xr @ Wr.T).reshape(B, L, H, S)
            k = (xk @ Wk.T).reshape(B, L, H, S)
            v = (xv @ Wv.T).reshape(B, L, H, S)
            g = jax.nn.silu(xg @ Wg.T)
            s0 = state[:, i0 + 2:i0 + 2 + S].reshape(B, H, S, S)

            def step(s, inp):
                k_l, v_l, w_l, r_l = inp
                a = k_l[..., :, None] * v_l[..., None, :]
                out = jnp.einsum('bhs,bhst->bht', r_l, faaaa * a + s)
                s_new = a + w_l[..., None] * s
                return (s_new, out)
            seq = tuple((z.transpose(1, 0, 2, 3) for z in (k, v, w, r)))
            _, outs = jax.lax.scan(step, s0, seq)
            y = outs.transpose(1, 0, 2, 3)
            gm = jnp.mean(y, axis=-1, keepdims=True)
            gv = jnp.mean((y - gm) ** 2, axis=-1, keepdims=True)
            y = ((y - gm) * jax.lax.rsqrt(gv + EPS)).reshape(B, L, C) * gn_w + gn_b
            x = x + y * g @ Wo.T
            xc = _ln(x, ln2_w, ln2_b)
            sxc = jnp.concatenate([state[:, i0][:, None], xc[:, :-1]], axis=1) - xc
            xk2 = xc + sxc * fmaa_k
            xr2 = xc + sxc * fmaa_r
            rr = jax.nn.sigmoid(xr2 @ fWr.T)
            kk = jnp.square(jax.nn.relu(xk2 @ fWk.T))
            x = x + rr * (kk @ fWv.T)
            return x
        key = jax.random.key(seed)
        B, L, C, H = (8, 128, 512, N_HEAD)
        S = C // H
        DM, DD = (32, 64)
        ks = jax.random.split(key, 32)
        n = lambda k, shp, s=1.0: jax.random.normal(k, shp, dtype=jnp.float32) * s
        u = lambda k, shp: jax.random.uniform(k, shp, dtype=jnp.float32)
        inp = {'x': n(ks[0], (B, L, C)), 'state': n(ks[1], (B, 2 + S, C), 0.1), 'i': 0, 'ln1_w': jnp.ones((C,), jnp.float32), 'ln1_b': jnp.zeros((C,), jnp.float32), 'ln2_w': jnp.ones((C,), jnp.float32), 'ln2_b': jnp.zeros((C,), jnp.float32), 'maa_x': u(ks[2], (C,)), 'maa_w': u(ks[3], (C,)), 'maa_k': u(ks[4], (C,)), 'maa_v': u(ks[5], (C,)), 'maa_r': u(ks[6], (C,)), 'maa_g': u(ks[7], (C,)), 'maa_w1': n(ks[8], (C, 5 * DM), 0.02), 'maa_w2': n(ks[9], (5, DM, C), 0.02), 'time_decay': n(ks[10], (C,), 0.5), 'decay_w1': n(ks[11], (C, DD), 0.02), 'decay_w2': n(ks[12], (DD, C), 0.02), 'faaaa': n(ks[13], (H, S, 1), 0.1), 'Wr': n(ks[14], (C, C), 0.02), 'Wk': n(ks[15], (C, C), 0.02), 'Wv': n(ks[16], (C, C), 0.02), 'Wg': n(ks[17], (C, C), 0.02), 'Wo': n(ks[18], (C, C), 0.02), 'gn_w': jnp.ones((C,), jnp.float32), 'gn_b': jnp.zeros((C,), jnp.float32), 'fmaa_k': u(ks[19], (C,)), 'fmaa_r': u(ks[20], (C,)), 'fWk': n(ks[21], (C, C), 0.02), 'fWr': n(ks[22], (C, C), 0.02), 'fWv': n(ks[23], (C, C), 0.02)}
        return inp
    _L1_xattn_all = _L1_xattn_setup()
    _L1_xattn_in = {k: v for k, v in _L1_xattn_all.items() if k in ('ln1_w', 'ln1_b', 'ln2_w', 'ln2_b', 'maa_x', 'maa_w', 'maa_k', 'maa_v', 'maa_r', 'maa_g', 'maa_w1', 'maa_w2', 'time_decay', 'decay_w1', 'decay_w2', 'faaaa', 'Wr', 'Wk', 'Wv', 'Wg', 'Wo', 'gn_w', 'gn_b', 'fmaa_k', 'fmaa_r', 'fWk', 'fWr', 'fWv')}
    del _L1_xattn_all

    def _L2_xattn_setup():
        import jax, jax.numpy as jnp
        import numpy as np
        H = 512
        B, L, S = (4, 1024, 10)
        key = jax.random.key(seed)
        k1, k2, k3, k4, k5, k6 = jax.random.split(key, 6)
        scale = 1.0 / np.sqrt(H)
        return {'h_english': jax.random.normal(k1, (B, L, H), dtype=jnp.float32), 'h_lojban': jax.random.normal(k2, (B, S, H), dtype=jnp.float32), 'w_q': jax.random.normal(k3, (H, H), dtype=jnp.float32) * scale, 'w_k': jax.random.normal(k4, (H, H), dtype=jnp.float32) * scale, 'w_v': jax.random.normal(k5, (H, H), dtype=jnp.float32) * scale, 'w_o': jax.random.normal(k6, (H, H), dtype=jnp.float32) * scale, 'alpha': jnp.float32(0.1)}
    _L2_xattn_all = _L2_xattn_setup()
    _L2_xattn_in = {k: v for k, v in _L2_xattn_all.items() if k in ('w_q', 'w_k', 'w_v', 'w_o', 'alpha')}
    del _L2_xattn_all

    def _L3_xattn_setup():
        import jax, jax.numpy as jnp
        import numpy as np
        B, Q, S1, S2 = (4, 64, 512, 512)
        D, H, K, F = (512, 16, 128, 2048)
        LN_EPS = 1e-05

        def _layer_norm(x, scale, offset):
            mu = jnp.mean(x, axis=-1, keepdims=True)
            var = jnp.var(x, axis=-1, keepdims=True)
            return (x - mu) * jax.lax.rsqrt(var + LN_EPS) * scale + offset

        def _cross_attention(q_in, kv_in, wq, bq, wk, bk, wv, bv, wo, bo, bias_k, bias_v):
            b, q_len, _ = q_in.shape
            t = kv_in.shape[1]
            qh = (q_in @ wq + bq).reshape(b, q_len, H, K)
            kh = (kv_in @ wk + bk).reshape(b, t, H, K)
            vh = (kv_in @ wv + bv).reshape(b, t, H, K)
            kh = jnp.concatenate([kh, jnp.broadcast_to(bias_k, (b, 1, H, K))], axis=1)
            vh = jnp.concatenate([vh, jnp.broadcast_to(bias_v, (b, 1, H, K))], axis=1)
            scale = jnp.sqrt(jnp.asarray(K, q_in.dtype))
            logits = jnp.einsum('bqhk,bthk->bhqt', qh, kh) / scale
            weights = jax.nn.softmax(logits, axis=-1)
            ctx = jnp.einsum('bhqt,bthk->bqhk', weights, vh).reshape(b, q_len, H * K)
            return ctx @ wo + bo

        def _forward(x, xf_1, xf_2, ln1_scale, ln1_offset, wq1, bq1, wk1, bk1, wv1, bv1, wo1, bo1, bias_k1, bias_v1, ln2_scale, ln2_offset, wq2, bq2, wk2, bk2, wv2, bv2, wo2, bo2, bias_k2, bias_v2, ln_mlp_scale, ln_mlp_offset, w_fc1, b_fc1, w_fc2, b_fc2):
            res = x
            h = _layer_norm(x, ln1_scale, ln1_offset)
            x = res + _cross_attention(h, xf_1, wq1, bq1, wk1, bk1, wv1, bv1, wo1, bo1, bias_k1, bias_v1)
            res = x
            h = _layer_norm(x, ln2_scale, ln2_offset)
            x = res + _cross_attention(h, xf_2, wq2, bq2, wk2, bk2, wv2, bv2, wo2, bo2, bias_k2, bias_v2)
            h = _layer_norm(x, ln_mlp_scale, ln_mlp_offset)
            h = jax.nn.gelu(h @ w_fc1 + b_fc1, approximate=False) @ w_fc2 + b_fc2
            return x + h
        key = jax.random.key(seed)
        ks = iter(jax.random.split(key, 64))

        def rn(shape, s=0.02):
            return jax.random.normal(next(ks), shape, jnp.float32) * s
        inp = {'x': rn((B, Q, D), 1.0), 'xf_1': rn((B, S1, D), 1.0), 'xf_2': rn((B, S2, D), 1.0)}
        for i in (1, 2):
            inp[f'ln{i}_scale'] = jnp.ones((D,), jnp.float32)
            inp[f'ln{i}_offset'] = jnp.zeros((D,), jnp.float32)
            inp[f'wq{i}'] = rn((D, H * K))
            inp[f'bq{i}'] = jnp.zeros((H * K,), jnp.float32)
            inp[f'wk{i}'] = rn((D, H * K))
            inp[f'bk{i}'] = jnp.zeros((H * K,), jnp.float32)
            inp[f'wv{i}'] = rn((D, H * K))
            inp[f'bv{i}'] = jnp.zeros((H * K,), jnp.float32)
            inp[f'wo{i}'] = rn((H * K, D))
            inp[f'bo{i}'] = jnp.zeros((D,), jnp.float32)
            inp[f'bias_k{i}'] = rn((1, 1, H, K))
            inp[f'bias_v{i}'] = rn((1, 1, H, K))
        inp['ln_mlp_scale'] = jnp.ones((D,), jnp.float32)
        inp['ln_mlp_offset'] = jnp.zeros((D,), jnp.float32)
        inp['w_fc1'] = rn((D, F))
        inp['b_fc1'] = jnp.zeros((F,), jnp.float32)
        inp['w_fc2'] = rn((F, D))
        inp['b_fc2'] = jnp.zeros((D,), jnp.float32)
        return inp
    _L3_xattn_all = _L3_xattn_setup()
    _L3_xattn_in = {k: v for k, v in _L3_xattn_all.items() if k in ('ln1_scale', 'ln1_offset', 'wq1', 'bq1', 'wk1', 'bk1', 'wv1', 'bv1', 'wo1', 'bo1', 'bias_k1', 'bias_v1', 'ln2_scale', 'ln2_offset', 'wq2', 'bq2', 'wk2', 'bk2', 'wv2', 'bv2', 'wo2', 'bo2', 'bias_k2', 'bias_v2', 'ln_mlp_scale', 'ln_mlp_offset', 'w_fc1', 'b_fc1', 'w_fc2', 'b_fc2')}
    del _L3_xattn_all
    return {'x': x, 'ctx_2048': ctx_2048, 'mask_Bx1xSxS2_ff0': mask_Bx1xSxS2_ff0, 'L0_xattn_Wq': _L0_xattn_in['Wq'], 'L0_xattn_bq': _L0_xattn_in['bq'], 'L0_xattn_Wk': _L0_xattn_in['Wk'], 'L0_xattn_bk': _L0_xattn_in['bk'], 'L0_xattn_Wv': _L0_xattn_in['Wv'], 'L0_xattn_bv': _L0_xattn_in['bv'], 'L0_xattn_Wo': _L0_xattn_in['Wo'], 'L0_xattn_bo': _L0_xattn_in['bo'], 'L0_xattn_gamma': _L0_xattn_in['gamma'], 'L0_xattn_beta': _L0_xattn_in['beta'], 'L1_xattn_ln1_w': _L1_xattn_in['ln1_w'], 'L1_xattn_ln1_b': _L1_xattn_in['ln1_b'], 'L1_xattn_ln2_w': _L1_xattn_in['ln2_w'], 'L1_xattn_ln2_b': _L1_xattn_in['ln2_b'], 'L1_xattn_maa_x': _L1_xattn_in['maa_x'], 'L1_xattn_maa_w': _L1_xattn_in['maa_w'], 'L1_xattn_maa_k': _L1_xattn_in['maa_k'], 'L1_xattn_maa_v': _L1_xattn_in['maa_v'], 'L1_xattn_maa_r': _L1_xattn_in['maa_r'], 'L1_xattn_maa_g': _L1_xattn_in['maa_g'], 'L1_xattn_maa_w1': _L1_xattn_in['maa_w1'], 'L1_xattn_maa_w2': _L1_xattn_in['maa_w2'], 'L1_xattn_time_decay': _L1_xattn_in['time_decay'], 'L1_xattn_decay_w1': _L1_xattn_in['decay_w1'], 'L1_xattn_decay_w2': _L1_xattn_in['decay_w2'], 'L1_xattn_faaaa': _L1_xattn_in['faaaa'], 'L1_xattn_Wr': _L1_xattn_in['Wr'], 'L1_xattn_Wk': _L1_xattn_in['Wk'], 'L1_xattn_Wv': _L1_xattn_in['Wv'], 'L1_xattn_Wg': _L1_xattn_in['Wg'], 'L1_xattn_Wo': _L1_xattn_in['Wo'], 'L1_xattn_gn_w': _L1_xattn_in['gn_w'], 'L1_xattn_gn_b': _L1_xattn_in['gn_b'], 'L1_xattn_fmaa_k': _L1_xattn_in['fmaa_k'], 'L1_xattn_fmaa_r': _L1_xattn_in['fmaa_r'], 'L1_xattn_fWk': _L1_xattn_in['fWk'], 'L1_xattn_fWr': _L1_xattn_in['fWr'], 'L1_xattn_fWv': _L1_xattn_in['fWv'], 'L2_xattn_w_q': _L2_xattn_in['w_q'], 'L2_xattn_w_k': _L2_xattn_in['w_k'], 'L2_xattn_w_v': _L2_xattn_in['w_v'], 'L2_xattn_w_o': _L2_xattn_in['w_o'], 'L2_xattn_alpha': _L2_xattn_in['alpha'], 'L3_xattn_ln1_scale': _L3_xattn_in['ln1_scale'], 'L3_xattn_ln1_offset': _L3_xattn_in['ln1_offset'], 'L3_xattn_wq1': _L3_xattn_in['wq1'], 'L3_xattn_bq1': _L3_xattn_in['bq1'], 'L3_xattn_wk1': _L3_xattn_in['wk1'], 'L3_xattn_bk1': _L3_xattn_in['bk1'], 'L3_xattn_wv1': _L3_xattn_in['wv1'], 'L3_xattn_bv1': _L3_xattn_in['bv1'], 'L3_xattn_wo1': _L3_xattn_in['wo1'], 'L3_xattn_bo1': _L3_xattn_in['bo1'], 'L3_xattn_bias_k1': _L3_xattn_in['bias_k1'], 'L3_xattn_bias_v1': _L3_xattn_in['bias_v1'], 'L3_xattn_ln2_scale': _L3_xattn_in['ln2_scale'], 'L3_xattn_ln2_offset': _L3_xattn_in['ln2_offset'], 'L3_xattn_wq2': _L3_xattn_in['wq2'], 'L3_xattn_bq2': _L3_xattn_in['bq2'], 'L3_xattn_wk2': _L3_xattn_in['wk2'], 'L3_xattn_bk2': _L3_xattn_in['bk2'], 'L3_xattn_wv2': _L3_xattn_in['wv2'], 'L3_xattn_bv2': _L3_xattn_in['bv2'], 'L3_xattn_wo2': _L3_xattn_in['wo2'], 'L3_xattn_bo2': _L3_xattn_in['bo2'], 'L3_xattn_bias_k2': _L3_xattn_in['bias_k2'], 'L3_xattn_bias_v2': _L3_xattn_in['bias_v2'], 'L3_xattn_ln_mlp_scale': _L3_xattn_in['ln_mlp_scale'], 'L3_xattn_ln_mlp_offset': _L3_xattn_in['ln_mlp_offset'], 'L3_xattn_w_fc1': _L3_xattn_in['w_fc1'], 'L3_xattn_b_fc1': _L3_xattn_in['b_fc1'], 'L3_xattn_w_fc2': _L3_xattn_in['w_fc2'], 'L3_xattn_b_fc2': _L3_xattn_in['b_fc2']}

def reference(x, ctx_2048, mask_Bx1xSxS2_ff0, L0_xattn_Wq, L0_xattn_bq, L0_xattn_Wk, L0_xattn_bk, L0_xattn_Wv, L0_xattn_bv, L0_xattn_Wo, L0_xattn_bo, L0_xattn_gamma, L0_xattn_beta, L1_xattn_ln1_w, L1_xattn_ln1_b, L1_xattn_ln2_w, L1_xattn_ln2_b, L1_xattn_maa_x, L1_xattn_maa_w, L1_xattn_maa_k, L1_xattn_maa_v, L1_xattn_maa_r, L1_xattn_maa_g, L1_xattn_maa_w1, L1_xattn_maa_w2, L1_xattn_time_decay, L1_xattn_decay_w1, L1_xattn_decay_w2, L1_xattn_faaaa, L1_xattn_Wr, L1_xattn_Wk, L1_xattn_Wv, L1_xattn_Wg, L1_xattn_Wo, L1_xattn_gn_w, L1_xattn_gn_b, L1_xattn_fmaa_k, L1_xattn_fmaa_r, L1_xattn_fWk, L1_xattn_fWr, L1_xattn_fWv, L2_xattn_w_q, L2_xattn_w_k, L2_xattn_w_v, L2_xattn_w_o, L2_xattn_alpha, L3_xattn_ln1_scale, L3_xattn_ln1_offset, L3_xattn_wq1, L3_xattn_bq1, L3_xattn_wk1, L3_xattn_bk1, L3_xattn_wv1, L3_xattn_bv1, L3_xattn_wo1, L3_xattn_bo1, L3_xattn_bias_k1, L3_xattn_bias_v1, L3_xattn_ln2_scale, L3_xattn_ln2_offset, L3_xattn_wq2, L3_xattn_bq2, L3_xattn_wk2, L3_xattn_bk2, L3_xattn_wv2, L3_xattn_bv2, L3_xattn_wo2, L3_xattn_bo2, L3_xattn_bias_k2, L3_xattn_bias_v2, L3_xattn_ln_mlp_scale, L3_xattn_ln_mlp_offset, L3_xattn_w_fc1, L3_xattn_b_fc1, L3_xattn_w_fc2, L3_xattn_b_fc2):
    import jax
    import jax.numpy as jnp

    def _L0_xattn_ref(hidden_state, encoder_hidden_state, encoder_attention_mask, Wq, bq, Wk, bk, Wv, bv, Wo, bo, gamma, beta):
        import jax, jax.numpy as jnp
        import numpy as np
        H = 512
        NH = 32
        KVH = 8
        HD = H // NH
        GROUPS = NH // KVH
        EPS = 1e-06
        B, L, S = (4, 256, 256)

        def _gqa_forward(hidden_state, encoder_hidden_state, encoder_attention_mask, Wq, bq, Wk, bk, Wv, bv, Wo, bo, gamma, beta):
            b, l, _ = hidden_state.shape
            s = encoder_hidden_state.shape[1]
            q = hidden_state @ Wq + bq
            k = encoder_hidden_state @ Wk + bk
            v = encoder_hidden_state @ Wv + bv
            q = q.reshape(b, l, KVH, GROUPS, HD).transpose(0, 2, 3, 1, 4)
            k = k.reshape(b, s, KVH, HD).transpose(0, 2, 1, 3)
            v = v.reshape(b, s, KVH, HD).transpose(0, 2, 1, 3)
            scale = 1.0 / jnp.sqrt(jnp.asarray(HD, q.dtype))
            scores = jnp.einsum('bkgld,bksd->bkgls', q, k) * scale
            scores = scores + encoder_attention_mask[:, :, None, :, :]
            attn = jax.nn.softmax(scores, axis=-1)
            out = jnp.einsum('bkgls,bksd->bkgld', attn, v)
            out = out.transpose(0, 3, 1, 2, 4).reshape(b, l, H)
            out = out @ Wo + bo
            x = out + hidden_state
            mu = jnp.mean(x, axis=-1, keepdims=True)
            var = jnp.var(x, axis=-1, keepdims=True)
            return (x - mu) * jax.lax.rsqrt(var + EPS) * gamma + beta
        return _gqa_forward(hidden_state, encoder_hidden_state, encoder_attention_mask, Wq, bq, Wk, bk, Wv, bv, Wo, bo, gamma, beta)

    def _L1_xattn_ref(x, state, i, ln1_w, ln1_b, ln2_w, ln2_b, maa_x, maa_w, maa_k, maa_v, maa_r, maa_g, maa_w1, maa_w2, time_decay, decay_w1, decay_w2, faaaa, Wr, Wk, Wv, Wg, Wo, gn_w, gn_b, fmaa_k, fmaa_r, fWk, fWr, fWv):
        import jax, jax.numpy as jnp
        import numpy as np
        N_HEAD = 32
        EPS = 1e-05

        def _ln(x, w, b):
            m = jnp.mean(x, axis=-1, keepdims=True)
            v = jnp.mean((x - m) ** 2, axis=-1, keepdims=True)
            return (x - m) * jax.lax.rsqrt(v + EPS) * w + b

        def _forward(x, state, i, ln1_w, ln1_b, ln2_w, ln2_b, maa_x, maa_w, maa_k, maa_v, maa_r, maa_g, maa_w1, maa_w2, time_decay, decay_w1, decay_w2, faaaa, Wr, Wk, Wv, Wg, Wo, gn_w, gn_b, fmaa_k, fmaa_r, fWk, fWr, fWv):
            B, L, C = x.shape
            H = N_HEAD
            S = C // H
            i0 = (2 + S) * i
            xa = _ln(x, ln1_w, ln1_b)
            sx = jnp.concatenate([state[:, i0 + 1][:, None], xa[:, :-1]], axis=1) - xa
            xxx = xa + sx * maa_x
            t = jnp.tanh(xxx @ maa_w1).reshape(B, L, 5, -1)
            m = jnp.einsum('blfd,fdc->blfc', t, maa_w2)
            mw, mk, mv, mr, mg = (m[:, :, j] for j in range(5))
            xw = xa + sx * (maa_w + mw)
            xk = xa + sx * (maa_k + mk)
            xv = xa + sx * (maa_v + mv)
            xr = xa + sx * (maa_r + mr)
            xg = xa + sx * (maa_g + mg)
            w = time_decay + jnp.tanh(xw @ decay_w1) @ decay_w2
            w = jnp.exp(-jnp.exp(w)).reshape(B, L, H, S)
            r = (xr @ Wr.T).reshape(B, L, H, S)
            k = (xk @ Wk.T).reshape(B, L, H, S)
            v = (xv @ Wv.T).reshape(B, L, H, S)
            g = jax.nn.silu(xg @ Wg.T)
            s0 = state[:, i0 + 2:i0 + 2 + S].reshape(B, H, S, S)

            def step(s, inp):
                k_l, v_l, w_l, r_l = inp
                a = k_l[..., :, None] * v_l[..., None, :]
                out = jnp.einsum('bhs,bhst->bht', r_l, faaaa * a + s)
                s_new = a + w_l[..., None] * s
                return (s_new, out)
            seq = tuple((z.transpose(1, 0, 2, 3) for z in (k, v, w, r)))
            _, outs = jax.lax.scan(step, s0, seq)
            y = outs.transpose(1, 0, 2, 3)
            gm = jnp.mean(y, axis=-1, keepdims=True)
            gv = jnp.mean((y - gm) ** 2, axis=-1, keepdims=True)
            y = ((y - gm) * jax.lax.rsqrt(gv + EPS)).reshape(B, L, C) * gn_w + gn_b
            x = x + y * g @ Wo.T
            xc = _ln(x, ln2_w, ln2_b)
            sxc = jnp.concatenate([state[:, i0][:, None], xc[:, :-1]], axis=1) - xc
            xk2 = xc + sxc * fmaa_k
            xr2 = xc + sxc * fmaa_r
            rr = jax.nn.sigmoid(xr2 @ fWr.T)
            kk = jnp.square(jax.nn.relu(xk2 @ fWk.T))
            x = x + rr * (kk @ fWv.T)
            return x
        return _forward(x, state, i, ln1_w, ln1_b, ln2_w, ln2_b, maa_x, maa_w, maa_k, maa_v, maa_r, maa_g, maa_w1, maa_w2, time_decay, decay_w1, decay_w2, faaaa, Wr, Wk, Wv, Wg, Wo, gn_w, gn_b, fmaa_k, fmaa_r, fWk, fWr, fWv)

    def _L2_xattn_ref(h_english, h_lojban, w_q, w_k, w_v, w_o, alpha):
        import jax, jax.numpy as jnp
        import numpy as np
        H = 512
        B, L, S = (4, 1024, 10)
        h = h_english.shape[-1]
        q = jnp.einsum('blh,oh->blo', h_english, w_q)
        k = jnp.einsum('bsh,oh->bso', h_lojban, w_k)
        v = jnp.einsum('bsh,oh->bso', h_lojban, w_v)
        scores = jnp.einsum('blh,bsh->bls', q, k) / jnp.sqrt(jnp.float32(h))
        probs = jax.nn.softmax(scores, axis=-1)
        context = jnp.einsum('bls,bsh->blh', probs, v)
        delta = jnp.einsum('blh,oh->blo', context, w_o)
        return h_english + alpha * delta

    def _L3_xattn_ref(x, xf_1, xf_2, ln1_scale, ln1_offset, wq1, bq1, wk1, bk1, wv1, bv1, wo1, bo1, bias_k1, bias_v1, ln2_scale, ln2_offset, wq2, bq2, wk2, bk2, wv2, bv2, wo2, bo2, bias_k2, bias_v2, ln_mlp_scale, ln_mlp_offset, w_fc1, b_fc1, w_fc2, b_fc2):
        import jax, jax.numpy as jnp
        import numpy as np
        B, Q, S1, S2 = (4, 64, 512, 512)
        D, H, K, F = (512, 16, 128, 2048)
        LN_EPS = 1e-05

        def _layer_norm(x, scale, offset):
            mu = jnp.mean(x, axis=-1, keepdims=True)
            var = jnp.var(x, axis=-1, keepdims=True)
            return (x - mu) * jax.lax.rsqrt(var + LN_EPS) * scale + offset

        def _cross_attention(q_in, kv_in, wq, bq, wk, bk, wv, bv, wo, bo, bias_k, bias_v):
            b, q_len, _ = q_in.shape
            t = kv_in.shape[1]
            qh = (q_in @ wq + bq).reshape(b, q_len, H, K)
            kh = (kv_in @ wk + bk).reshape(b, t, H, K)
            vh = (kv_in @ wv + bv).reshape(b, t, H, K)
            kh = jnp.concatenate([kh, jnp.broadcast_to(bias_k, (b, 1, H, K))], axis=1)
            vh = jnp.concatenate([vh, jnp.broadcast_to(bias_v, (b, 1, H, K))], axis=1)
            scale = jnp.sqrt(jnp.asarray(K, q_in.dtype))
            logits = jnp.einsum('bqhk,bthk->bhqt', qh, kh) / scale
            weights = jax.nn.softmax(logits, axis=-1)
            ctx = jnp.einsum('bhqt,bthk->bqhk', weights, vh).reshape(b, q_len, H * K)
            return ctx @ wo + bo

        def _forward(x, xf_1, xf_2, ln1_scale, ln1_offset, wq1, bq1, wk1, bk1, wv1, bv1, wo1, bo1, bias_k1, bias_v1, ln2_scale, ln2_offset, wq2, bq2, wk2, bk2, wv2, bv2, wo2, bo2, bias_k2, bias_v2, ln_mlp_scale, ln_mlp_offset, w_fc1, b_fc1, w_fc2, b_fc2):
            res = x
            h = _layer_norm(x, ln1_scale, ln1_offset)
            x = res + _cross_attention(h, xf_1, wq1, bq1, wk1, bk1, wv1, bv1, wo1, bo1, bias_k1, bias_v1)
            res = x
            h = _layer_norm(x, ln2_scale, ln2_offset)
            x = res + _cross_attention(h, xf_2, wq2, bq2, wk2, bk2, wv2, bv2, wo2, bo2, bias_k2, bias_v2)
            h = _layer_norm(x, ln_mlp_scale, ln_mlp_offset)
            h = jax.nn.gelu(h @ w_fc1 + b_fc1, approximate=False) @ w_fc2 + b_fc2
            return x + h
        return _forward(x, xf_1, xf_2, ln1_scale, ln1_offset, wq1, bq1, wk1, bk1, wv1, bv1, wo1, bo1, bias_k1, bias_v1, ln2_scale, ln2_offset, wq2, bq2, wk2, bk2, wv2, bv2, wo2, bo2, bias_k2, bias_v2, ln_mlp_scale, ln_mlp_offset, w_fc1, b_fc1, w_fc2, b_fc2)
    x = _L0_xattn_ref(x, ctx_2048, mask_Bx1xSxS2_ff0, L0_xattn_Wq, L0_xattn_bq, L0_xattn_Wk, L0_xattn_bk, L0_xattn_Wv, L0_xattn_bv, L0_xattn_Wo, L0_xattn_bo, L0_xattn_gamma, L0_xattn_beta)
    x = _L1_xattn_ref(x, ctx_2048, 0, L1_xattn_ln1_w, L1_xattn_ln1_b, L1_xattn_ln2_w, L1_xattn_ln2_b, L1_xattn_maa_x, L1_xattn_maa_w, L1_xattn_maa_k, L1_xattn_maa_v, L1_xattn_maa_r, L1_xattn_maa_g, L1_xattn_maa_w1, L1_xattn_maa_w2, L1_xattn_time_decay, L1_xattn_decay_w1, L1_xattn_decay_w2, L1_xattn_faaaa, L1_xattn_Wr, L1_xattn_Wk, L1_xattn_Wv, L1_xattn_Wg, L1_xattn_Wo, L1_xattn_gn_w, L1_xattn_gn_b, L1_xattn_fmaa_k, L1_xattn_fmaa_r, L1_xattn_fWk, L1_xattn_fWr, L1_xattn_fWv)
    x = _L2_xattn_ref(x, ctx_2048, L2_xattn_w_q, L2_xattn_w_k, L2_xattn_w_v, L2_xattn_w_o, L2_xattn_alpha)
    x = _L3_xattn_ref(x, ctx_2048, ctx_2048, L3_xattn_ln1_scale, L3_xattn_ln1_offset, L3_xattn_wq1, L3_xattn_bq1, L3_xattn_wk1, L3_xattn_bk1, L3_xattn_wv1, L3_xattn_bv1, L3_xattn_wo1, L3_xattn_bo1, L3_xattn_bias_k1, L3_xattn_bias_v1, L3_xattn_ln2_scale, L3_xattn_ln2_offset, L3_xattn_wq2, L3_xattn_bq2, L3_xattn_wk2, L3_xattn_bk2, L3_xattn_wv2, L3_xattn_bv2, L3_xattn_wo2, L3_xattn_bo2, L3_xattn_bias_k2, L3_xattn_bias_v2, L3_xattn_ln_mlp_scale, L3_xattn_ln_mlp_offset, L3_xattn_w_fc1, L3_xattn_b_fc1, L3_xattn_w_fc2, L3_xattn_b_fc2)
    return x

_drawn_inputs = setup_inputs


def setup_inputs(seed=0):
    import zlib

    import numpy as np

    out = dict(_drawn_inputs(seed))
    spreads = {'L0_xattn_bq': (0.0, 0.8),
     'L0_xattn_bk': (0.0, 2.0),
     'L0_xattn_bv': (0.0, 0.1),
     'L0_xattn_bo': (0.0, 0.1),
     'L0_xattn_gamma': (1.0, 0.2),
     'L0_xattn_beta': (0.0, 0.1),
     'L1_xattn_ln1_w': (1.0, 0.2),
     'L1_xattn_ln1_b': (0.0, 0.31),
     'L1_xattn_ln2_w': (1.0, 0.6),
     'L1_xattn_ln2_b': (0.0, 0.8),
     'L1_xattn_gn_w': (1.0, 0.6),
     'L1_xattn_gn_b': (0.0, 0.8),
     'L3_xattn_ln1_scale': (1.0, 0.6),
     'L3_xattn_ln1_offset': (0.0, 0.8),
     'L3_xattn_bq1': (0.0, 0.8),
     'L3_xattn_bk1': (0.0, 2.0),
     'L3_xattn_bv1': (0.0, 0.1),
     'L3_xattn_bo1': (0.0, 0.1),
     'L3_xattn_ln2_scale': (1.0, 0.6),
     'L3_xattn_ln2_offset': (0.0, 0.8),
     'L3_xattn_bq2': (0.0, 0.8),
     'L3_xattn_bk2': (0.0, 2.0),
     'L3_xattn_bv2': (0.0, 0.1),
     'L3_xattn_bo2': (0.0, 0.1),
     'L3_xattn_ln_mlp_scale': (1.0, 0.2),
     'L3_xattn_ln_mlp_offset': (0.0, 0.389),
     'L3_xattn_b_fc1': (0.0, 0.1),
     'L3_xattn_b_fc2': (0.0, 0.1)}
    factors = {'L0_xattn_Wq': 7.79,
     'L0_xattn_Wk': 7.584,
     'L1_xattn_maa_x': 7.461,
     'L1_xattn_maa_w': 8.0,
     'L1_xattn_maa_w1': 3.82,
     'L1_xattn_maa_w2': 3.894,
     'L1_xattn_decay_w1': 8.0,
     'L1_xattn_decay_w2': 8.0,
     'L1_xattn_faaaa': 4.104,
     'L1_xattn_fmaa_k': 2.948,
     'L1_xattn_fmaa_r': 8.0,
     'L1_xattn_fWr': 8.0,
     'L2_xattn_w_q': 2.922,
     'L2_xattn_w_k': 2.995,
     'L3_xattn_wq1': 4.032,
     'L3_xattn_wk1': 3.948,
     'L3_xattn_bias_k1': 64.0,
     'L3_xattn_bias_v1': 64.0,
     'L3_xattn_wq2': 4.064,
     'L3_xattn_wk2': 3.965,
     'L3_xattn_bias_k2': 64.0,
     'L3_xattn_bias_v2': 64.0}
    for name, (base, spread) in spreads.items():
        noise = np.random.default_rng([zlib.crc32(name.encode()), seed]).standard_normal(out[name].shape)
        drawn = base * np.exp(spread * noise) if base else spread * noise
        out[name] = jnp.asarray(drawn.astype(out[name].dtype))
    for name, factor in factors.items():
        out[name] = (out[name] * factor).astype(out[name].dtype)
    return out
```

```python
from contextlib import ExitStack

import concourse.bass as bass
from concourse import mybir

F32 = mybir.dt.float32
F32R = mybir.dt.float32r
ALU = mybir.AluOpType
ACT = mybir.ActivationFunctionType
AX_X = mybir.AxisListType.X

B, L, C = 8, 100, 512
S = 361
SP = S + 1
P = 128
CC = C // P
STILES = [(0, 128), (128, 128), (256, S - 256)]
NT = B * L
HALF = NT // 2


class Scope:

    retired = []

    def __init__(self, nc, prefix):
        self.nc, self.prefix, self.stack = nc, prefix, ExitStack()

    def __enter__(self):
        return self

    def __exit__(self, *exc):
        return self.stack.__exit__(*exc)

    def sb(self, name, shape, dt=F32):
        return self.stack.enter_context(self.nc.sbuf_tensor(f"{self.prefix}_{name}", shape, dt))

    def bank(self, name, shape=(P, 512)):
        return self.stack.enter_context(self.nc.psum_tensor(f"{self.prefix}_{name}", list(shape), F32))

    def sem(self, name):
        sem = self.nc.alloc_semaphore(f"{self.prefix}_{name}")
        Scope.retired.append(sem)
        return sem

    def block(self):
        return self.stack.enter_context(self.nc.Block())


def clear_semaphores(nc):
    nc.clear_and_free_semaphores(Scope.retired)
    Scope.retired.clear()
    nc.all_engine_barrier()


def row_statistics(nc, prefix, X, eps, mean, rstd):
    with Scope(nc, prefix) as sc:
        stats = sc.sb("stats", [L, B, 6])
        moments = sc.sb("moments", [L, B, 2])
        std = sc.sb("std", [L, B])
        vareps = sc.sb("vareps", [L, B])
        stats_done, moments_done = sc.sem("stats_done"), sc.sem("moments_done")
        var_ready, std_ready, rstd_ready = sc.sem("var_ready"), sc.sem("std_ready"), sc.sem("rstd_ready")
        block = sc.block()

        @block.vector
        def _(dve):
            for b in range(B):
                nc.vector.bn_stats(stats[:, b, :], X[:, b, :]).then_inc(stats_done, 1)
            for b in range(B):
                dve.wait_ge(stats_done, b + 1)
                nc.vector.bn_aggr(moments[:, b, :], stats[:, b, :]).then_inc(moments_done, 1)
            dve.wait_ge(moments_done, B)
            nc.vector.tensor_scalar(vareps[:], moments[:, :, 1], eps, None, ALU.add).then_inc(var_ready, 1)
            nc.vector.tensor_copy(mean[:], moments[:, :, 0])
            dve.wait_ge(std_ready, 1)
            nc.vector.reciprocal(rstd[:], std[:]).then_inc(rstd_ready, 1)
            dve.wait_ge(rstd_ready, 1)

        @block.scalar
        def _(act):
            act.wait_ge(var_ready, 1)
            nc.scalar.activation(std[:], vareps[:], ACT.Sqrt).then_inc(std_ready, 1)


def layer_norm_transposed(nc, prefix, X, eps, weight, offset, ident, write_out, out_engines):
    with Scope(nc, prefix + "s") as outer:
        mean, rstd = outer.sb("mean", [L, B]), outer.sb("rstd", [L, B])
        row_statistics(nc, prefix + "t", X, eps, mean, rstd)
        with Scope(nc, prefix) as sc:
            xn = sc.sb("xn", [L, 2, C])
            affine = sc.sb("affine", [P, 2, CC, L])
            turned = [sc.bank(f"turned{i}", [P, CC, P]) for i in range(2)]
            xn_ready, turned_ready, affine_done, high_done, low_done = (
                sc.sem(n) for n in ("xn_ready", "turned_ready", "affine_done", "high_done", "low_done"))
            block = sc.block()

            @block.gpsimd
            def _(pool):
                if out_engines == "split":
                    for b in range(B):
                        high, low = write_out(b)
                        pool.wait_ge(high_done, b + 1)
                        nc.gpsimd.tensor_tensor(low, affine[:, b % 2], high.bitcast(F32), ALU.subtract).then_inc(low_done, 1)

            @block.scalar
            def _(act):
                if out_engines == "split":
                    for b in range(B):
                        act.wait_ge(affine_done, CC * (b + 1))
                        nc.scalar.activation(write_out(b)[0], affine[:, b % 2], ACT.Copy).then_inc(high_done, 1)

            @block.vector
            def _(dve):
                def normalise(b):
                    if b >= 2:
                        dve.wait_ge(turned_ready, b - 1)
                    nc.vector.tensor_scalar(xn[:, b % 2, :], X[:, b, :], mean[:, b:b + 1], rstd[:, b:b + 1],
                                            ALU.subtract, ALU.mult).then_inc(xn_ready, 1)
                normalise(0)
                for b in range(B):
                    if b + 1 < B:
                        normalise(b + 1)
                    dve.wait_ge(turned_ready, b + 1)
                    if out_engines == "split" and b >= 2:
                        dve.wait_ge(low_done, b - 1)
                    for c in range(CC):
                        dst = affine[:, b % 2, c, :] if out_engines == "split" else write_out(b)[0][:, c, :]
                        nc.vector.tensor_scalar(dst, turned[b % 2][:, c, 0:L], weight[:, c:c + 1], offset[:, c:c + 1],
                                                ALU.mult, ALU.add).then_inc(affine_done, 1)

            @block.tensor
            def _(pe):
                for b in range(B):
                    pe.wait_ge(xn_ready, b + 1)
                    if b >= 2:
                        pe.wait_ge(affine_done, CC * (b - 1))
                    for c in range(CC):
                        last = nc.tensor.transpose(turned[b % 2][:, c, 0:L], xn[:, b % 2, c * P:(c + 1) * P],
                                                   ident[0:L, 0:L])
                    last.then_inc(turned_ready, 1)

H0, D0, KV0 = 32, 16, 8
HC = P // D0
SPAD = 3 * P


def grouped_attention(nc, qT, Wk, Wv, bk, bv, heads_of, ctxT, mask, ident, out):
    LAG_T, LAG_AV, LAG_ACT, LAG_DVE = 5, 7, 3, 6
    RM = 8
    with Scope(nc, "ga") as sc:
        ctx = sc.sb("ctx", [P, 2, CC, SP])
        maskb = sc.sb("maskb", [L, 2, S])
        kT = sc.sb("kT", [P, 2, S])
        v = sc.sb("v", [P, 2, 3, KV0 * D0])
        only = sc.sb("only", [P, 2, CC, HC, L])
        masked = sc.sb("masked", [L, RM, S])
        probs = sc.sb("probs", [L, 4, SPAD])
        turned = sc.sb("turned", [P, 4, 3, L])
        top, shift = sc.sb("top", [L, 2, H0]), sc.sb("shift", [L, 2, H0])
        total, share = sc.sb("total", [L, 2, H0]), sc.sb("share", [L, 2, H0])
        spacer = sc.sb("spacer", [1, 3])
        pspacer = sc.sb("pspacer", [1, 3])
        mark = sc.sb("mark", [1, 16])
        front = [sc.bank(f"front{i}") for i in range(2)]
        score = [sc.bank(f"score{i}") for i in range(2)]
        turn = [sc.bank(f"turn{i}", [P, CC, P]) for i in range(2)]
        mixed = [sc.bank(f"mixed{i}") for i in range(2)]
        ctx_in = [sc.sem(f"ctx_in{i}") for i in range(2)]
        mask_in = [sc.sem(f"mask_in{i}") for i in range(2)]
        (front_full, k_done, v_done, only_done, score_full, masked_done, shift_done, exp_done, turn_full,
         kept_act, kept_dve, av_done, share_done, out_done, set_up, pset) = (sc.sem(n) for n in (
             "front_full", "k_done", "v_done", "only_done", "score_full", "masked_done", "shift_done", "exp_done",
             "turn_full", "kept_act", "kept_dve", "av_done", "share_done", "out_done", "set_up", "pset"))
        FRONT0, K0, V0, ONLY0, SCORE0, MASKED0, EXP0, TURN0, KEPT0, AV0, OUT0 = 4, 1, 1, 0, 64, 2, RM, 4, 1, 4, 2
        block = sc.block()

        def batches(engine, body):
            with engine.Fori(0, B // 2 - 1) as j:
                body(2 * j, 0)
                body(2 * j + 1, 1)
            body(B - 2, 0)
            body(B - 1, 1)

        @block.sync
        def _(sp):
            def load(b, par):
                sp.wait_ge(front_full, 2 * (b - 2) + 2 + FRONT0)
                sp.dma_start(ctx[:, par], one(ctxT, b, "a p c s -> p (a c) s")).then_inc(ctx_in[par], 16)
                sp.wait_ge(masked_done, H0 * (b - 2) + H0 + MASKED0 + 32)
                sp.dma_start(maskb[:, par], one(mask, b, "a l s -> (a l) s")).then_inc(mask_in[par], 16)
            batches(sp, load)

        @block.gpsimd
        def _(pool):
            nc.gpsimd.memset(pspacer[:], 0.0).then_inc(pset, 1)
            pool.wait_ge(pset, 1)

            def body(b, par):
                pool.wait_ge(score_full, H0 * (b - 2) + H0 + SCORE0)
                nc.gpsimd.tensor_tensor(pspacer[:, par:par + 1], pspacer[:, 2:3], pspacer[:, 2:3], ALU.add)
                for c in range(CC):
                    q = one(qT, b, "p a c l -> p (a c) l")[:, c:c + 1, :]
                    nc.gpsimd.tensor_tensor(only[:, par, c], q.broadcast_to([P, HC, L]),
                                            heads_of[:].rearrange("p (h a) -> p h a", a=1).broadcast_to([P, HC, L]),
                                            ALU.mult).then_inc(only_done, 1)
            batches(pool, body)

        @block.scalar
        def _(act):
            nc.scalar.activation(mark[:, 0:1], ident[0:1, 0:1], ACT.Copy).then_inc(k_done, K0)
            nc.scalar.activation(mark[:, 1:2], ident[0:1, 0:1], ACT.Copy).then_inc(exp_done, EXP0)
            nc.scalar.activation(mark[:, 2:3], ident[0:1, 0:1], ACT.Copy).then_inc(kept_act, KEPT0)

            def keep_key(b, par):
                act.wait_ge(front_full, 2 * b + 1 + FRONT0)
                nc.scalar.activation(kT[:, par, :], front[0][:, 0:S], ACT.Identity, bias=bk[:, 0:1]).then_inc(k_done, 1)

            act.wait_ge(set_up, 1)
            keep_key(0, 0)

            def body(b, par):
                for i in range(H0 + LAG_ACT):
                    h = i
                    if h < H0:
                        act.wait_ge(shift_done, HC * b + h // 4 + 1)
                        act.wait_ge(turn_full, H0 * b + h - 3 + TURN0)
                        nc.scalar.activation(probs[:, h % 4, 0:S], masked[:, h % RM, :], ACT.Exp,
                                             bias=shift[:, par, h:h + 1], accum_out=total[:, par, h:h + 1]).then_inc(exp_done, 1)
                    h = i - LAG_ACT
                    if h >= 0 and h % 2 == 0:
                        act.wait_ge(turn_full, H0 * b + h + 1 + TURN0)
                        act.wait_ge(av_done, H0 * b + h - 3 + AV0)
                        nc.scalar.activation(turned[:, h % 4], turn[0][:, 0:3, 0:L], ACT.Copy).then_inc(kept_act, 1)
                    if i == FRONT_SLOTS[0] and not (isinstance(b, int) and b == B - 1):
                        keep_key(b + 1, 1 - par)
            batches(act, body)

        @block.vector
        def _(dve):
            nc.vector.memset(v[:, :, 2, :], 0.0).then_inc(share_done, 1)
            nc.vector.memset(probs[:, :, S:SPAD], 0.0).then_inc(set_up, 1)
            nc.vector.memset(mark[:, 3:4], 0.0).then_inc(v_done, V0)
            nc.vector.memset(mark[:, 4:5], 0.0).then_inc(masked_done, MASKED0 + 32)
            nc.vector.memset(mark[:, 5:6], 0.0).then_inc(kept_dve, KEPT0)
            nc.vector.memset(mark[:, 6:7], 0.0).then_inc(out_done, OUT0)
            nc.vector.memset(spacer[:], 0.0).then_inc(share_done, 1)
            dve.wait_ge(share_done, 2)

            def keep_value(b, par):
                dve.wait_ge(front_full, 2 * b + 2 + FRONT0)
                f = front[1][:].rearrange("p (t n) -> p t n", t=4)
                nc.vector.tensor_tensor(v[:, par, 0:2, :], f[:, 0:2, :],
                                        bv[:].rearrange("p (a n) -> p a n", a=1).broadcast_to([P, 2, P]), ALU.add)
                rows = STILES[2][1]
                nc.vector.tensor_tensor(v[0:rows, par, 2, :], f[0:rows, 2, :], bv[0:rows, :], ALU.add).then_inc(v_done, 1)

            keep_value(0, 0)

            def body(b, par):
                for i in range(H0 + LAG_DVE):
                    h = i
                    if h < H0:
                        dve.wait_ge(score_full, H0 * b + h + 1 + SCORE0)
                        if h == 0:
                            dve.wait_ge(mask_in[par], 8 * b + (16 - 8 * par))
                        dve.wait_ge(exp_done, H0 * b + h - RM + 1 + EXP0)
                        nc.vector.tensor_copy(spacer[:, h % 2:h % 2 + 1], spacer[:, 2:3])
                        nc.vector.tensor_tensor_reduce(masked[:, h % RM, :], score[h % 2][0:L, 0:S], maskb[:, par, :], 1.0,
                                                       -3.0e38, ALU.add, ALU.max, top[:, par, h:h + 1]).then_inc(masked_done, 1)
                        if h % 4 == 3:
                            dve.wait_ge(masked_done, H0 * b + h + 1 + MASKED0 + 32)
                            nc.vector.tensor_scalar(shift[:, par, h - 3:h + 1], top[:, par, h - 3:h + 1], -1.0, None,
                                                    ALU.mult).then_inc(shift_done, 1)
                    h = i - LAG_DVE
                    if h >= 0 and h % 2 == 1:
                        dve.wait_ge(turn_full, H0 * b + h + 1 + TURN0)
                        dve.wait_ge(av_done, H0 * b + h - 3 + AV0)
                        nc.vector.tensor_copy(turned[:, h % 4], turn[1][:, 0:3, 0:L]).then_inc(kept_dve, 1)
                    if i == FRONT_SLOTS[1] and not (isinstance(b, int) and b == B - 1):
                        keep_value(b + 1, 1 - par)
                dve.wait_ge(exp_done, H0 * b + H0 + EXP0)
                nc.vector.reciprocal(share[:, par, :], total[:, par, :]).then_inc(share_done, 1)
                dve.wait_ge(share_done, b + 3)
                dve.wait_ge(av_done, H0 * b + H0 + AV0)
                nc.vector.tensor_tensor(one(out, b, "l a (h d) -> l (a h) d", d=D0),
                                        mixed[par][0:L, :].rearrange("l (h d) -> l h d", d=D0),
                                        share[:, par, :].rearrange("l (h a) -> l h a", a=1).broadcast_to([L, H0, D0]),
                                        ALU.mult).then_inc(out_done, 1)
            batches(dve, body)

        @block.tensor
        def _(pe):
            for sem, count in ((front_full, FRONT0), (score_full, SCORE0), (turn_full, TURN0), (av_done, AV0)):
                nc.tensor.matmul(mixed[0][0:1, 0:2], ident[:, 0:1], ident[:, 0:2], start=True, stop=True).then_inc(sem, count)

            def make_keys(b, par):
                pe.wait_ge(ctx_in[par], 8 * b + (16 - 8 * par))
                pe.wait_ge(k_done, b + K0)
                for c in range(CC):
                    last = nc.tensor.matmul(front[0][:, 0:S], Wk[:, c, :], ctx[:, par, c, 0:S], start=(c == 0), stop=(c == CC - 1))
                last.then_inc(front_full, 1)

            def make_values(b, par):
                pe.wait_ge(v_done, b + V0)
                for t, (s0, rows) in enumerate(STILES):
                    for c in range(CC):
                        last = nc.tensor.matmul(front[1][0:rows, t * P:(t + 1) * P], ctx[:, par, c, s0:s0 + rows], Wv[:, c, :],
                                                start=(c == 0), stop=(c == CC - 1))
                last.then_inc(front_full, 1)

            make_keys(0, 0)
            make_values(0, 0)

            def body(b, par):
                for i in range(H0 + LAG_AV):
                    h = i
                    if h < H0:
                        if h % HC == 0:
                            pe.wait_ge(only_done, CC * b + h // HC + 1)
                            pe.wait_ge(k_done, b + 1 + K0)
                        pe.wait_ge(masked_done, H0 * b + h - 1 + MASKED0 + 32)
                        nc.tensor.matmul(score[h % 2][0:L, 0:S], only[:, par, h // HC, h % HC, :], kT[:, par, :],
                                         start=True, stop=True).then_inc(score_full, 1)
                    h = i - LAG_T
                    if 0 <= h < H0:
                        pe.wait_ge(exp_done, H0 * b + h + 1 + EXP0)
                        kept = kept_dve if h % 2 else kept_act
                        pe.wait_ge(kept, H0 // 2 * b + h // 2 + KEPT0)
                        for t in range(3):
                            last = nc.tensor.transpose(turn[h % 2][:, t, 0:L], probs[:, h % 4, t * P:(t + 1) * P], ident[0:L, 0:L])
                        last.then_inc(turn_full, 1)
                    h = i - LAG_AV
                    if h >= 0:
                        kept = kept_dve if h % 2 else kept_act
                        pe.wait_ge(kept, H0 // 2 * b + h // 2 + 1 + KEPT0)
                        if h == 0:
                            pe.wait_ge(out_done, b - 1 + OUT0)
                            pe.wait_ge(v_done, b + 1 + V0)
                        kv = h % KV0
                        for t in range(3):
                            last = nc.tensor.matmul(mixed[par][0:L, h * D0:(h + 1) * D0], turned[:, h % 4, t, :],
                                                    v[:, par, t, kv * D0:(kv + 1) * D0], start=(t == 0), stop=(t == 2))
                        last.then_inc(av_done, 1)
                    if i in FRONT_SLOTS and not (isinstance(b, int) and b == B - 1):
                        (make_keys, make_values)[FRONT_SLOTS.index(i)](b + 1, 1 - par)
            batches(pe, body)


FRONT_SLOTS = [10, 20]


def one(t, b, pattern, **sizes):
    dims = pattern.split(" a")[0].split()
    index = [slice(None)] * (0 if pattern.startswith("a") else len(dims)) + [bass.ds(b, 1)]
    return t[tuple(index)].rearrange(pattern, **sizes)


def layer_norm_rows(nc, prefix, X, eps, gamma, beta):
    with Scope(nc, prefix) as outer:
        mean, rstd = outer.sb("mean", [L, B]), outer.sb("rstd", [L, B])
        row_statistics(nc, prefix + "t", X, eps, mean, rstd)
        with Scope(nc, prefix + "a") as sc:
            tmp = sc.sb("tmp", [L, 2, C])
            tmp2 = sc.sb("tmp2", [L, 2, C])
            centred, scaled, moved = sc.sem("centred"), sc.sem("scaled"), sc.sem("moved")
            block = sc.block()

            @block.vector
            def _(dve):
                for b in range(B):
                    if b >= 2:
                        dve.wait_ge(scaled, b - 1)
                    nc.vector.tensor_scalar(tmp[:, b % 2, :], X[:, b, :], mean[:, b:b + 1], rstd[:, b:b + 1],
                                            ALU.subtract, ALU.mult).then_inc(centred, 1)
                    if b >= 1:
                        dve.wait_ge(scaled, b)
                        nc.vector.tensor_tensor(X[:, b - 1, :], tmp2[:, (b - 1) % 2, :], beta[:], ALU.add).then_inc(moved, 1)
                dve.wait_ge(scaled, B)
                nc.vector.tensor_tensor(X[:, B - 1, :], tmp2[:, (B - 1) % 2, :], beta[:], ALU.add)

            @block.gpsimd
            def _(pool):
                for b in range(B):
                    pool.wait_ge(centred, b + 1)
                    if b >= 2:
                        pool.wait_ge(moved, b - 1)
                    nc.gpsimd.tensor_tensor(tmp2[:, b % 2, :], tmp[:, b % 2, :], gamma[:], ALU.mult).then_inc(scaled, 1)


def gqa_layer(nc, a, X, ident, column):
    with Scope(nc, "l0") as sc:
        gamma, beta = sc.sb("gamma", [L, C]), sc.sb("beta", [L, C])
        Wq, Wo = (sc.sb(n, [P, CC, C]) for n in ("Wq", "Wo"))
        Wk, Wv = sc.sb("Wk", [P, CC, P]), sc.sb("Wv", [P, CC, P])
        bk, bv, heads_of = sc.sb("bk", [P, 1]), sc.sb("bv", [P, P]), sc.sb("heads_of", [P, HC])
        xT, qT = sc.sb("xT", [P, B, CC, L]), sc.sb("qT", [P, B, CC, L])
        out = sc.sb("out", [L, B, C])
        query_weights, other_weights = sc.sem("query_weights"), sc.sem("other_weights")
        start_copies(nc, "l0u", query_weights, [(Wq[:], by_chunks(a["L0_Wq"]))])
        start_copies(nc, "l0w", other_weights, [(Wk[:], by_chunks(a["L0_Wk"])), (Wo[:], by_chunks(a["L0_Wo"])),
                                 (Wv[:], by_chunks(a["L0_Wv"])), (bk[:], a["L0_bk"]), (bv[:], a["L0_bv"]),
                                 (heads_of[:], a["heads_of"]), (gamma[:], a["L0_gamma"]), (beta[:], a["L0_beta"])])
        transposed(nc, "l0x", X, ident, xT)
        await_copies(nc, "l0v", (query_weights, 1))
        add_row(nc, "l0b", X, a["L0_bo"])

        def keep_query(engine, n, half, bank):
            engine.tensor_scalar(qT[:, 4 * half:4 * half + 4, n, :], bank, column("L0_bq")[:, n:n + 1], float(D0) ** -0.5,
                                 ALU.add, ALU.mult)

        product_transposed(nc, "l0q", Wq, xT, keep_query, engines=("vector",))
        await_copies(nc, "l0y", (other_weights, 8))
        grouped_attention(nc, qT, Wk, Wv, bk, bv, heads_of, a["ctxT"], a["mask"], ident, out)
        transposed(nc, "l0t", out, ident, xT)
        product_rows(nc, "l0o", Wo, xT, lambda e, b, bank: e.tensor_tensor(X[:, b, :], X[:, b, :], bank, ALU.add))
        layer_norm_rows(nc, "l0n", X, 1e-6, gamma, beta)

HD = 16
HEADS_CHUNK = P // HD


def shifted_difference(nc, prefix, cur, before, out, mixes):
    with Scope(nc, prefix) as sc:
        done = sc.sem("done")
        block = sc.block()

        @block.vector
        def _(dve):
            flat = "p b c l -> p (b c) l"
            c3, o3 = cur.rearrange(flat), out.rearrange(flat)
            nc.vector.tensor_tensor(o3[:, :, 1:L], c3[:, :, 0:L - 1], c3[:, :, 1:L], ALU.subtract).then_inc(done, 1)
            nc.vector.tensor_tensor(o3[:, :, 0], before.rearrange("p b c -> p (b c)"), c3[:, :, 0], ALU.subtract).then_inc(done, 1)
            dve.wait_ge(done, 2)
            for col, dst in mixes:
                for c in range(CC):
                    nc.vector.scalar_tensor_tensor(dst[:, :, c, :], out[:, :, c, :], col[:, c:c + 1], cur[:, :, c, :],
                                                   ALU.mult, ALU.add)


def mix_and_product(nc, prefix, mixing=None, product=None):
    with Scope(nc, prefix) as sc:
        mbank = [sc.bank(f"mix{i}", [P, 4, P]) for i in range(4)]
        pbank = [sc.bank(f"prod{i}", [P, 4, P]) for i in range(4)]
        scaled = sc.sb("scaled", [P, 2, 4, L])
        mix_full, mix_scaled, mix_done = sc.sem("mix_full"), sc.sem("mix_scaled"), sc.sem("mix_done")
        full, kept = sc.sem("full"), sc.sem("kept")
        block = sc.block()
        mslots = [(half, n) for half in range(2) for n in range(CC)] if mixing else []
        pslots = [(half, n) for half in range(2) for n in range(product[0])] if product else []

        @block.tensor
        def _(pe):
            for u, (half, n) in enumerate(mslots):
                if u >= 4:
                    pe.wait_ge(mix_scaled, u - 3)
                nc.tensor.matmul(mbank[u % 4][:, :, 0:L], mixing[0](n), mixing[1](half), start=True, stop=True).then_inc(mix_full, 1)
            for u, (half, n) in enumerate(pslots):
                if u >= 4:
                    pe.wait_ge(kept, u - 3)
                terms = product[1](n, half)
                rows = terms[0][0].shape[-1]
                for k, (x, y) in enumerate(terms):
                    last = nc.tensor.matmul(pbank[u % 4][0:rows, :, 0:L], x, y, start=(k == 0), stop=(k == len(terms) - 1))
                last.then_inc(full, 1)

        @block.vector
        def _(dve):
            for u, (half, n) in enumerate(mslots):
                _, _, col, diff, cur, out = mixing
                dve.wait_ge(mix_full, u + 1)
                if u >= 2:
                    dve.wait_ge(mix_done, u - 1)
                nc.vector.scalar_tensor_tensor(scaled[:, u % 2], mbank[u % 4][:, :, 0:L], col[:, n:n + 1],
                                               diff[:, 4 * half:4 * half + 4, n, :], ALU.add, ALU.mult).then_inc(mix_scaled, 1)

        @block.gpsimd
        def _(pool):
            for u, (half, n) in enumerate(mslots):
                _, _, col, diff, cur, out = mixing
                pool.wait_ge(mix_scaled, u + 1)
                nc.gpsimd.tensor_tensor(out[:, 4 * half:4 * half + 4, n, :], scaled[:, u % 2],
                                        cur[:, 4 * half:4 * half + 4, n, :], ALU.add).then_inc(mix_done, 1)

        @block.scalar
        def _(act):
            for u, (half, n) in enumerate(pslots):
                act.wait_ge(full, u + 1)
                product[2](act, n, half, pbank[u % 4][0:product[1](n, half)[0][0].shape[-1], :, 0:L]).then_inc(kept, 1)


def recurrence(nc, key, value, decay, receive, first, bonus, spread, gather, blocks, out):
    N = CC * L
    AHEAD = 4
    EARLY = 3
    with Scope(nc, "rec") as sc:
        kb, vb, wb, rb = (sc.sb(n, [P, 2, CC, L]) for n in ("kb", "vb", "wb", "rb"))
        vh, vl = sc.sb("vh", [P, 2, CC, L], F32R), sc.sb("vl", [P, 2, CC, L], F32R)
        spreadr = sc.sb("spreadr", [P, HD, P], F32R)
        s0 = sc.sb("s0", [P, 2, HD, CC])
        rank1 = sc.sb("rank1", [P, HD, CC, L])
        state = [sc.sb(f"state{i}", [P, N]) for i in range(4)]
        seen = [sc.sb(f"seen{i}", [P, N]) for i in range(4)]
        ruk = sc.sb("ruk", [P, CC, L])
        now = sc.sb("now", [P, 2, N])
        mark = sc.sb("mark", [1, 4])
        spreadb = [sc.bank(f"spread{i}", [P, 4, P]) for i in range(AHEAD)]
        sumb = [sc.bank(f"sum{i}", [P, 4, P]) for i in range(2)]
        nowb = sc.bank("nowb", [P, 4, P])
        inputs_in = [sc.sem(f"inputs_in{i}") for i in range(2)]
        (spread_rounded, v_high, v_low, spread_full, rank1_done, first_done, scan_done, seen_done, gathered, ruk_done,
         now_full, now_done, out_done) = (sc.sem(n) for n in (
             "spread_rounded", "v_high", "v_low", "spread_full", "rank1_done", "first_done", "scan_done", "seen_done",
             "gathered", "ruk_done", "now_full", "now_done", "out_done"))
        SEEN0, GATHER0, NOW0, OUT0 = 4, 4, 1, 2
        block = sc.block()

        def one(t, b):
            return t[:, bass.ds(b, 1)].rearrange("p a c l -> p (a c) l")

        def batches(engine, body):
            with engine.Fori(0, B // 2 - 1) as j:
                body(2 * j, 0, False)
                body(2 * j + 1, 1, False)
            body(B - 2, 0, False)
            body(B - 1, 1, True)

        def inputs(engine, b, par):
            engine.wait_ge(inputs_in[par], 40 * b + (80 - 40 * par))

        @block.sync
        def _(sp):
            def load(b, par, last):
                sp.wait_ge(out_done, b - 1 + OUT0)
                for dst, src in ((kb, key), (vb, value), (wb, decay), (rb, receive)):
                    sp.dma_start(dst[:, par], one(src, b)).then_inc(inputs_in[par], 16)
                sp.dma_start(s0[:, par], first[bass.ds(b, 1)].rearrange("a p j c -> p (a j) c")).then_inc(inputs_in[par], 16)
            batches(sp, load)

        @block.scalar
        def _(act):
            nc.scalar.activation(spreadr[:], spread[:], ACT.Copy).then_inc(spread_rounded, 1)

            def high(b, par, last):
                inputs(act, b, par)
                nc.scalar.activation(vh[:, par], vb[:, par], ACT.Copy).then_inc(v_high, 1)
            batches(act, high)

        @block.tensor
        def _(pe):
            nc.tensor.matmul(nowb[0:1, 0, 0:2], blocks[:, 0:1], blocks[:, 0:2], start=True, stop=True).then_inc(gathered, GATHER0)
            pe.wait_ge(spread_rounded, 1)

            def spread_column(b, par, j, first=False):
                if j == 0:
                    pe.wait_ge(v_low, b + 1)
                if not first:
                    pe.wait_ge(rank1_done, HD * b + (j + 1 - AHEAD))
                nc.tensor.matmul(spreadb[j % AHEAD][:, :, 0:L], spreadr[:, j, :], vl[:, par], start=True, stop=False)
                nc.tensor.matmul(spreadb[j % AHEAD][:, :, 0:L], spreadr[:, j, :], vh[:, par], start=False, stop=True).then_inc(spread_full, 1)

            for j in range(AHEAD):
                spread_column(0, 0, j, first=True)

            def body(b, par, last):
                for j in range(HD):
                    if j + AHEAD < HD:
                        spread_column(b, par, j + AHEAD)
                    elif not last:
                        spread_column(b + 1, 1 - par, j + AHEAD - HD)
                    if j == 2:
                        pe.wait_ge(ruk_done, CC * b + CC)
                        pe.wait_ge(now_done, b + NOW0)
                        nc.tensor.matmul(nowb[:, :, 0:L], blocks[:], ruk[:], start=True, stop=True).then_inc(now_full, 1)
                    if j == 0:
                        pe.wait_ge(out_done, b - 1 + OUT0)
                    pe.wait_ge(seen_done, HD * b + j + 1 + SEEN0)
                    nc.tensor.matmul(sumb[par][:, :, 0:L], gather[:, j, :],
                                     seen[j % 4][:].rearrange("p (c l) -> p c l", l=L),
                                     start=(j == 0), stop=(j == HD - 1)).then_inc(gathered, 1)
            batches(pe, body)

        @block.gpsimd
        def _(pool):
            nc.gpsimd.memset(mark[:, 0:1], 0.0).then_inc(seen_done, SEEN0)

            def body(b, par, last):
                inputs(pool, b, par)
                for j in range(HD):
                    pool.wait_ge(scan_done, HD * b + j + 1)
                    pool.wait_ge(gathered, HD * b + j - 3 + GATHER0)
                    nc.gpsimd.tensor_tensor(seen[j % 4][:], state[j % 4][:], rb[:, par].rearrange("p c l -> p (c l)"),
                                            ALU.mult).then_inc(seen_done, 1)
            batches(pool, body)

        @block.vector
        def _(dve):
            nc.vector.memset(mark[:, 2:3], 0.0).then_inc(now_done, NOW0)
            nc.vector.memset(mark[:, 3:4], 0.0).then_inc(out_done, OUT0)

            def low(b, par):
                inputs(dve, b, par)
                dve.wait_ge(v_high, b + 1)
                nc.vector.tensor_tensor(vl[:, par], vb[:, par], vh[:, par].bitcast(F32), ALU.subtract).then_inc(v_low, 1)

            def rank1_column(b, par, j):
                dve.wait_ge(spread_full, HD * b + j + 1)
                nc.vector.tensor_tensor(rank1[:, j, :, 1:L], spreadb[j % AHEAD][:, :, 0:L - 1], kb[:, par, :, 0:L - 1],
                                        ALU.mult).then_inc(rank1_done, 1)

            def column(b, par, j):
                if j + 1 < HD:
                    rank1_column(b, par, j + 1)
                dve.wait_ge(rank1_done, HD * b + j + 1)
                dve.wait_ge(seen_done, HD * b + j - 3 + SEEN0)
                nc.vector.tensor_tensor_scan(state[j % 4][:], wb[:, par].rearrange("p c l -> p (c l)"),
                                             rank1[:, j].rearrange("p c l -> p (c l)"), 0.0,
                                             ALU.mult, ALU.add).then_inc(scan_done, 1)

            def begin(b, par, first=False):
                if not first:
                    dve.wait_ge(scan_done, HD * b)
                nc.vector.tensor_copy(rank1[:, :, :, 0], s0[:, par]).then_inc(first_done, 1)
                rank1_column(b, par, 0)
                dve.wait_ge(first_done, b + 1)
                column(b, par, 0)
                for c in range(CC):
                    nc.vector.scalar_tensor_tensor(ruk[:, c, :], rb[:, par, c, :], bonus[:, c:c + 1], kb[:, par, c, :],
                                                   ALU.mult, ALU.mult).then_inc(ruk_done, 1)
                for j in range(1, EARLY):
                    column(b, par, j)

            low(0, 0)
            begin(0, 0, first=True)

            def body(b, par, last):
                for j in range(EARLY, HD):
                    column(b, par, j)
                    if j == 7:
                        dve.wait_ge(now_full, b + 1)
                        nc.vector.tensor_tensor(now[:, par].rearrange("p (c l) -> p c l", l=L), nowb[:, :, 0:L], vb[:, par],
                                                ALU.mult).then_inc(now_done, 1)
                    if j == 9 and not last:
                        low(b + 1, 1 - par)
                if not last:
                    begin(b + 1, 1 - par)
                dve.wait_ge(now_done, b + 1 + NOW0)
                dve.wait_ge(gathered, HD * b + HD + GATHER0)
                nc.vector.tensor_tensor(one(out, b), sumb[par][:, :, 0:L], now[:, par].rearrange("p (c l) -> p c l", l=L),
                                        ALU.add).then_inc(out_done, 1)
            batches(dve, body)


def head_norm(nc, y, dev, sq, means, scale, offset, gate, eps, out):
    slots = [(half, n) for half in range(2) for n in range(CC)]

    def part(t, half, n):
        return t[:, 4 * half:4 * half + 4, n, :]

    with Scope(nc, "hn") as sc:
        banks = [sc.bank(f"bank{i}", [P, 4, P]) for i in range(8)]
        root = sc.sb("root", [P, 2, 4, L])
        spread = sc.sb("spread", [P, 2, 4, L])
        epst = sc.sb("epst", [P, 1])
        (mean_full, dev_done, sq_done, var_full, root_done, inv_done, norm_done, affine_done, eps_set, out_done) = (
            sc.sem(n) for n in ("mean_full", "dev_done", "sq_done", "var_full", "root_done", "inv_done",
                                "norm_done", "affine_done", "eps_set", "out_done"))
        block = sc.block()

        @block.tensor
        def _(pe):
            for u, (half, n) in enumerate(slots):
                nc.tensor.matmul(banks[u][:, :, 0:L], means[:], part(y, half, n), start=True, stop=True).then_inc(mean_full, 1)
            for u, (half, n) in enumerate(slots):
                pe.wait_ge(sq_done, u + 1)
                nc.tensor.matmul(banks[u][:, :, 0:L], means[:], part(sq, half, n), start=True, stop=True).then_inc(var_full, 1)

        @block.scalar
        def _(act):
            for u, (half, n) in enumerate(slots):
                act.wait_ge(dev_done, u + 1)
                nc.scalar.activation(part(sq, half, n), part(dev, half, n), ACT.Square).then_inc(sq_done, 1)
            act.wait_ge(eps_set, 1)
            for u, (half, n) in enumerate(slots):
                act.wait_ge(var_full, u + 1)
                if u >= 2:
                    act.wait_ge(inv_done, u - 1)
                nc.scalar.activation(root[:, u % 2], banks[u][:, :, 0:L], ACT.Sqrt, bias=epst[:, 0:1]).then_inc(root_done, 1)

        @block.vector
        def _(dve):
            nc.vector.memset(epst[:], eps).then_inc(eps_set, 1)
            for u, (half, n) in enumerate(slots):
                dve.wait_ge(mean_full, u + 1)
                nc.vector.tensor_tensor(part(dev, half, n), part(y, half, n), banks[u][:, :, 0:L], ALU.subtract).then_inc(dev_done, 1)
            for u, (half, n) in enumerate(slots):
                dve.wait_ge(root_done, u + 1)
                if u >= 2:
                    dve.wait_ge(norm_done, u - 1)
                nc.vector.reciprocal(spread[:, u % 2], root[:, u % 2]).then_inc(inv_done, 1)
                dve.wait_ge(inv_done, u + 1)
                nc.vector.tensor_tensor(part(sq, half, n), part(dev, half, n), spread[:, u % 2], ALU.mult).then_inc(norm_done, 1)
                dve.wait_ge(norm_done, u + 1)
                nc.vector.tensor_scalar(part(dev, half, n), part(sq, half, n), scale[:, n:n + 1], offset[:, n:n + 1],
                                        ALU.mult, ALU.add).then_inc(affine_done, 1)

        @block.gpsimd
        def _(pool):
            for u, (half, n) in enumerate(slots):
                pool.wait_ge(affine_done, u + 1)
                nc.gpsimd.tensor_tensor(part(out, half, n), part(dev, half, n), part(gate, half, n), ALU.mult).then_inc(out_done, 1)


def rwkv_layer(nc, a, X, ident, column):
    def col(n):
        return column(f"L1_xattn_{n}")

    def tokens(t, half):
        return t[:, 4 * half:4 * half + 4, :]

    with Scope(nc, "l1") as sc:
        big = [P, B, CC, L]
        before = sc.sb("before", [P, 2, B, CC])
        with Scope(nc, "l1t") as st:
            W = {n: st.sb(n, [P, CC, C]) for n in ("WkT", "WvT", "WrT", "WgT")}
            w1, w2 = st.sb("w1", [P, CC, 5 * 32]), st.sb("w2", [P, C])
            w2g = st.sb("w2g", [32, C])
            d1, d2 = st.sb("d1", [P, CC, 64]), st.sb("d2", [64, C])
            low, lowg, lowd = st.sb("low", [P, B, L]), st.sb("lowg", [32, B, L]), st.sb("lowd", [64, B, L])
            cur, diff = st.sb("cur", big), st.sb("diff", big)
            mix = [st.sb(f"mix{i}", big) for i in range(2)]
            key, value, decay, receive, gate = (st.sb(n, big) for n in ("key", "value", "decay", "receive", "gate"))
            grow = st.sb("grow", [P, 2, 4, L])
            loaded, kept = st.sem("loaded"), st.sem("kept")
            start_copies(nc, "l1w", loaded, [(before[:], a["before"]), (w1[:], by_chunks(a["L1_maa_w1"])), (w2[:], a["L1_maa_w2"][0:P, :]),
                                     (w2g[:], a["L1_maa_w2"][P:, :]), (d1[:], by_chunks(a["L1_decay_w1"])),
                                     (d2[:], a["L1_decay_w2"])] + [(W[n][:], by_chunks(a[f"L1_{n}"])) for n in W])
            layer_norm_transposed(nc, "l1a", X, 1e-5, col("ln1_w"), col("ln1_b"), ident, lambda b: (cur[:, b],), "plain")
            await_copies(nc, "l1j", (loaded, 10))
            shifted_difference(nc, "l1d", cur[:], before[:, 1], diff[:], [(col("maa_x"), mix[0])])

            def dense(weight, source):
                return lambda n, half: [(weight[:, c, n * P:(n + 1) * P], source[:, 4 * half:4 * half + 4, c, :]) for c in range(CC)]

            def keep(out, func=ACT.Copy):
                return lambda act, n, half, bank: nc.scalar.activation(out[:, 4 * half:4 * half + 4, n, :], bank, func)

            mix_and_product(nc, "l1m", product=(
                1, lambda n, half: [(w1[:, c, 0:P], mix[0][:, 4 * half:4 * half + 4, c, :]) for c in range(CC)],
                lambda act, n, half, bank: nc.scalar.activation(tokens(low, half), bank, ACT.Tanh)))
            mix_and_product(nc, "l1n", product=(
                1, lambda n, half: [(w1[:, c, P:P + 32], mix[0][:, 4 * half:4 * half + 4, c, :]) for c in range(CC)],
                lambda act, n, half, bank: nc.scalar.activation(tokens(lowg, half), bank, ACT.Tanh)))

            def mixing(f, out):
                name = "wkvrg"[f]
                if f < 4:
                    return (lambda n: w2[32 * f:32 * f + 32, n * P:(n + 1) * P], lambda half: low[32 * f:32 * f + 32, 4 * half:4 * half + 4, :],
                            col(f"maa_{name}"), diff, cur, out)
                return lambda n: w2g[:, n * P:(n + 1) * P], lambda half: tokens(lowg, half), col("maa_g"), diff, cur, out

            grown = st.sem("grown")
            grown_count = [0]

            def keep_decay(act, n, half, bank):
                g = grow[:, grown_count[0] % 2]
                grown_count[0] += 1
                nc.scalar.activation(g, bank, ACT.Exp, bias=col("time_decay")[:, n:n + 1]).then_inc(grown, 1)
                act.wait_ge(grown, grown_count[0])
                return nc.scalar.activation(decay[:, 4 * half:4 * half + 4, n, 1:L], g[:, :, 0:L - 1], ACT.Exp, scale=-1.0)

            mix_and_product(nc, "l1o", mixing(0, mix[1]))
            mix_and_product(nc, "l1p", mixing(1, mix[0]), (
                1, lambda n, half: [(d1[:, c, :], mix[1][:, 4 * half:4 * half + 4, c, :]) for c in range(CC)],
                lambda act, n, half, bank: nc.scalar.activation(tokens(lowd, half), bank, ACT.Tanh)))
            clear(nc, decay[:].rearrange("p b c l -> p (b c) l")[:, :, 0])
            mix_and_product(nc, "l1q", None, (CC, lambda n, half: [(d2[:, n * P:(n + 1) * P], tokens(lowd, half))], keep_decay))
            keep_in_dram(nc, "decay", decay, a, kept)
            mix_and_product(nc, "l1r", mixing(2, mix[1]), (CC, dense(W["WkT"], mix[0]), keep(key)))
            keep_in_dram(nc, "key", key, a, kept)
            mix_and_product(nc, "l1s", mixing(3, mix[0]), (CC, dense(W["WvT"], mix[1]), keep(value)))
            keep_in_dram(nc, "value", value, a, kept)
            mix_and_product(nc, "l1u", mixing(4, mix[1]), (CC, dense(W["WrT"], mix[0]), keep(receive)))
            keep_in_dram(nc, "receive", receive, a, kept)
            mix_and_product(nc, "l1v", None, (CC, dense(W["WgT"], mix[1]), keep(gate, ACT.Silu)))
            keep_in_dram(nc, "gate", gate, a, kept)
            await_copies(nc, "l1k", (kept, 5))
        y, gate = sc.sb("y", big), sc.sb("gate2", big)
        means = sc.sb("means", [P, P])
        W = {n: sc.sb(n, [P, CC, C]) for n in ("WoT", "fWkT", "fWrT", "fWvT")}
        later = sc.sem("later")
        with Scope(nc, "l1c") as st:
            spread, gather = st.sb("spread", [P, HD, P]), st.sb("gather", [P, HD, P])
            blocks = st.sb("blocks", [P, P])
            matrices = st.sem("matrices")
            start_copies(nc, "l1x", matrices, [(spread[:], a["spread"]), (gather[:], a["gather"]), (blocks[:], a["blocks"])])
            await_copies(nc, "l1t", (matrices, 3))
            start_copies(nc, "l1y", later, [(means[:], a["means"]), (gate[:], a["kept_gate"])] + [(W[n][:], by_chunks(a[f"L1_{n}"])) for n in W])
            recurrence(nc, a["kept_key"], a["kept_value"], a["kept_decay"], a["kept_receive"], a["first"], col("faaaa"),
                       spread, gather, blocks, y)
        with Scope(nc, "l1e") as st:
            dev, sq, z = st.sb("dev", big), st.sb("sq", big), st.sb("z", big)
            rr = st.sb("rr", [L, B, C])
            tmp = st.sb("tmp", [L, 2, C])
            await_copies(nc, "l1aw", (later, 6))
            head_norm(nc, y, dev, sq, means, col("gn_w"), col("gn_b"), gate, 1e-5, z)
            product_rows(nc, "l1z", W["WoT"], z, lambda e, b, bank: e.tensor_tensor(X[:, b, :], X[:, b, :], bank, ALU.add))
            layer_norm_transposed(nc, "l1b", X, 1e-5, col("ln2_w"), col("ln2_b"), ident, lambda b: (y[:, b],), "plain")
            shifted_difference(nc, "l1f", y[:], before[:, 0], dev[:], [(col("fmaa_k"), sq), (col("fmaa_r"), z)])
            product_rows(nc, "l1g", W["fWrT"], z, lambda e, b, bank: e.activation(rr[:, b, :], bank, ACT.Sigmoid), "scalar")
            product_transposed(nc, "l1h", W["fWkT"], sq, lambda e, n, half, bank: e.activation(dev[:, 4 * half:4 * half + 4, n, :], bank, ACT.Relu),
                               engines=("scalar",))
            square(nc, dev[:].rearrange("p b c l -> p (b c l)"))
            gated = st.sem("gated")

            def add_gated(e, b, bank):
                e.tensor_tensor(tmp[:, b % 2, :], bank, rr[:, b, :], ALU.mult).then_inc(gated, 1)
                e.wait_ge(gated, b + 1)
                e.tensor_tensor(X[:, b, :], X[:, b, :], tmp[:, b % 2, :], ALU.add)

            product_rows(nc, "l1i", W["fWvT"], dev, add_gated)


def clear(nc, t):
    with Scope(nc, "clear") as sc:
        block = sc.block()

        @block.vector
        def _(dve):
            nc.vector.memset(t, 0.0)


def square(nc, t):
    with Scope(nc, "square") as sc:
        block = sc.block()

        @block.vector
        def _(dve):
            nc.vector.tensor_tensor(t, t, t, ALU.mult)


def keep_in_dram(nc, name, t, a, kept):
    a[f"kept_{name}"] = nc.dram_tensor(f"kept_{name}", tuple(t.shape), F32).ap()
    start_copies(nc, f"keep_{name}", kept, [(a[f"kept_{name}"], t[:])])


def start_copies(nc, prefix, sem, pairs):
    with Scope(nc, prefix) as sc:
        block = sc.block()

        @block.sync
        def _(sp):
            for tile, src in pairs:
                sp.dma_start(tile, src).then_inc(sem, 16)


def await_copies(nc, prefix, *waits):
    with Scope(nc, prefix) as sc:
        block = sc.block()

        @block.sync
        def _(sp):
            for sem, count in waits:
                sp.wait_ge(sem, 16 * count)


def by_chunks(w):
    return w.rearrange("(c p) n -> p c n", p=P)


def product_transposed(nc, prefix, weight, source, store, engines=("scalar", "vector"), tiles=CC):
    with Scope(nc, prefix) as sc:
        banks = [sc.bank(f"bank{i}", [P, 4, P]) for i in range(2 * tiles)]
        full = sc.sem("full")
        block = sc.block()
        slots = [(half, n) for half in range(2) for n in range(tiles)]

        @block.tensor
        def _(pe):
            for u, (half, n) in enumerate(slots):
                for c in range(CC):
                    last = nc.tensor.matmul(banks[u][:, :, 0:L], weight[:, c, n * P:(n + 1) * P],
                                            source[:, 4 * half:4 * half + 4, c, :], start=(c == 0), stop=(c == CC - 1))
                last.then_inc(full, 1)

        def keep(name, engine, other):
            for u, (half, n) in enumerate(slots):
                if engines[u % len(engines)] == name:
                    other.wait_ge(full, u + 1)
                    store(engine, n, half, banks[u][:, :, 0:L])

        @block.scalar
        def _(act):
            keep("scalar", nc.scalar, act)

        @block.vector
        def _(dve):
            keep("vector", nc.vector, dve)


def product_rows(nc, prefix, weight, source, store, engine_name="vector"):
    with Scope(nc, prefix) as sc:
        banks = [sc.bank(f"bank{i}") for i in range(B)]
        full = sc.sem("full")
        block = sc.block()

        @block.tensor
        def _(pe):
            for b in range(B):
                for c in range(CC):
                    last = nc.tensor.matmul(banks[b][0:L, :], source[:, b, c, :], weight[:, c, :],
                                            start=(c == 0), stop=(c == CC - 1))
                last.then_inc(full, 1)

        if engine_name == "vector":
            @block.vector
            def _(dve):
                for b in range(B):
                    dve.wait_ge(full, b + 1)
                    store(nc.vector, b, banks[b][0:L, :])
        else:
            @block.scalar
            def _(act):
                for b in range(B):
                    act.wait_ge(full, b + 1)
                    store(nc.scalar, b, banks[b][0:L, :])


def transposed(nc, prefix, X, ident, out):
    with Scope(nc, prefix) as sc:
        banks = [sc.bank(f"bank{i}", [P, CC, P]) for i in range(B)]
        full = sc.sem("full")
        block = sc.block()

        @block.tensor
        def _(pe):
            for b in range(B):
                for c in range(CC):
                    last = nc.tensor.transpose(banks[b][:, c, 0:L], X[:, b, c * P:(c + 1) * P], ident[0:L, 0:L])
                last.then_inc(full, 1)

        @block.scalar
        def _(act):
            for b in range(0, B, 2):
                act.wait_ge(full, b + 1)
                nc.scalar.activation(out[:, b], banks[b][:, :, 0:L], ACT.Copy)

        @block.vector
        def _(dve):
            for b in range(1, B, 2):
                dve.wait_ge(full, b + 1)
                nc.vector.tensor_copy(out[:, b], banks[b][:, :, 0:L])


def store_copy(out):
    def store(engine, n, half, bank):
        dst = out[:, 4 * half:4 * half + 4, n, :]
        if hasattr(engine, "activation"):
            return engine.activation(dst, bank, ACT.Copy)
        return engine.tensor_copy(dst, bank)
    return store


def plain_attention_layer(nc, a, X, ident):
    scale = float(C) ** -0.5
    with Scope(nc, "l2") as sc:
        w = {n: sc.sb(n, [P, CC, C]) for n in ("w_qT", "w_k", "w_vT", "w_oT")}
        alpha = sc.sb("alpha", [L, 1])
        one, two = sc.sb("one", [P, B, CC, L]), sc.sb("two", [P, B, CC, L])
        query_weights, other_weights = sc.sem("query_weights"), sc.sem("other_weights")
        start_copies(nc, "l2w", query_weights, [(w[n][:], by_chunks(a[f"L2_{n}"])) for n in ("w_qT", "w_k")])
        start_copies(nc, "l2z", other_weights, [(w[n][:], by_chunks(a[f"L2_{n}"])) for n in ("w_vT", "w_oT")] + [(alpha[:], a["alpha_rows"])])
        transposed(nc, "l2x", X, ident, one)
        await_copies(nc, "l2u", (query_weights, 2))
        product_transposed(nc, "l2q", w["w_qT"], one, store_copy(two))
        product_transposed(nc, "l2k", w["w_k"], two, store_copy(one))
        with Scope(nc, "l2a") as s2:
            ctxT = s2.sb("ctxT", [P, 2, CC, SP])
            ctxN = s2.sb("ctxN", [P, 2, 3, C])
            probs = s2.sb("probs", [L, 2, S])
            turned = s2.sb("turned", [P, 2, 3, L])
            top, shift = s2.sb("top", [L, B]), s2.sb("shift", [L, B])
            total, share = s2.sb("total", [L, B]), s2.sb("share", [L, B])
            score = [s2.bank(f"score{i}") for i in range(2)]
            turn = [s2.bank(f"turn{i}", [P, CC, P]) for i in range(2)]
            mixed = [s2.bank(f"mixed{i}", [P, CC, P]) for i in range(2)]
            in_t = [s2.sem(f"in_t{i}") for i in range(2)]
            in_n = [s2.sem(f"in_n{i}") for i in range(2)]
            (score_full, top_done, shift_done, exp_done, share_done, probs_done, turn_full, turned_done,
             mixed_full, mixed_done) = (s2.sem(n) for n in (
                 "score_full", "top_done", "shift_done", "exp_done", "share_done", "probs_done", "turn_full",
                 "turned_done", "mixed_full", "mixed_done"))
            block = s2.block()

            @block.sync
            def _(sp):
                for b in range(B):
                    if b >= 2:
                        sp.wait_ge(mixed_full, b - 1)
                    sp.dma_start(ctxT[:, b % 2], a["ctxT"][b]).then_inc(in_t[b % 2], 16)
                    sp.dma_start(ctxN[:, b % 2, 0:2, :], a["ctx"][b, 0:2 * P, :].rearrange("(t p) c -> p t c", p=P)).then_inc(in_n[b % 2], 16)
                    sp.dma_start(ctxN[0:S - 2 * P, b % 2, 2, :], a["ctx"][b, 2 * P:S, :]).then_inc(in_n[b % 2], 16)

            @block.tensor
            def _(pe):
                def scores(b):
                    pe.wait_ge(in_t[b % 2], 16 * (b // 2 + 1))
                    if b >= 2:
                        pe.wait_ge(exp_done, b - 1)
                    for c in range(CC):
                        last = nc.tensor.matmul(score[b % 2][0:L, 0:S], one[:, b, c, :], ctxT[:, b % 2, c, 0:S],
                                                start=(c == 0), stop=(c == CC - 1))
                    last.then_inc(score_full, 1)

                scores(0)
                for b in range(B):
                    if b + 1 < B:
                        scores(b + 1)
                    pe.wait_ge(probs_done, b + 1)
                    if b >= 2:
                        pe.wait_ge(turned_done, 2 * (b - 1))
                    for t, (s0, rows) in enumerate(STILES):
                        last = nc.tensor.transpose(turn[b % 2][0:rows, t, 0:L], probs[:, b % 2, s0:s0 + rows], ident[0:L, 0:L])
                    last.then_inc(turn_full, 1)
                    pe.wait_ge(turned_done, 2 * (b + 1))
                    pe.wait_ge(in_n[b % 2], 32 * (b // 2 + 1))
                    if b >= 2:
                        pe.wait_ge(mixed_done, b - 1)
                    for c in range(CC):
                        for t, (s0, rows) in enumerate(STILES):
                            last = nc.tensor.matmul(mixed[b % 2][:, c, 0:L], ctxN[0:rows, b % 2, t, c * P:(c + 1) * P],
                                                    turned[0:rows, b % 2, t, :], start=(t == 0), stop=(t == 2))
                    last.then_inc(mixed_full, 1)

            @block.scalar
            def _(act):
                for b in range(B):
                    act.wait_ge(shift_done, b + 1)
                    if b >= 2:
                        act.wait_ge(turn_full, b - 1)
                    nc.scalar.activation(probs[:, b % 2, :], score[b % 2][0:L, 0:S], ACT.Exp, bias=shift[:, b:b + 1],
                                         scale=scale, accum_out=total[:, b:b + 1]).then_inc(exp_done, 1)
                    act.wait_ge(turn_full, b + 1)
                    if b >= 2:
                        act.wait_ge(mixed_full, b - 1)
                    nc.scalar.activation(turned[:, b % 2, 0:2, :], turn[b % 2][:, 0:2, 0:L], ACT.Copy).then_inc(turned_done, 1)
                    rows = STILES[2][1]
                    nc.scalar.activation(turned[0:rows, b % 2, 2, :], turn[b % 2][0:rows, 2, 0:L], ACT.Copy).then_inc(turned_done, 1)

            @block.vector
            def _(dve):
                def maxima(b):
                    dve.wait_ge(score_full, b + 1)
                    nc.vector.reduce_max(top[:, b:b + 1], score[b % 2][0:L, 0:S], AX_X).then_inc(top_done, 1)
                    dve.wait_ge(top_done, b + 1)
                    nc.vector.tensor_scalar(shift[:, b:b + 1], top[:, b:b + 1], -scale, None, ALU.mult).then_inc(shift_done, 1)

                maxima(0)
                for b in range(B):
                    dve.wait_ge(exp_done, b + 1)
                    nc.vector.reciprocal(share[:, b:b + 1], total[:, b:b + 1]).then_inc(share_done, 1)
                    dve.wait_ge(share_done, b + 1)
                    nc.vector.tensor_scalar(probs[:, b % 2, :], probs[:, b % 2, :], share[:, b:b + 1], None,
                                            ALU.mult).then_inc(probs_done, 1)
                    if b + 1 < B:
                        maxima(b + 1)
                    dve.wait_ge(mixed_full, b + 1)
                    nc.vector.tensor_copy(two[:, b], mixed[b % 2][:, :, 0:L]).then_inc(mixed_done, 1)

        await_copies(nc, "l2t", (other_weights, 3))
        product_transposed(nc, "l2v", w["w_vT"], two, store_copy(one))

        def add_scaled(engine, b, bank):
            engine.scalar_tensor_tensor(X[:, b, :], bank, alpha[:, 0:1], X[:, b, :], ALU.mult, ALU.add)

        product_rows(nc, "l2o", w["w_oT"], one, add_scaled)

H3, K3 = 16, 128
G3 = 4
NG3 = H3 // G3
F3 = 2048
RING = 4
W3 = G3 * K3
BH = B // 2
U_K, U_T, U_AV, U_V = 0, 4, 7, 8
UNITS = 11
FILLED = {U_AV: 9, U_V: 9, U_V + 1: 10, U_V + 2: 11}
BANK = {U_AV: 0, U_V: RING + 1, U_V + 1: 2, U_V + 2: 3}


def load_group(engine, raw, weights, m, g):
    if m < 3:
        src = weights.rearrange("(c p) n -> p c n", p=P)[:, :, bass.ds(g * W3, W3)]
    else:
        src = weights.rearrange("(h p) n -> p h n", p=P)[:, bass.ds(g * G3, G3), :]
    return engine.dma_start(raw[:, m % 2, :].rearrange("p (c n) -> p c n", c=CC), src)


def cross_attention(nc, prefix, X, highT, lowT, ctxT, weights, head_columns, value_rows, bias_rows, scratch, ident,
                    raw, craw, raw_in, ctx_in):
    scale = float(K3) ** -0.5
    W = W3
    steps = NG3 * B
    with Scope(nc, prefix) as sc:
        wh = sc.sb("wh", [P, 4, CC * W], F32R)
        wl = sc.sb("wl", [P, 4, CC * W], F32R)
        columns = sc.sb("columns", [P, H3 * 4])
        keyh, keyl = sc.sb("keyh", [P, H3], F32R), sc.sb("keyl", [P, H3], F32R)
        ch = sc.sb("ch", [P, 2, CC, SP], F32R)
        cl = sc.sb("cl", [P, 2, CC, SP], F32R)
        qh, ql = sc.sb("qh", [P, G3, HALF], F32R), sc.sb("ql", [P, G3, HALF], F32R)
        kh, kl = sc.sb("kh", [P, G3, SP], F32R), sc.sb("kl", [P, G3, SP], F32R)
        vh, vl = sc.sb("vh", [P, 3, W], F32R), sc.sb("vl", [P, 3, W], F32R)
        probs = sc.sb("probs", [L, G3, SP])
        ph, pl = sc.sb("ph", [P, 3, G3 * L], F32R), sc.sb("pl", [P, 3, G3 * L], F32R)
        oh, ol = sc.sb("oh", [P, G3, L], F32R), sc.sb("ol", [P, G3, L], F32R)
        top, shift = sc.sb("top", [L, G3]), sc.sb("shift", [L, G3])
        total, share = sc.sb("total", [L, G3]), sc.sb("share", [L, G3])
        early = probs[:].rearrange("l h s -> l (h s)")
        bias = early[:, 0:C]
        vrow = early[0:H3, C:C + 2 * K3].rearrange("h (i k) -> h i k", k=K3)
        vdiff = early[0:H3, C + 2 * K3:C + 3 * K3]
        vdh, vdl = sc.sb("vdh", [H3, K3], F32R), sc.sb("vdl", [H3, K3], F32R)
        nothing = sc.sb("nothing", [P, 1])
        mark = sc.sb("mark", [1, 2])

        ring = [sc.bank(f"ring{i}") for i in range(RING)]
        score = [sc.bank(f"score{i}") for i in range(G3)]
        banks = ring + score

        (columns_in, rows_in, bias_in, bias_added, rows_out, extra_put, nothing_set,
         key_high, key_ready, diff_ready, diff_high, diff_split, keyx_ready,
         weight_high, weight_ready, ctx_high, ctx_ready,
         ring_full, high_done, bank_free, score_full, top_done, shift_ready,
         exp_done, share_ready, probs_ready, out_full, added) = (sc.sem(n) for n in (
             "columns_in", "rows_in", "bias_in", "bias_added", "rows_out", "extra_put", "nothing_set",
             "key_high", "key_ready", "diff_ready", "diff_high", "diff_split", "keyx_ready",
             "weight_high", "weight_ready", "ctx_high", "ctx_ready",
             "ring_full", "high_done", "bank_free", "score_full", "top_done", "shift_ready",
             "exp_done", "share_ready", "probs_ready", "out_full", "added"))
        block = sc.block()

        def before(n, i):
            halves = (n - i) // BH + 1 if i else 0
            return UNITS * n + halves * G3

        def column(i, n, h):
            return columns[:, bass.ds((n // B) * (4 * G3) + h * 4 + i, 1)]

        def steps_of(engine, step, after):
            step(0, 0)
            with engine.Fori(0, steps // BH - 1) as m:
                for i in range(1, BH + 1):
                    step(m * BH + i, i)
            for i in range(1, BH):
                step(steps - BH + i, i)
            after(steps)

        @block.sync
        def _(sp):
            sp.dma_start(columns[:], head_columns).then_inc(columns_in, 16)
            sp.dma_start(vrow, value_rows).then_inc(rows_in, 16)
            sp.dma_start(bias, bias_rows).then_inc(bias_in, 16)
            sp.wait_ge(diff_split, 2)
            sp.dma_start(scratch[0], vdh[:].bitcast(F32)).then_inc(rows_out, 16)
            sp.dma_start(scratch[1], vdl[:].bitcast(F32)).then_inc(rows_out, 16)

            def load_weights(g, m):
                sp.wait_ge(weight_ready, 4 * g + m - 1)
                load_group(sp, raw, weights[m], m, g).then_inc(raw_in[m % 2], 16)

            def load_context(n):
                sp.wait_ge(ctx_ready, n)
                sp.dma_start(craw[:], ctxT[bass.ds(n % B, 1)].rearrange("a p c s -> p (a c) s")).then_inc(ctx_in, 16)

            load_weights(0, 2)
            load_context(1)
            load_weights(0, 3)
            with sp.Fori(0, NG3 - 1) as g:
                load_context(g * B + 2)
                load_weights(g + 1, 0)
                load_weights(g + 1, 1)
                for b in (3, 4, 5, 6):
                    load_context(g * B + b)
                load_weights(g + 1, 2)
                for b in (7, 8, 9):
                    load_context(g * B + b)
                load_weights(g + 1, 3)
            for n in range(B * (NG3 - 1) + 2, steps):
                load_context(n)

        @block.gpsimd
        def _(pool):
            nc.gpsimd.memset(nothing[:], 0.0).then_inc(nothing_set, 1)
            pool.wait_ge(nothing_set, 1)
            pool.wait_ge(key_ready, 1)

            def flat(t):
                return t.rearrange("p c s -> p (c s)")

            def split_context(n, parity, wait=True, more=0):
                pool.wait_ge(ctx_in, 16 * n + 16)
                if wait:
                    pool.wait_ge(ring_full, before_any(n - 1) + more)
                nc.gpsimd.tensor_tensor(flat(ch[:, parity]), flat(craw[:]), nothing[:].broadcast_to([P, CC * SP]), ALU.add).then_inc(ctx_high, 1)
                pool.wait_ge(ctx_high, n + 1)
                nc.gpsimd.tensor_tensor(cl[:, parity], craw[:], ch[:, parity].bitcast(F32),
                                        ALU.subtract).then_inc(ctx_ready, 1)

            def before_any(n):
                return UNITS * n + ((n + BH - 1) // BH) * G3

            def split_weights(g, m):
                past = (before_any(g * B - BH) + G3, before_any(g * B - 1) + U_T, before_any(g * B), before_any(g * B + 1))
                pool.wait_ge(raw_in[m % 2], 32 * g + 16 * (m // 2) + 16)
                pool.wait_ge(ring_full, past[m])
                nc.gpsimd.tensor_tensor(wh[:, m, :], raw[:, m % 2, :], nothing[:].broadcast_to([P, CC * W]), ALU.add).then_inc(weight_high, 1)
                pool.wait_ge(weight_high, 4 * g + m + 1)
                nc.gpsimd.tensor_tensor(wl[:, m, :], raw[:, m % 2, :], wh[:, m, :].bitcast(F32),
                                        ALU.subtract).then_inc(weight_ready, 1)

            def learned_key(g):
                nc.gpsimd.tensor_copy(kh[:, :, S], keyh[:, bass.ds(g * G3, G3)].bitcast(F32)).then_inc(keyx_ready, 1)
                nc.gpsimd.tensor_copy(kl[:, :, S], keyl[:, bass.ds(g * G3, G3)].bitcast(F32)).then_inc(keyx_ready, 1)

            split_context(0, 0, False)
            pool.wait_ge(bias_in, 16)
            for b in range(B):
                nc.gpsimd.tensor_tensor(X[:, b, :], X[:, b, :], bias, ALU.add).then_inc(bias_added, 1)
            split_context(1, 1, False)
            learned_key(0)
            with pool.Fori(0, NG3 - 1) as g:
                for b in (2, 3, 4, 5):
                    split_context(g * B + b, b % 2)
                split_weights(g + 1, 0)
                for b in (6, 7, 8):
                    split_context(g * B + b, b % 2)
                split_weights(g + 1, 1)
                split_weights(g + 1, 2)
                split_context(g * B + 9, 1, more=1)
                learned_key(g + 1)
                split_weights(g + 1, 3)
            for n in range(B * (NG3 - 1) + 2, steps):
                split_context(n, n % 2)

        @block.scalar
        def _(act):
            act.wait_ge(columns_in, 16)
            for m in range(4):
                act.wait_ge(raw_in[m % 2], 16 * (m // 2) + 16)
                nc.scalar.activation(wh[:, m, :], raw[:, m % 2, :], ACT.Copy).then_inc(weight_high, 1)
                if m == 1:
                    act.wait_ge(rows_out, 32)

            def exponentials(n):
                act.wait_ge(shift_ready, n)
                for h in range(G3):
                    nc.scalar.activation(probs[:, h, :], score[h][0:L, 0:SP], ACT.Exp, bias=shift[:, h:h + 1],
                                         scale=scale, accum_out=total[:, h:h + 1]).then_inc(exp_done, 1)

            def turned_tiles(at):
                for t in range(3):
                    rows = STILES[t][1] + (t == 2)
                    act.wait_ge(ring_full, at + U_T + t + 1)
                    nc.scalar.activation(ph[0:rows, t, :], ring[t][0:rows, 0:G3 * L], ACT.Copy).then_inc(high_done, 1)

            def attended(n, filled):
                act.wait_ge(ring_full, filled)
                for h in range(G3):
                    last = nc.scalar.activation(oh[:, h, :], banks[BANK[U_AV]][:, h * L:(h + 1) * L], ACT.Identity,
                                                bias=column(2, n - 1, h))
                last.then_inc(high_done, 1)

            def step(n, i):
                at = before(n, i)
                if i:
                    exponentials(n)
                else:
                    act.wait_ge(bias_added, B)
                if i % BH == 0:
                    for h in range(G3):
                        act.wait_ge(ring_full, at + h + 1)
                        nc.scalar.activation(qh[:, h, :], ring[h][:, 0:HALF], ACT.Identity, bias=column(0, n, h)).then_inc(high_done, 1)
                    at = at + G3
                for h in range(G3):
                    act.wait_ge(ring_full, at + h + 1)
                    nc.scalar.activation(kh[:, h, 0:S], ring[h][:, 0:S], ACT.Identity, bias=column(1, n, h)).then_inc(
                        high_done, 1 if i or h < G3 - 1 else 1 + U_V - U_T)
                if i:
                    turned_tiles(at)
                    attended(n, at + FILLED[U_AV])
                for t in range(3):
                    rows = STILES[t][1]
                    act.wait_ge(ring_full, at + FILLED[U_V + t])
                    nc.scalar.activation(vh[0:rows, t, :], banks[BANK[U_V + t]][0:rows, :], ACT.Copy).then_inc(high_done, 1)
                if i % BH == 0:
                    row = STILES[2][1]
                    for part, values in enumerate((vh, vl)):
                        act.dma_start(values[row:row + 1, 2, :].bitcast(F32),
                                      scratch[part:part + 1].rearrange("a h k -> a (h k)")[:, bass.ds((n // B) * W, W)]).then_inc(extra_put, 16)

            def after(n):
                at = before(n, BH) - U_T
                exponentials(n)
                turned_tiles(at)
                attended(n, at + U_AV + 1)

            steps_of(act, step, after)

        @block.vector
        def _(dve):
            dve.wait_ge(columns_in, 16)
            bias_k = columns[:].rearrange("p (h i) -> p h i", i=4)[:, :, 3]
            nc.vector.tensor_copy(keyh[:], bias_k).then_inc(key_high, 1)
            dve.wait_ge(key_high, 1)
            nc.vector.tensor_tensor(keyl[:], bias_k, keyh[:].bitcast(F32), ALU.subtract).then_inc(key_ready, 1)
            dve.wait_ge(rows_in, 16)
            nc.vector.tensor_tensor(vdiff, vrow[:, 0, :], vrow[:, 1, :], ALU.subtract).then_inc(diff_ready, 1)
            dve.wait_ge(diff_ready, 1)
            nc.vector.tensor_copy(vdh[:], vdiff).then_inc(diff_split, 1)
            dve.wait_ge(diff_split, 1)
            nc.vector.tensor_tensor(vdl[:], vdiff, vdh[:].bitcast(F32), ALU.subtract).then_inc(diff_split, 1)
            for m in range(4):
                dve.wait_ge(weight_high, m + 1)
                nc.vector.tensor_tensor(wl[:, m, :], raw[:, m % 2, :], wh[:, m, :].bitcast(F32), ALU.subtract).then_inc(weight_ready, 1)

            def shares(n):
                dve.wait_ge(exp_done, G3 * n)
                nc.vector.reciprocal(share[:], total[:]).then_inc(share_ready, 1)
                dve.wait_ge(share_ready, n)
                for h in range(G3):
                    nc.vector.tensor_scalar(probs[:, h, :], probs[:, h, :], share[:, h:h + 1], None, ALU.mult).then_inc(probs_ready, 1)

            def turned_tiles(at):
                for t in range(3):
                    rows = STILES[t][1] + (t == 2)
                    dve.wait_ge(high_done, at + U_T + t + 1)
                    nc.vector.tensor_tensor(pl[0:rows, t, :], ring[t][0:rows, 0:G3 * L], ph[0:rows, t, :].bitcast(F32),
                                            ALU.subtract).then_inc(bank_free, 1)

            def attended(n, at):
                dve.wait_ge(high_done, at + U_AV + 1)
                for h in range(G3):
                    last = nc.vector.scalar_tensor_tensor(ol[:, h, :], banks[BANK[U_AV]][:, h * L:(h + 1) * L], column(2, n - 1, h),
                                                          oh[:, h, :].bitcast(F32), ALU.add, ALU.subtract)
                last.then_inc(bank_free, 1)

            def add_output(n):
                dve.wait_ge(out_full, n)
                xb = X[:, bass.ds((n - 1) % B, 1), :].rearrange("p a c -> p (a c)")
                nc.vector.tensor_tensor(xb, xb, score[0][0:L, :], ALU.add).then_inc(added, 1)

            def step(n, i):
                at = before(n, i)
                if i:
                    shares(n)
                else:
                    dve.wait_ge(bias_added, B)
                if i % BH == 0:
                    for h in range(G3):
                        dve.wait_ge(high_done, at + h + 1)
                        nc.vector.scalar_tensor_tensor(ql[:, h, :], ring[h][:, 0:HALF], column(0, n, h), qh[:, h, :].bitcast(F32),
                                                       ALU.add, ALU.subtract).then_inc(bank_free, 1)
                    at = at + G3
                for h in range(G3):
                    dve.wait_ge(high_done, at + h + 1)
                    nc.vector.scalar_tensor_tensor(kl[:, h, 0:S], ring[h][:, 0:S], column(1, n, h), kh[:, h, 0:S].bitcast(F32),
                                                   ALU.add, ALU.subtract).then_inc(bank_free, 1 if i or h < G3 - 1 else 1 + U_V - U_T)
                if i:
                    turned_tiles(at)
                    attended(n, at)
                for t in range(3):
                    if i and t == 2:
                        add_output(n)
                    rows = STILES[t][1]
                    dve.wait_ge(high_done, at + U_V + t + 1)
                    nc.vector.tensor_tensor(vl[0:rows, t, :], banks[BANK[U_V + t]][0:rows, :], vh[0:rows, t, :].bitcast(F32),
                                            ALU.subtract).then_inc(bank_free, 1)
                for h in range(G3):
                    dve.wait_ge(score_full, G3 * n + h + 1)
                    nc.vector.reduce_max(top[:, h:h + 1], score[h][0:L, 0:SP], AX_X).then_inc(top_done, 1)
                dve.wait_ge(top_done, G3 * n + G3)
                nc.vector.tensor_scalar(shift[:], top[:], -scale, None, ALU.mult).then_inc(shift_ready, 1)

            def after(n):
                at = before(n, BH) - U_T
                shares(n)
                turned_tiles(at)
                attended(n, at)
                add_output(n)

            steps_of(dve, step, after)

        @block.tensor
        def _(pe):
            def products(out, terms):
                count = 3 * len(terms)
                k = 0
                for (ah, al), (bh, bl) in terms:
                    for a, b in ((al, bh), (ah, bl), (ah, bh)):
                        last = nc.tensor.matmul(out, a, b, start=(k == 0), stop=(k == count - 1))
                        k += 1
                return last

            def weights_there(n, m):
                pe.wait_ge(weight_ready, (n // B) * 4 + m + 1)

            def queries(n, at):
                weights_there(n, 0)
                b0 = n % B
                for h in range(G3):
                    products(ring[h][:, 0:HALF].rearrange("p (b l) -> p b l", l=L), [
                        ((wh[:, 0, c * W + h * K3:c * W + (h + 1) * K3], wl[:, 0, c * W + h * K3:c * W + (h + 1) * K3]),
                         (highT[:, bass.ds(b0, BH), c, :], lowT[:, bass.ds(b0, BH), c, :])) for c in range(CC)]).then_inc(ring_full, 1)

            def turned_tiles(n, at):
                pe.wait_ge(probs_ready, G3 * n)
                for t in range(3):
                    pe.wait_ge(bank_free, at + t + 1)
                    s0 = STILES[t][0]
                    rows = STILES[t][1] + (t == 2)
                    for h in range(G3):
                        last = nc.tensor.transpose(ring[t][0:rows, h * L:(h + 1) * L],
                                                   probs[:, h, s0:s0 + rows], ident[0:L, 0:L])
                    last.then_inc(ring_full, 1)

            def attended(at, halves):
                pe.wait_ge(bank_free, at + U_AV)
                pe.wait_ge(extra_put, 32 * halves)
                for h in range(G3):
                    last = products(banks[BANK[U_AV]][:, h * L:(h + 1) * L], [
                        ((vh[0:rows, t, h * K3:(h + 1) * K3], vl[0:rows, t, h * K3:(h + 1) * K3]),
                         (ph[0:rows, t, h * L:(h + 1) * L], pl[0:rows, t, h * L:(h + 1) * L]))
                        for t, rows in ((0, P), (1, P), (2, STILES[2][1] + 1))])
                last.then_inc(ring_full, 1)

            def output(n, at):
                pe.wait_ge(bank_free, at + U_AV + 1)
                weights_there(n - 1, 3)
                products(score[0][0:L, :], [
                    ((oh[:, h, :], ol[:, h, :]), (wh[:, 3, h * C:(h + 1) * C], wl[:, 3, h * C:(h + 1) * C]))
                    for h in range(G3)]).then_inc(out_full, 1)

            def step(n, i):
                parity = i % 2
                at = before(n, i)
                last_use = (at - 3, at - 3, at - 1, at)
                if i % BH == 0:
                    if i:
                        pe.wait_ge(bank_free, at)
                    queries(n, at)
                    last_use = (at + 1, at + 2, at + 3, at + 4)
                    at = at + G3
                weights_there(n, 1)
                pe.wait_ge(ctx_ready, n + 1)
                for h in range(G3):
                    if i or i % BH == 0:
                        pe.wait_ge(bank_free, last_use[h])
                    products(ring[h][:, 0:SP], [
                        ((wh[:, 1, c * W + h * K3:c * W + (h + 1) * K3], wl[:, 1, c * W + h * K3:c * W + (h + 1) * K3]),
                         (ch[:, parity, c, :], cl[:, parity, c, :])) for c in range(CC)]).then_inc(
                             ring_full, 1 if i or h < G3 - 1 else 1 + U_V - U_T - 1)

                def value_tile(t, count=1):
                    if t == 1:
                        pe.wait_ge(bank_free, at + (U_T + 3 if i else 3))
                    if t == 2:
                        pe.wait_ge(bank_free, at + 4)
                    s0, rows = STILES[t]
                    products(banks[BANK[U_V + t]][0:rows, :], [
                        ((ch[:, parity, c, s0:s0 + rows], cl[:, parity, c, s0:s0 + rows]),
                         (wh[:, 2, c * W:(c + 1) * W], wl[:, 2, c * W:(c + 1) * W])) for c in range(CC)]).then_inc(ring_full, count)

                if i:
                    turned_tiles(n, at)
                weights_there(n, 2)
                value_tile(0, 1 if i else 2)
                if i:
                    attended(at, (n - i) // BH + 1)
                value_tile(1)
                if i:
                    output(n, at)
                value_tile(2)
                pe.wait_ge(keyx_ready, (n // B) * 2 + 2)
                if i:
                    pe.wait_ge(added, n)
                j = i % BH
                pe.wait_ge(bank_free, at + U_V + 1)
                for h in range(G3):
                    products(score[h][0:L, 0:SP], [((qh[:, h, j * L:(j + 1) * L], ql[:, h, j * L:(j + 1) * L]),
                                                    (kh[:, h, :], kl[:, h, :]))]).then_inc(score_full, 1)

            def after(n):
                at = before(n, BH)
                pe.wait_ge(bank_free, at)
                turned_tiles(n, at - U_T)
                attended(at - U_T, steps // BH)
                output(n, at - U_T)

            steps_of(pe, step, after)


def add_row(nc, prefix, X, row):
    with Scope(nc, prefix) as sc:
        bias = sc.sb("bias", [L, C])
        bias_in, done = sc.sem("bias_in"), sc.sem("done")
        block = sc.block()

        @block.sync
        def _(sp):
            sp.dma_start(bias[:], row).then_inc(bias_in, 16)

        @block.vector
        def _(dve):
            dve.wait_ge(bias_in, 16)
            for b in range(B):
                nc.vector.tensor_tensor(X[:, b, :], X[:, b, :], bias[:], ALU.add).then_inc(done, 1)
            dve.wait_ge(done, B)


def mlp(nc, a, X, ident, column):
    FH = F3 // 2
    FT = FH // P
    with Scope(nc, "mlp") as sc:
        highT = sc.sb("highT", [P, B, CC, L], F32R)
        lowT = sc.sb("lowT", [P, B, CC, L], F32R)
        layer_norm_transposed(nc, "lnm", X, 1e-5, column("L3_xattn_ln_mlp_scale"), column("L3_xattn_ln_mlp_offset"),
                              ident, lambda b: (highT[:, b], lowT[:, b]), "split")
        add_row(nc, "bo3", X, a["fc2_rows"])
        raw = [sc.sb(f"raw{i}", [P, CC * FH]) for i in range(2)]
        wh = [sc.sb(f"wh{i}", [P, CC * FH], F32R) for i in range(2)]
        wl = [sc.sb(f"wl{i}", [P, CC * FH], F32R) for i in range(2)]
        bias = sc.sb("bias", [P, FT])
        act32 = sc.sb("act32", [P, 2, HALF])
        fh, fl = sc.sb("fh", [P, FT, HALF], F32R), sc.sb("fl", [P, FT, HALF], F32R)
        mark = sc.sb("mark", [1, 4])
        ring = [sc.bank(f"ring{i}") for i in range(RING)]
        outs = [sc.bank(f"outs{i}") for i in range(2)]
        (bias_in, raw_in0, raw_in1, high_w, weight_ready, full, gelu_done, high_done, low_done, out_full, added) = (
            sc.sem(n) for n in ("bias_in", "raw_in0", "raw_in1", "high_w", "weight_ready", "full", "gelu_done",
                                "high_done", "low_done", "out_full", "added"))
        raw_in = [raw_in0, raw_in1]
        HIDDEN = 2 * FT
        WEIGHT0, GELU0, LOW0, OUT0, ADDED0 = 2, RING, 2, B, 2
        block = sc.block()

        @block.sync
        def _(sp):
            with sp.Fori(0, 2) as part:
                sp.wait_ge(gelu_done, HIDDEN * part + GELU0)
                sp.dma_start(bias[:], a["fc1_columns"][:, bass.ds(part * FT, FT)]).then_inc(bias_in, 16)
                sp.wait_ge(weight_ready, 2 * part + 1)
                sp.dma_start(raw[0][:].rearrange("p (c n) -> p c n", c=CC),
                             a["L3_xattn_w_fc1"].rearrange("(c p) n -> p c n", p=P)[:, :, bass.ds(part * FH, FH)]).then_inc(raw_in[0], 16)
                sp.wait_ge(weight_ready, 2 * part + 2)
                sp.dma_start(raw[1][:].rearrange("p (c n) -> p c n", c=FT),
                             a["L3_xattn_w_fc2"].rearrange("(c p) n -> p c n", p=P)[:, bass.ds(part * FT, FT), :]).then_inc(raw_in[1], 16)

        @block.scalar
        def _(act):
            with act.Fori(0, 2) as part:
                for m in range(2):
                    act.wait_ge(raw_in[m], 16 * part + 16)
                    act.wait_ge(out_full, 8 * part + OUT0)
                    nc.scalar.activation(wh[m][:], raw[m][:], ACT.Copy).then_inc(high_w, 1)
                act.wait_ge(bias_in, 16 * part + 16)
                for u in range(HIDDEN):
                    act.wait_ge(full, HIDDEN * part + u + 1)
                    act.wait_ge(low_done, HIDDEN * part + u - 2 + 1 + LOW0)
                    nc.scalar.activation(act32[:, u % 2, :], ring[u % RING][:, 0:HALF], ACT.Gelu,
                                         bias=bias[:, u % FT:u % FT + 1]).then_inc(gelu_done, 1)

        @block.vector
        def _(dve):
            nc.vector.memset(mark[:, 0:1], 0.0).then_inc(weight_ready, WEIGHT0)
            nc.vector.memset(mark[:, 1:2], 0.0).then_inc(low_done, LOW0)
            nc.vector.memset(mark[:, 2:3], 0.0).then_inc(added, ADDED0)
            with dve.Fori(0, 2) as part:
                for m in range(2):
                    dve.wait_ge(high_w, 2 * part + m + 1)
                    nc.vector.tensor_tensor(wl[m][:], raw[m][:], wh[m][:].bitcast(F32), ALU.subtract).then_inc(weight_ready, 1)
                for u in range(HIDDEN):
                    dve.wait_ge(gelu_done, HIDDEN * part + u + 1 + GELU0)
                    if u == 0:
                        dve.wait_ge(out_full, 8 * part + OUT0)
                    if u == FT:
                        dve.wait_ge(out_full, 8 * part + 4 + OUT0)
                    nc.vector.tensor_copy(fh[:, u % FT, :], act32[:, u % 2, :]).then_inc(high_done, 1)
                    dve.wait_ge(high_done, HIDDEN * part + u + 1)
                    nc.vector.tensor_tensor(fl[:, u % FT, :], act32[:, u % 2, :], fh[:, u % FT, :].bitcast(F32),
                                            ALU.subtract).then_inc(low_done, 1)
                    if u % FT == FT - 1:
                        for b in range(4 * (u // FT), 4 * (u // FT) + 4):
                            dve.wait_ge(out_full, 8 * part + b + 1 + OUT0)
                            dve.wait_ge(added, 8 * part + b + ADDED0)
                            nc.vector.tensor_tensor(X[:, b, :], X[:, b, :], outs[b % 2][0:L, :], ALU.add).then_inc(added, 1)

        @block.tensor
        def _(pe):
            nc.tensor.matmul(outs[0][0:1, 0:2], ident[:, 0:1], ident[:, 0:2], start=True, stop=True).then_inc(gelu_done, GELU0)
            nc.tensor.matmul(outs[0][0:1, 0:2], ident[:, 0:1], ident[:, 0:2], start=True, stop=True).then_inc(out_full, OUT0)

            def products(out, terms):
                k = 0
                for (ah, al), (bh, bl) in terms:
                    for x, y in ((al, bh), (ah, bl), (ah, bh)):
                        last = nc.tensor.matmul(out, x, y, start=(k == 0), stop=(k == 3 * len(terms) - 1))
                        k += 1
                return last

            with pe.Fori(0, 2) as part:
                for half in range(2):
                    for f in range(FT):
                        u = FT * half + f
                        pe.wait_ge(weight_ready, 2 * part + 1 + WEIGHT0)
                        pe.wait_ge(gelu_done, HIDDEN * part + u - RING + 1 + GELU0)
                        products(ring[u % RING][:, 0:HALF].rearrange("p (b l) -> p b l", l=L), [
                            ((wh[0][:, c * FH + f * P:c * FH + (f + 1) * P], wl[0][:, c * FH + f * P:c * FH + (f + 1) * P]),
                             (highT[:, 4 * half:4 * half + 4, c, :], lowT[:, 4 * half:4 * half + 4, c, :]))
                            for c in range(CC)]).then_inc(full, 1)
                    pe.wait_ge(weight_ready, 2 * part + 2 + WEIGHT0)
                    pe.wait_ge(low_done, HIDDEN * part + FT * (half + 1) + LOW0)
                    for j in range(4):
                        b = 4 * half + j
                        pe.wait_ge(added, 8 * part + b - 1 + ADDED0)
                        products(outs[b % 2][0:L, :], [
                            ((fh[:, f, j * L:(j + 1) * L], fl[:, f, j * L:(j + 1) * L]),
                             (wh[1][:, f * C:(f + 1) * C], wl[1][:, f * C:(f + 1) * C])) for f in range(FT)]).then_inc(out_full, 1)


def load_state(nc, X, x_dram, ident, ident_dram, columns, columns_dram):
    with Scope(nc, "load") as sc:
        come = sc.sem("come")
        block = sc.block()

        @block.sync
        def _(sp):
            sp.dma_start(X[:], x_dram.rearrange("b l c -> l b c")).then_inc(come, 16)
            sp.dma_start(ident[:], ident_dram).then_inc(come, 16)
            sp.dma_start(columns[:], columns_dram).then_inc(come, 16)
            sp.wait_ge(come, 48)


def store_state(nc, X, out):
    with Scope(nc, "store") as sc:
        gone = sc.sem("gone")
        block = sc.block()

        @block.sync
        def _(sp):
            sp.dma_start(out.rearrange("b l c -> l b c"), X[:]).then_inc(gone, 16)
            sp.wait_ge(gone, 16)


def attention_block(nc, a, X, ident, column, i):
    weights = [a[f"L3_xattn_w{w}{i}"] for w in "qkvo"]
    with Scope(nc, f"att{i}") as sc:
        highT = sc.sb("highT", [P, B, CC, L], F32R)
        lowT = sc.sb("lowT", [P, B, CC, L], F32R)
        raw = sc.sb("raw", [P, 2, CC * W3])
        craw = sc.sb("craw", [P, CC, SP])
        raw_in = [sc.sem(f"raw_in{k}") for k in range(2)]
        ctx_in = sc.sem("ctx_in")
        with Scope(nc, f"fetch{i}") as fetch:
            block = fetch.block()

            @block.sync
            def _(sp):
                load_group(sp, raw, weights[0], 0, 0).then_inc(raw_in[0], 16)
                sp.dma_start(craw[:], a["ctxT"][0]).then_inc(ctx_in, 16)
                load_group(sp, raw, weights[1], 1, 0).then_inc(raw_in[1], 16)

        layer_norm_transposed(nc, f"ln{i}", X, 1e-5, column(f"L3_xattn_ln{i}_scale"), column(f"L3_xattn_ln{i}_offset"),
                              ident, lambda b: (highT[:, b], lowT[:, b]), "split")
        cross_attention(nc, f"ca{i}", X, highT, lowT, a["ctxT"], weights, a[f"head_columns{i}"], a[f"value_rows{i}"], a[f"bo{i}_rows"],
                        nc.dram_tensor(f"value_parts{i}", (2, H3, K3), F32).ap(), ident, raw, craw, raw_in, ctx_in)


def program(nc, a, out):
    with Scope(nc, "state") as sc:
        X = sc.sb("X", [L, B, C])
        ident = sc.sb("ident", [P, P])
        columns = sc.sb("columns", [P, len(COLUMNS), CC])

        def column(name):
            return columns[:, COLUMNS.index(name), :]

        load_state(nc, X, a["x"], ident, a["ident"], columns, a["columns"])
        gqa_layer(nc, a, X, ident, column)
        clear_semaphores(nc)
        rwkv_layer(nc, a, X, ident, column)
        clear_semaphores(nc)
        plain_attention_layer(nc, a, X, ident)
        clear_semaphores(nc)
        attention_block(nc, a, X, ident, column, 1)
        clear_semaphores(nc)
        attention_block(nc, a, X, ident, column, 2)
        clear_semaphores(nc)
        mlp(nc, a, X, ident, column)
        store_state(nc, X, out)
        clear_semaphores(nc)


COLUMNS = ["L3_xattn_ln1_scale", "L3_xattn_ln1_offset", "L3_xattn_ln2_scale", "L3_xattn_ln2_offset",
           "L3_xattn_ln_mlp_scale", "L3_xattn_ln_mlp_offset",
           "L1_xattn_ln1_w", "L1_xattn_ln1_b", "L1_xattn_ln2_w", "L1_xattn_ln2_b",
           "L1_xattn_maa_x", "L1_xattn_maa_w", "L1_xattn_maa_k", "L1_xattn_maa_v", "L1_xattn_maa_r", "L1_xattn_maa_g",
           "L1_xattn_time_decay", "L1_xattn_faaaa", "L1_xattn_gn_w", "L1_xattn_gn_b",
           "L1_xattn_fmaa_k", "L1_xattn_fmaa_r", "L0_bq"]


def lay_out(inputs):
    import numpy as np

    def rows(v):
        return np.repeat(np.asarray(v).reshape(1, -1), L, axis=0)

    f = {k: np.asarray(v) for k, v in inputs.items()}
    a = {"x": f["x"], "ident": np.eye(P, dtype=np.float32)}
    ctx = f["ctx_2048"]
    ctxT = ctx.transpose(0, 2, 1).reshape(B, CC, P, S).transpose(0, 2, 1, 3)
    a["ctxT"] = np.pad(ctxT, ((0, 0), (0, 0), (0, 0), (0, SP - S)))
    a["columns"] = np.stack([f[n if n in f else "L0_xattn_bq"].reshape(CC, P).T for n in COLUMNS], axis=1)
    for i in (1, 2):
        for w in "qkvo":
            a[f"L3_xattn_w{w}{i}"] = f[f"L3_xattn_w{w}{i}"]
        a[f"bo{i}_rows"] = rows(f[f"L3_xattn_bo{i}"])
        a[f"head_columns{i}"] = np.stack([f[f"L3_xattn_{n}{i}"].reshape(H3, K3).T for n in ("bq", "bk", "bv", "bias_k")],
                                         axis=2).reshape(P, H3 * 4)
        a[f"value_rows{i}"] = np.stack([f[f"L3_xattn_{n}{i}"].reshape(H3, K3) for n in ("bias_v", "bv")], axis=1)
    order = np.arange(C).reshape(KV0, CC, D0).transpose(1, 0, 2).reshape(C)
    a["L0_Wq"], a["L0_Wv"], a["L0_Wo"] = f["L0_xattn_Wq"][:, order], f["L0_xattn_Wv"], f["L0_xattn_Wo"][order]
    a["L0_Wk"], a["L0_bk"] = f["L0_xattn_Wk"], f["L0_xattn_bk"].reshape(P, 1)
    a["L0_bv"] = np.repeat(f["L0_xattn_bv"].reshape(1, -1), P, axis=0)
    a["columns"][:, COLUMNS.index("L0_bq")] = f["L0_xattn_bq"][order].reshape(CC, P).T
    a["heads_of"] = (np.arange(P)[:, None] // D0 == np.arange(HC)[None, :]).astype(np.float32)
    a["mask"] = f["mask_Bx1xSxS2_ff0"][:, 0]
    a["L0_bo"], a["L0_gamma"], a["L0_beta"] = (rows(f[f"L0_xattn_{n}"]) for n in ("bo", "gamma", "beta"))
    for n in ("Wk", "Wv", "Wr", "Wg", "Wo", "fWk", "fWr", "fWv"):
        a[f"L1_{n}T"] = f[f"L1_xattn_{n}"].T
    a["L1_maa_w1"], a["L1_maa_w2"] = f["L1_xattn_maa_w1"], f["L1_xattn_maa_w2"].reshape(5 * 32, C)
    a["L1_decay_w1"], a["L1_decay_w2"] = f["L1_xattn_decay_w1"], f["L1_xattn_decay_w2"]
    a["before"] = ctx[:, 0:2, :].reshape(B, 2, CC, P).transpose(3, 1, 0, 2)
    a["first"] = ctx[:, 2:2 + HD, :].reshape(B, CC, P, HD).transpose(0, 2, 3, 1)
    spread = np.zeros((P, HD, P), np.float32)
    for p in range(P):
        for j in range(HD):
            spread[p // HD * HD + j, j, p] = 1.0
    a["spread"], a["gather"] = spread, spread.transpose(2, 1, 0)
    head = np.arange(P) // HD
    a["blocks"] = (head[:, None] == head[None, :]).astype(np.float32)
    a["means"] = a["blocks"] / np.float32(HD)
    a["ctx"] = ctx
    a["L2_w_qT"], a["L2_w_k"] = f["L2_xattn_w_q"].T, f["L2_xattn_w_k"]
    a["L2_w_vT"], a["L2_w_oT"] = f["L2_xattn_w_v"].T, f["L2_xattn_w_o"].T
    a["alpha_rows"] = np.repeat(f["L2_xattn_alpha"].reshape(1, 1), L, axis=0)
    a["L3_xattn_w_fc1"], a["L3_xattn_w_fc2"] = f["L3_xattn_w_fc1"], f["L3_xattn_w_fc2"]
    a["fc1_columns"] = f["L3_xattn_b_fc1"].reshape(F3 // P, P).T
    a["fc2_rows"] = rows(f["L3_xattn_b_fc2"])
    return {k: np.ascontiguousarray(v) for k, v in a.items()}


def kernel(**inputs):
    import concourse.bacc as bacc
    from concourse.bass_utils import run_bass_kernel_spmd

    nc = bacc.Bacc("TRN2", target_bir_lowering=False, num_devices=1)
    arrays = {f"in_{k}": v for k, v in lay_out(inputs).items()}
    a = {k[3:]: nc.dram_tensor(k, v.shape, mybir.dt.from_np(v.dtype), kind="ExternalInput").ap() for k, v in arrays.items()}
    out = nc.dram_tensor("out", (B, L, C), F32, kind="ExternalOutput").ap()
    program(nc, a, out)
    r = run_bass_kernel_spmd(nc, [arrays], core_ids=[0])
    return r.results[0]["out"]
```

```python
from contextlib import ExitStack

import concourse.bass as bass
from concourse import mybir

F32 = mybir.dt.float32
F32R = mybir.dt.float32r
ALU = mybir.AluOpType
ACT = mybir.ActivationFunctionType
AX_X = mybir.AxisListType.X

B, L, C = 8, 100, 512
S = 361
SP = S + 1
P = 128
CC = C // P
STILES = [(0, 128), (128, 128), (256, S - 256)]
NT = B * L
HALF = NT // 2


class Scope:

    retired = []

    def __init__(self, nc, prefix):
        self.nc, self.prefix, self.stack = nc, prefix, ExitStack()

    def __enter__(self):
        return self

    def __exit__(self, *exc):
        return self.stack.__exit__(*exc)

    def sb(self, name, shape, dt=F32):
        return self.stack.enter_context(self.nc.sbuf_tensor(f"{self.prefix}_{name}", shape, dt))

    def bank(self, name, shape=(P, 512)):
        return self.stack.enter_context(self.nc.psum_tensor(f"{self.prefix}_{name}", list(shape), F32))

    def sem(self, name):
        sem = self.nc.alloc_semaphore(f"{self.prefix}_{name}")
        Scope.retired.append(sem)
        return sem

    def block(self):
        return self.stack.enter_context(self.nc.Block())


def clear_semaphores(nc):
    nc.clear_and_free_semaphores(Scope.retired)
    Scope.retired.clear()
    nc.all_engine_barrier()


def row_statistics(nc, prefix, X, eps, mean, rstd):
    with Scope(nc, prefix) as sc:
        stats = sc.sb("stats", [L, B, 6])
        moments = sc.sb("moments", [L, B, 2])
        std = sc.sb("std", [L, B])
        vareps = sc.sb("vareps", [L, B])
        stats_done, moments_done = sc.sem("stats_done"), sc.sem("moments_done")
        var_ready, std_ready, rstd_ready = sc.sem("var_ready"), sc.sem("std_ready"), sc.sem("rstd_ready")
        block = sc.block()

        @block.vector
        def _(dve):
            for b in range(B):
                nc.vector.bn_stats(stats[:, b, :], X[:, b, :]).then_inc(stats_done, 1)
            for b in range(B):
                dve.wait_ge(stats_done, b + 1)
                nc.vector.bn_aggr(moments[:, b, :], stats[:, b, :]).then_inc(moments_done, 1)
            dve.wait_ge(moments_done, B)
            nc.vector.tensor_scalar(vareps[:], moments[:, :, 1], eps, None, ALU.add).then_inc(var_ready, 1)
            nc.vector.tensor_copy(mean[:], moments[:, :, 0])
            dve.wait_ge(std_ready, 1)
            nc.vector.reciprocal(rstd[:], std[:]).then_inc(rstd_ready, 1)
            dve.wait_ge(rstd_ready, 1)

        @block.scalar
        def _(act):
            act.wait_ge(var_ready, 1)
            nc.scalar.activation(std[:], vareps[:], ACT.Sqrt).then_inc(std_ready, 1)


def layer_norm_transposed(nc, prefix, X, eps, weight, offset, ident, write_out, out_engines):
    with Scope(nc, prefix + "s") as outer:
        mean, rstd = outer.sb("mean", [L, B]), outer.sb("rstd", [L, B])
        row_statistics(nc, prefix + "t", X, eps, mean, rstd)
        with Scope(nc, prefix) as sc:
            xn = sc.sb("xn", [L, 2, C])
            affine = sc.sb("affine", [P, 2, CC, L])
            CD = CC // 2
            turned = [[sc.bank(f"turned{i}{half}", [P, CC, P]) for half in range(2)] for i in range(2)]
            (xn_ready, turned_ready, affine_dve, affine_act, high_done, low_done) = (
                sc.sem(n) for n in ("xn_ready", "turned_ready", "affine_dve", "affine_act", "high_done", "low_done"))
            block = sc.block()
            split = out_engines == "split"

            def target(b, c):
                return affine[:, b % 2, c, :] if split else write_out(b)[0][:, c, :]

            @block.gpsimd
            def _(pool):
                if split:
                    for b in range(B):
                        high, low = write_out(b)
                        pool.wait_ge(high_done, b + 1)
                        nc.gpsimd.tensor_tensor(low, affine[:, b % 2], high.bitcast(F32), ALU.subtract).then_inc(low_done, 1)

            @block.scalar
            def _(act):
                for b in range(B):
                    act.wait_ge(turned_ready, b + 1)
                    if split and b >= 2:
                        act.wait_ge(low_done, b - 1)
                    for c in range(CD, CC):
                        nc.scalar.activation(target(b, c), turned[b % 2][c // CD][:, c, 0:L], ACT.Identity, bias=offset[:, c:c + 1],
                                             scale=weight[:, c:c + 1]).then_inc(affine_act, 1)
                    if split:
                        act.wait_ge(affine_dve, CD * (b + 1))
                        act.wait_ge(affine_act, (CC - CD) * (b + 1))
                        nc.scalar.activation(write_out(b)[0], affine[:, b % 2], ACT.Copy).then_inc(high_done, 1)

            @block.vector
            def _(dve):
                def normalise(b):
                    if b >= 2:
                        dve.wait_ge(turned_ready, b - 1)
                    nc.vector.tensor_scalar(xn[:, b % 2, :], X[:, b, :], mean[:, b:b + 1], rstd[:, b:b + 1],
                                            ALU.subtract, ALU.mult).then_inc(xn_ready, 1)
                normalise(0)
                for b in range(B):
                    if b + 1 < B:
                        normalise(b + 1)
                    dve.wait_ge(turned_ready, b + 1)
                    if split and b >= 2:
                        dve.wait_ge(low_done, b - 1)
                    for c in range(CD):
                        nc.vector.tensor_scalar(target(b, c), turned[b % 2][c // CD][:, c, 0:L], weight[:, c:c + 1], offset[:, c:c + 1],
                                                ALU.mult, ALU.add).then_inc(affine_dve, 1)

            @block.tensor
            def _(pe):
                for b in range(B):
                    pe.wait_ge(xn_ready, b + 1)
                    if b >= 2:
                        pe.wait_ge(affine_dve, CD * (b - 1))
                        pe.wait_ge(affine_act, (CC - CD) * (b - 1))
                    for c in range(CC):
                        last = nc.tensor.transpose(turned[b % 2][c // CD][:, c, 0:L], xn[:, b % 2, c * P:(c + 1) * P],
                                                   ident[0:L, 0:L])
                    last.then_inc(turned_ready, 1)

H0, D0, KV0 = 32, 16, 8
HC = P // D0
SPAD = 3 * P


def grouped_attention(nc, qh, ql, Wk, Wv, bk, bv, heads_of, ctxT, mask, ident, out):
    LAG_T, LAG_AV, LAG_ACT, LAG_DVE = 6, 8, 2, 7
    RM = 8
    with Scope(nc, "ga") as sc:
        ctx = sc.sb("ctx", [P, 2, CC, SP])
        maskb = sc.sb("maskb", [L, 2, S])
        kh, kl = sc.sb("kh", [P, 2, SP], F32R), sc.sb("kl", [P, 2, SP], F32R)
        v = sc.sb("v", [P, 2, 3, KV0 * D0])
        onlyh, onlyl = (sc.sb(n, [P, 2, CC, HC, L], F32R) for n in ("onlyh", "onlyl"))
        masked = sc.sb("masked", [L, RM, S])
        probs = sc.sb("probs", [L, 4, SPAD])
        turned = sc.sb("turned", [P, 4, 3, L])
        top, shift = sc.sb("top", [L, 2, H0]), sc.sb("shift", [L, 2, H0])
        total, share = sc.sb("total", [L, 2, H0]), sc.sb("share", [L, 2, H0])
        spacer = sc.sb("spacer", [1, 3])
        pspacer = sc.sb("pspacer", [1, 3])
        mark = sc.sb("mark", [1, 16])
        front = [sc.bank(f"front{i}") for i in range(2)]
        score = [sc.bank(f"score{i}") for i in range(2)]
        turn = [sc.bank(f"turn{i}", [P, CC, P]) for i in range(2)]
        mixed = [sc.bank(f"mixed{i}") for i in range(2)]
        ctx_in = [sc.sem(f"ctx_in{i}") for i in range(2)]
        mask_in = [sc.sem(f"mask_in{i}") for i in range(2)]
        (front_full, k_high, k_done, v_done, only_done, score_full, masked_done, shift_done, exp_done, turn_full,
         kept_act, kept_dve, av_done, share_done, out_done, set_up, pset) = (sc.sem(n) for n in (
             "front_full", "k_high", "k_done", "v_done", "only_done", "score_full", "masked_done", "shift_done", "exp_done",
             "turn_full", "kept_act", "kept_dve", "av_done", "share_done", "out_done", "set_up", "pset"))
        FRONT0, K0, V0, ONLY0, SCORE0, MASKED0, EXP0, TURN0, KEPT0, AV0, OUT0 = 4, 1, 1, 0, 64, 2, RM, 4, 1, 4, 2
        block = sc.block()

        def batches(engine, body):
            with engine.Fori(0, B // 2 - 1) as j:
                body(2 * j, 0)
                body(2 * j + 1, 1)
            body(B - 2, 0)
            body(B - 1, 1)

        @block.sync
        def _(sp):
            def load(b, par):
                sp.wait_ge(front_full, 2 * (b - 2) + 2 + FRONT0)
                sp.dma_start(ctx[:, par], one(ctxT, b, "a p c s -> p (a c) s")).then_inc(ctx_in[par], 16)
                sp.wait_ge(masked_done, H0 * (b - 2) + H0 + MASKED0 + 32)
                sp.dma_start(maskb[:, par], one(mask, b, "a l s -> (a l) s")).then_inc(mask_in[par], 16)
            batches(sp, load)

        @block.gpsimd
        def _(pool):
            nc.gpsimd.memset(pspacer[:], 0.0).then_inc(pset, 1)
            pool.wait_ge(pset, 1)

            def body(b, par):
                pool.wait_ge(score_full, H0 * (b - 2) + H0 + SCORE0)
                nc.gpsimd.tensor_tensor(pspacer[:, par:par + 1], pspacer[:, 2:3], pspacer[:, 2:3], ALU.add)
                for c in range(CC):
                    for part, only in ((qh, onlyh), (ql, onlyl)):
                        q = one(part, b, "p a c l -> p (a c) l")[:, c:c + 1, :].bitcast(F32)
                        nc.gpsimd.tensor_tensor(only[:, par, c], q.broadcast_to([P, HC, L]),
                                                heads_of[:].rearrange("p (h a) -> p h a", a=1).broadcast_to([P, HC, L]),
                                                ALU.mult).then_inc(only_done, 1)
            batches(pool, body)

        @block.scalar
        def _(act):
            nc.scalar.activation(mark[:, 1:2], ident[0:1, 0:1], ACT.Copy).then_inc(exp_done, EXP0)
            nc.scalar.activation(mark[:, 2:3], ident[0:1, 0:1], ACT.Copy).then_inc(kept_act, KEPT0)

            def keep_key(b, par):
                act.wait_ge(front_full, 2 * b + 1 + FRONT0)
                nc.scalar.activation(kh[:, par, :], front[0][:, 0:SP], ACT.Identity, bias=bk[:, 0:1]).then_inc(k_high, 1)

            act.wait_ge(set_up, 1)
            keep_key(0, 0)

            def body(b, par):
                for i in range(H0 + LAG_ACT):
                    h = i
                    if h < H0:
                        act.wait_ge(shift_done, HC * b + h // 4 + 1)
                        act.wait_ge(turn_full, H0 * b + h - 3 + TURN0)
                        nc.scalar.activation(probs[:, h % 4, 0:S], masked[:, h % RM, :], ACT.Exp,
                                             bias=shift[:, par, h:h + 1], accum_out=total[:, par, h:h + 1]).then_inc(exp_done, 1)
                    h = i - LAG_ACT
                    if h >= 0 and h % 2 == 0:
                        act.wait_ge(turn_full, H0 * b + h + 1 + TURN0)
                        act.wait_ge(av_done, H0 * b + h - 3 + AV0)
                        nc.scalar.activation(turned[:, h % 4], turn[0][:, 0:3, 0:L], ACT.Copy).then_inc(kept_act, 1)
                    if i == FRONT_SLOTS[0] and not (isinstance(b, int) and b == B - 1):
                        keep_key(b + 1, 1 - par)
            batches(act, body)

        @block.vector
        def _(dve):
            nc.vector.memset(v[:, :, 2, :], 0.0).then_inc(share_done, 1)
            nc.vector.memset(probs[:, :, S:SPAD], 0.0).then_inc(set_up, 1)
            nc.vector.memset(mark[:, 3:4], 0.0).then_inc(v_done, V0)
            nc.vector.memset(mark[:, 0:1], 0.0).then_inc(k_done, K0)
            nc.vector.memset(mark[:, 4:5], 0.0).then_inc(masked_done, MASKED0 + 32)
            nc.vector.memset(mark[:, 5:6], 0.0).then_inc(kept_dve, KEPT0)
            nc.vector.memset(mark[:, 6:7], 0.0).then_inc(out_done, OUT0)
            nc.vector.memset(spacer[:], 0.0).then_inc(share_done, 1)
            dve.wait_ge(share_done, 2)

            def keep_key(b, par):
                dve.wait_ge(k_high, b + 1)
                nc.vector.scalar_tensor_tensor(kl[:, par, :], front[0][:, 0:SP], bk[:, 0:1], kh[:, par, :].bitcast(F32),
                                               ALU.add, ALU.subtract).then_inc(k_done, 1)

            def keep_value(b, par):
                dve.wait_ge(front_full, 2 * b + 2 + FRONT0)
                f = front[1][:].rearrange("p (t n) -> p t n", t=4)
                nc.vector.tensor_tensor(v[:, par, 0:2, :], f[:, 0:2, :],
                                        bv[:].rearrange("p (a n) -> p a n", a=1).broadcast_to([P, 2, P]), ALU.add)
                rows = STILES[2][1]
                nc.vector.tensor_tensor(v[0:rows, par, 2, :], f[0:rows, 2, :], bv[0:rows, :], ALU.add).then_inc(v_done, 1)

            keep_key(0, 0)
            keep_value(0, 0)

            def body(b, par):
                for i in range(H0 + LAG_DVE):
                    h = i
                    if h < H0:
                        dve.wait_ge(score_full, H0 * b + h + 1 + SCORE0)
                        if h == 0:
                            dve.wait_ge(mask_in[par], 8 * b + (16 - 8 * par))
                        dve.wait_ge(exp_done, H0 * b + h - RM + 1 + EXP0)
                        nc.vector.tensor_copy(spacer[:, h % 2:h % 2 + 1], spacer[:, 2:3])
                        nc.vector.tensor_tensor_reduce(masked[:, h % RM, :], score[h % 2][0:L, 0:S], maskb[:, par, :], 1.0,
                                                       -3.0e38, ALU.add, ALU.max, top[:, par, h:h + 1]).then_inc(masked_done, 1)
                        if h % 4 == 3:
                            dve.wait_ge(masked_done, H0 * b + h + 1 + MASKED0 + 32)
                            nc.vector.tensor_scalar(shift[:, par, h - 3:h + 1], top[:, par, h - 3:h + 1], -1.0, None,
                                                    ALU.mult).then_inc(shift_done, 1)
                    h = i - LAG_DVE
                    if h >= 0 and h % 2 == 1:
                        dve.wait_ge(turn_full, H0 * b + h + 1 + TURN0)
                        dve.wait_ge(av_done, H0 * b + h - 3 + AV0)
                        nc.vector.tensor_copy(turned[:, h % 4], turn[1][:, 0:3, 0:L]).then_inc(kept_dve, 1)
                    if i == FRONT_SLOTS[0] + 6 and not (isinstance(b, int) and b == B - 1):
                        keep_key(b + 1, 1 - par)
                    if i == FRONT_SLOTS[1] and not (isinstance(b, int) and b == B - 1):
                        keep_value(b + 1, 1 - par)
                dve.wait_ge(exp_done, H0 * b + H0 + EXP0)
                nc.vector.reciprocal(share[:, par, :], total[:, par, :]).then_inc(share_done, 1)
                dve.wait_ge(share_done, b + 3)
                dve.wait_ge(av_done, H0 * b + H0 + AV0)
                nc.vector.tensor_tensor(one(out, b, "l a (h d) -> l (a h) d", d=D0),
                                        mixed[par][0:L, :].rearrange("l (h d) -> l h d", d=D0),
                                        share[:, par, :].rearrange("l (h a) -> l h a", a=1).broadcast_to([L, H0, D0]),
                                        ALU.mult).then_inc(out_done, 1)
            batches(dve, body)

        @block.tensor
        def _(pe):
            for sem, count in ((front_full, FRONT0), (score_full, SCORE0), (turn_full, TURN0), (av_done, AV0)):
                nc.tensor.matmul(mixed[0][0:1, 0:2], ident[:, 0:1], ident[:, 0:2], start=True, stop=True).then_inc(sem, count)

            def make_keys(b, par):
                pe.wait_ge(ctx_in[par], 8 * b + (16 - 8 * par))
                pe.wait_ge(k_done, b + K0)
                for c in range(CC):
                    last = nc.tensor.matmul(front[0][:, 0:SP], Wk[:, c, :], ctx[:, par, c, :], start=(c == 0), stop=(c == CC - 1))
                last.then_inc(front_full, 1)

            def make_values(b, par):
                pe.wait_ge(v_done, b + V0)
                for t, (s0, rows) in enumerate(STILES):
                    for c in range(CC):
                        last = nc.tensor.matmul(front[1][0:rows, t * P:(t + 1) * P], ctx[:, par, c, s0:s0 + rows], Wv[:, c, :],
                                                start=(c == 0), stop=(c == CC - 1))
                last.then_inc(front_full, 1)

            make_keys(0, 0)
            make_values(0, 0)

            def body(b, par):
                for i in range(H0 + LAG_AV):
                    h = i
                    if h < H0:
                        if h % HC == 0:
                            pe.wait_ge(only_done, CC * b * 2 + 2 * (h // HC + 1))
                            pe.wait_ge(k_done, b + 1 + K0)
                        pe.wait_ge(masked_done, H0 * b + h - 1 + MASKED0 + 32)
                        low, high = (t[:, par, h // HC, h % HC, :] for t in (onlyl, onlyh))
                        nc.tensor.matmul(score[h % 2][0:L, 0:SP], low, kh[:, par, :], start=True, stop=False)
                        nc.tensor.matmul(score[h % 2][0:L, 0:SP], high, kl[:, par, :], start=False, stop=False)
                        nc.tensor.matmul(score[h % 2][0:L, 0:SP], high, kh[:, par, :], start=False, stop=True).then_inc(score_full, 1)
                    h = i - LAG_T
                    if 0 <= h < H0:
                        pe.wait_ge(exp_done, H0 * b + h + 1 + EXP0)
                        kept = kept_dve if h % 2 else kept_act
                        pe.wait_ge(kept, H0 // 2 * b + h // 2 + KEPT0)
                        for t in range(3):
                            last = nc.tensor.transpose(turn[h % 2][:, t, 0:L], probs[:, h % 4, t * P:(t + 1) * P], ident[0:L, 0:L])
                        last.then_inc(turn_full, 1)
                    h = i - LAG_AV
                    if h >= 0:
                        kept = kept_dve if h % 2 else kept_act
                        pe.wait_ge(kept, H0 // 2 * b + h // 2 + 1 + KEPT0)
                        if h == 0:
                            pe.wait_ge(out_done, b - 1 + OUT0)
                            pe.wait_ge(v_done, b + 1 + V0)
                        kv = h % KV0
                        for t in range(3):
                            last = nc.tensor.matmul(mixed[par][0:L, h * D0:(h + 1) * D0], turned[:, h % 4, t, :],
                                                    v[:, par, t, kv * D0:(kv + 1) * D0], start=(t == 0), stop=(t == 2))
                        last.then_inc(av_done, 1)
                    if i in FRONT_SLOTS and not (isinstance(b, int) and b == B - 1):
                        (make_keys, make_values)[FRONT_SLOTS.index(i)](b + 1, 1 - par)
            batches(pe, body)


FRONT_SLOTS = [10, 20]


def one(t, b, pattern, **sizes):
    dims = pattern.split(" a")[0].split()
    index = [slice(None)] * (0 if pattern.startswith("a") else len(dims)) + [bass.ds(b, 1)]
    return t[tuple(index)].rearrange(pattern, **sizes)


def layer_norm_rows(nc, prefix, X, eps, gamma, beta):
    with Scope(nc, prefix) as outer:
        mean, rstd = outer.sb("mean", [L, B]), outer.sb("rstd", [L, B])
        row_statistics(nc, prefix + "t", X, eps, mean, rstd)
        with Scope(nc, prefix + "a") as sc:
            tmp = sc.sb("tmp", [L, 2, C])
            tmp2 = sc.sb("tmp2", [L, 2, C])
            centred, scaled, moved = sc.sem("centred"), sc.sem("scaled"), sc.sem("moved")
            block = sc.block()

            @block.vector
            def _(dve):
                for b in range(B):
                    if b >= 2:
                        dve.wait_ge(scaled, b - 1)
                    nc.vector.tensor_scalar(tmp[:, b % 2, :], X[:, b, :], mean[:, b:b + 1], rstd[:, b:b + 1],
                                            ALU.subtract, ALU.mult).then_inc(centred, 1)
                    if b >= 1:
                        dve.wait_ge(scaled, b)
                        nc.vector.tensor_tensor(X[:, b - 1, :], tmp2[:, (b - 1) % 2, :], beta[:], ALU.add).then_inc(moved, 1)
                dve.wait_ge(scaled, B)
                nc.vector.tensor_tensor(X[:, B - 1, :], tmp2[:, (B - 1) % 2, :], beta[:], ALU.add)

            @block.gpsimd
            def _(pool):
                for b in range(B):
                    pool.wait_ge(centred, b + 1)
                    if b >= 2:
                        pool.wait_ge(moved, b - 1)
                    nc.gpsimd.tensor_tensor(tmp2[:, b % 2, :], tmp[:, b % 2, :], gamma[:], ALU.mult).then_inc(scaled, 1)


def split_pair(nc, prefix, source, high, low):
    with Scope(nc, prefix) as sc:
        rounded = sc.sem("rounded")
        block = sc.block()

        @block.scalar
        def _(act):
            for b in range(B):
                nc.scalar.activation(high[:, b], source[:, b], ACT.Copy).then_inc(rounded, 1)

        @block.vector
        def _(dve):
            for b in range(B):
                dve.wait_ge(rounded, b + 1)
                nc.vector.tensor_tensor(low[:, b], source[:, b], high[:, b].bitcast(F32), ALU.subtract)


def gqa_layer(nc, a, X, ident, column):
    with Scope(nc, "l0") as sc:
        gamma, beta = sc.sb("gamma", [L, C]), sc.sb("beta", [L, C])
        Wq, Wo = (sc.sb(n, [P, CC, C]) for n in ("Wq", "Wo"))
        Wk, Wv = sc.sb("Wk", [P, CC, P]), sc.sb("Wv", [P, CC, P])
        bk, bv, heads_of = sc.sb("bk", [P, 1]), sc.sb("bv", [P, P]), sc.sb("heads_of", [P, HC])
        xT, qT = sc.sb("xT", [P, B, CC, L]), sc.sb("qT", [P, B, CC, L])
        qh = sc.sb("qh", [P, B, CC, L], F32R)
        out = sc.sb("out", [L, B, C])
        query_weights, other_weights = sc.sem("query_weights"), sc.sem("other_weights")
        start_copies(nc, "l0u", query_weights, [(Wq[:], by_chunks(a["L0_Wq"]))])
        start_copies(nc, "l0w", other_weights, [(Wk[:], by_chunks(a["L0_Wk"])), (Wo[:], by_chunks(a["L0_Wo"])),
                                 (Wv[:], by_chunks(a["L0_Wv"])), (bk[:], a["L0_bk"]), (bv[:], a["L0_bv"]),
                                 (heads_of[:], a["heads_of"]), (gamma[:], a["L0_gamma"]), (beta[:], a["L0_beta"])])
        transposed(nc, "l0x", X, ident, xT)
        await_copies(nc, "l0v", (query_weights, 1))
        add_row(nc, "l0b", X, a["L0_bo"])

        def keep_query(engine, n, half, bank):
            engine.tensor_scalar(qT[:, 4 * half:4 * half + 4, n, :], bank, column("L0_bq")[:, n:n + 1], float(D0) ** -0.5,
                                 ALU.add, ALU.mult)

        product_transposed(nc, "l0q", Wq, xT, keep_query, engines=("vector",))
        await_copies(nc, "l0y", (other_weights, 8))
        ql = xT[:].bitcast(F32R)
        split_pair(nc, "l0s", qT, qh, ql)
        grouped_attention(nc, qh, ql, Wk, Wv, bk, bv, heads_of, a["ctxT"], a["mask"], ident, out)
        transposed(nc, "l0t", out, ident, xT)
        product_rows(nc, "l0o", Wo, xT, lambda e, b, bank: e.tensor_tensor(X[:, b, :], X[:, b, :], bank, ALU.add))
        layer_norm_rows(nc, "l0n", X, 1e-6, gamma, beta)

HD = 16
HEADS_CHUNK = P // HD


def shifted_difference(nc, prefix, cur, before, out, mixes):
    with Scope(nc, prefix) as sc:
        done = sc.sem("done")
        block = sc.block()

        @block.vector
        def _(dve):
            flat = "p b c l -> p (b c) l"
            c3, o3 = cur.rearrange(flat), out.rearrange(flat)
            nc.vector.tensor_tensor(o3[:, :, 1:L], c3[:, :, 0:L - 1], c3[:, :, 1:L], ALU.subtract).then_inc(done, 1)
            nc.vector.tensor_tensor(o3[:, :, 0], before.rearrange("p b c -> p (b c)"), c3[:, :, 0], ALU.subtract).then_inc(done, 1)
            dve.wait_ge(done, 2)
            for col, dst in mixes:
                for c in range(CC):
                    nc.vector.scalar_tensor_tensor(dst[:, :, c, :], out[:, :, c, :], col[:, c:c + 1], cur[:, :, c, :],
                                                   ALU.mult, ALU.add)


def mix_and_product(nc, prefix, mixing=None, product=None):
    with Scope(nc, prefix) as sc:
        mbank = [sc.bank(f"mix{i}", [P, 4, P]) for i in range(4)]
        pbank = [sc.bank(f"prod{i}", [P, 4, P]) for i in range(4)]
        scaled = sc.sb("scaled", [P, 2, 4, L])
        mix_full, mix_scaled, mix_done = sc.sem("mix_full"), sc.sem("mix_scaled"), sc.sem("mix_done")
        full, kept = sc.sem("full"), sc.sem("kept")
        block = sc.block()
        mslots = [(half, n) for half in range(2) for n in range(CC)] if mixing else []
        pslots = [(half, n) for half in range(2) for n in range(product[0])] if product else []

        @block.tensor
        def _(pe):
            for u, (half, n) in enumerate(mslots):
                if u >= 4:
                    pe.wait_ge(mix_scaled, u - 3)
                nc.tensor.matmul(mbank[u % 4][:, :, 0:L], mixing[0](n), mixing[1](half), start=True, stop=True).then_inc(mix_full, 1)
            for u, (half, n) in enumerate(pslots):
                if u >= 4:
                    pe.wait_ge(kept, u - 3)
                terms = product[1](n, half)
                rows = terms[0][0].shape[-1]
                for k, (x, y) in enumerate(terms):
                    last = nc.tensor.matmul(pbank[u % 4][0:rows, :, 0:L], x, y, start=(k == 0), stop=(k == len(terms) - 1))
                last.then_inc(full, 1)

        @block.vector
        def _(dve):
            for u, (half, n) in enumerate(mslots):
                _, _, col, diff, cur, out = mixing
                dve.wait_ge(mix_full, u + 1)
                if u >= 2:
                    dve.wait_ge(mix_done, u - 1)
                nc.vector.scalar_tensor_tensor(scaled[:, u % 2], mbank[u % 4][:, :, 0:L], col[:, n:n + 1],
                                               diff[:, 4 * half:4 * half + 4, n, :], ALU.add, ALU.mult).then_inc(mix_scaled, 1)

        @block.gpsimd
        def _(pool):
            for u, (half, n) in enumerate(mslots):
                _, _, col, diff, cur, out = mixing
                pool.wait_ge(mix_scaled, u + 1)
                nc.gpsimd.tensor_tensor(out[:, 4 * half:4 * half + 4, n, :], scaled[:, u % 2],
                                        cur[:, 4 * half:4 * half + 4, n, :], ALU.add).then_inc(mix_done, 1)

        @block.scalar
        def _(act):
            for u, (half, n) in enumerate(pslots):
                act.wait_ge(full, u + 1)
                product[2](act, n, half, pbank[u % 4][0:product[1](n, half)[0][0].shape[-1], :, 0:L]).then_inc(kept, 1)


def recurrence(nc, key, value, decay, receive, first, bonus, spread, gather, blocks, out):
    N = CC * L
    AHEAD = 4
    EARLY = 3
    with Scope(nc, "rec") as sc:
        kb, vb, wb, rb = (sc.sb(n, [P, 2, CC, L]) for n in ("kb", "vb", "wb", "rb"))
        vh, vl = sc.sb("vh", [P, 2, CC, L], F32R), sc.sb("vl", [P, 2, CC, L], F32R)
        spreadr = sc.sb("spreadr", [P, HD, P], F32R)
        s0 = sc.sb("s0", [P, 2, HD, CC])
        rank1 = sc.sb("rank1", [P, HD, CC, L])
        state = [sc.sb(f"state{i}", [P, N]) for i in range(4)]
        seen = [sc.sb(f"seen{i}", [P, N]) for i in range(4)]
        ruk = sc.sb("ruk", [P, CC, L])
        now = sc.sb("now", [P, 2, N])
        mark = sc.sb("mark", [1, 4])
        spreadb = [sc.bank(f"spread{i}", [P, 4, P]) for i in range(AHEAD)]
        sumb = [sc.bank(f"sum{i}", [P, 4, P]) for i in range(2)]
        nowb = sc.bank("nowb", [P, 4, P])
        inputs_in = [sc.sem(f"inputs_in{i}") for i in range(2)]
        (spread_rounded, v_high, v_low, spread_full, rank1_done, first_done, scan_done, seen_done, gathered, ruk_done,
         now_full, now_done, out_done) = (sc.sem(n) for n in (
             "spread_rounded", "v_high", "v_low", "spread_full", "rank1_done", "first_done", "scan_done", "seen_done",
             "gathered", "ruk_done", "now_full", "now_done", "out_done"))
        SEEN0, GATHER0, NOW0, OUT0 = 4, 4, 1, 2
        block = sc.block()

        def one(t, b):
            return t[:, bass.ds(b, 1)].rearrange("p a c l -> p (a c) l")

        def batches(engine, body):
            with engine.Fori(0, B // 2 - 1) as j:
                body(2 * j, 0, False)
                body(2 * j + 1, 1, False)
            body(B - 2, 0, False)
            body(B - 1, 1, True)

        def inputs(engine, b, par):
            engine.wait_ge(inputs_in[par], 40 * b + (80 - 40 * par))

        @block.sync
        def _(sp):
            def load(b, par, last):
                sp.wait_ge(out_done, b - 1 + OUT0)
                for dst, src in ((kb, key), (vb, value), (wb, decay), (rb, receive)):
                    sp.dma_start(dst[:, par], one(src, b)).then_inc(inputs_in[par], 16)
                sp.dma_start(s0[:, par], first[bass.ds(b, 1)].rearrange("a p j c -> p (a j) c")).then_inc(inputs_in[par], 16)
            batches(sp, load)

        @block.scalar
        def _(act):
            nc.scalar.activation(spreadr[:], spread[:], ACT.Copy).then_inc(spread_rounded, 1)

            def high(b, par, last):
                inputs(act, b, par)
                nc.scalar.activation(vh[:, par], vb[:, par], ACT.Copy).then_inc(v_high, 1)
            batches(act, high)

        @block.tensor
        def _(pe):
            nc.tensor.matmul(nowb[0:1, 0, 0:2], blocks[:, 0:1], blocks[:, 0:2], start=True, stop=True).then_inc(gathered, GATHER0)
            pe.wait_ge(spread_rounded, 1)

            def spread_column(b, par, j, first=False):
                if j == 0:
                    pe.wait_ge(v_low, b + 1)
                if not first:
                    pe.wait_ge(rank1_done, HD * b + (j + 1 - AHEAD))
                nc.tensor.matmul(spreadb[j % AHEAD][:, :, 0:L], spreadr[:, j, :], vl[:, par], start=True, stop=False)
                nc.tensor.matmul(spreadb[j % AHEAD][:, :, 0:L], spreadr[:, j, :], vh[:, par], start=False, stop=True).then_inc(spread_full, 1)

            for j in range(AHEAD):
                spread_column(0, 0, j, first=True)

            def body(b, par, last):
                for j in range(HD):
                    if j + AHEAD < HD:
                        spread_column(b, par, j + AHEAD)
                    elif not last:
                        spread_column(b + 1, 1 - par, j + AHEAD - HD)
                    if j == 2:
                        pe.wait_ge(ruk_done, CC * b + CC)
                        pe.wait_ge(now_done, b + NOW0)
                        nc.tensor.matmul(nowb[:, :, 0:L], blocks[:], ruk[:], start=True, stop=True).then_inc(now_full, 1)
                    if j == 0:
                        pe.wait_ge(out_done, b - 1 + OUT0)
                    pe.wait_ge(seen_done, HD * b + j + 1 + SEEN0)
                    nc.tensor.matmul(sumb[par][:, :, 0:L], gather[:, j, :],
                                     seen[j % 4][:].rearrange("p (c l) -> p c l", l=L),
                                     start=(j == 0), stop=(j == HD - 1)).then_inc(gathered, 1)
            batches(pe, body)

        @block.gpsimd
        def _(pool):
            nc.gpsimd.memset(mark[:, 0:1], 0.0).then_inc(seen_done, SEEN0)

            def body(b, par, last):
                inputs(pool, b, par)
                for j in range(HD):
                    pool.wait_ge(scan_done, HD * b + j + 1)
                    pool.wait_ge(gathered, HD * b + j - 3 + GATHER0)
                    nc.gpsimd.tensor_tensor(seen[j % 4][:], state[j % 4][:], rb[:, par].rearrange("p c l -> p (c l)"),
                                            ALU.mult).then_inc(seen_done, 1)
            batches(pool, body)

        @block.vector
        def _(dve):
            nc.vector.memset(mark[:, 2:3], 0.0).then_inc(now_done, NOW0)
            nc.vector.memset(mark[:, 3:4], 0.0).then_inc(out_done, OUT0)

            def low(b, par):
                inputs(dve, b, par)
                dve.wait_ge(v_high, b + 1)
                nc.vector.tensor_tensor(vl[:, par], vb[:, par], vh[:, par].bitcast(F32), ALU.subtract).then_inc(v_low, 1)

            def rank1_column(b, par, j):
                dve.wait_ge(spread_full, HD * b + j + 1)
                nc.vector.tensor_tensor(rank1[:, j, :, 1:L], spreadb[j % AHEAD][:, :, 0:L - 1], kb[:, par, :, 0:L - 1],
                                        ALU.mult).then_inc(rank1_done, 1)

            def column(b, par, j):
                if j + 1 < HD:
                    rank1_column(b, par, j + 1)
                dve.wait_ge(rank1_done, HD * b + j + 1)
                dve.wait_ge(seen_done, HD * b + j - 3 + SEEN0)
                nc.vector.tensor_tensor_scan(state[j % 4][:], wb[:, par].rearrange("p c l -> p (c l)"),
                                             rank1[:, j].rearrange("p c l -> p (c l)"), 0.0,
                                             ALU.mult, ALU.add).then_inc(scan_done, 1)

            def begin(b, par, first=False):
                if not first:
                    dve.wait_ge(scan_done, HD * b)
                nc.vector.tensor_copy(rank1[:, :, :, 0], s0[:, par]).then_inc(first_done, 1)
                rank1_column(b, par, 0)
                dve.wait_ge(first_done, b + 1)
                column(b, par, 0)
                for c in range(CC):
                    nc.vector.scalar_tensor_tensor(ruk[:, c, :], rb[:, par, c, :], bonus[:, c:c + 1], kb[:, par, c, :],
                                                   ALU.mult, ALU.mult).then_inc(ruk_done, 1)
                for j in range(1, EARLY):
                    column(b, par, j)

            low(0, 0)
            begin(0, 0, first=True)

            def body(b, par, last):
                for j in range(EARLY, HD):
                    column(b, par, j)
                    if j == 7:
                        dve.wait_ge(now_full, b + 1)
                        nc.vector.tensor_tensor(now[:, par].rearrange("p (c l) -> p c l", l=L), nowb[:, :, 0:L], vb[:, par],
                                                ALU.mult).then_inc(now_done, 1)
                    if j == 9 and not last:
                        low(b + 1, 1 - par)
                if not last:
                    begin(b + 1, 1 - par)
                dve.wait_ge(now_done, b + 1 + NOW0)
                dve.wait_ge(gathered, HD * b + HD + GATHER0)
                nc.vector.tensor_tensor(one(out, b), sumb[par][:, :, 0:L], now[:, par].rearrange("p (c l) -> p c l", l=L),
                                        ALU.add).then_inc(out_done, 1)
            batches(dve, body)


def head_norm(nc, y, dev, sq, means, scale, offset, gate, eps, out):
    slots = [(half, n) for half in range(2) for n in range(CC)]

    def part(t, half, n):
        return t[:, 4 * half:4 * half + 4, n, :]

    with Scope(nc, "hn") as sc:
        banks = [sc.bank(f"bank{i}", [P, 4, P]) for i in range(8)]
        root = sc.sb("root", [P, 2, 4, L])
        spread = sc.sb("spread", [P, 2, 4, L])
        epst = sc.sb("epst", [P, 1])
        (mean_full, dev_done, sq_done, var_full, root_done, inv_done, norm_done, affine_done, eps_set, out_done) = (
            sc.sem(n) for n in ("mean_full", "dev_done", "sq_done", "var_full", "root_done", "inv_done",
                                "norm_done", "affine_done", "eps_set", "out_done"))
        block = sc.block()

        @block.tensor
        def _(pe):
            for u, (half, n) in enumerate(slots):
                nc.tensor.matmul(banks[u][:, :, 0:L], means[:], part(y, half, n), start=True, stop=True).then_inc(mean_full, 1)
            for u, (half, n) in enumerate(slots):
                pe.wait_ge(sq_done, u + 1)
                nc.tensor.matmul(banks[u][:, :, 0:L], means[:], part(sq, half, n), start=True, stop=True).then_inc(var_full, 1)

        @block.scalar
        def _(act):
            for u, (half, n) in enumerate(slots):
                act.wait_ge(dev_done, u + 1)
                nc.scalar.activation(part(sq, half, n), part(dev, half, n), ACT.Square).then_inc(sq_done, 1)
            act.wait_ge(eps_set, 1)
            for u, (half, n) in enumerate(slots):
                act.wait_ge(var_full, u + 1)
                if u >= 2:
                    act.wait_ge(inv_done, u - 1)
                nc.scalar.activation(root[:, u % 2], banks[u][:, :, 0:L], ACT.Sqrt, bias=epst[:, 0:1]).then_inc(root_done, 1)

        @block.vector
        def _(dve):
            nc.vector.memset(epst[:], eps).then_inc(eps_set, 1)
            for u, (half, n) in enumerate(slots):
                dve.wait_ge(mean_full, u + 1)
                nc.vector.tensor_tensor(part(dev, half, n), part(y, half, n), banks[u][:, :, 0:L], ALU.subtract).then_inc(dev_done, 1)
            for u, (half, n) in enumerate(slots):
                dve.wait_ge(root_done, u + 1)
                if u >= 2:
                    dve.wait_ge(norm_done, u - 1)
                nc.vector.reciprocal(spread[:, u % 2], root[:, u % 2]).then_inc(inv_done, 1)
                dve.wait_ge(inv_done, u + 1)
                nc.vector.tensor_tensor(part(sq, half, n), part(dev, half, n), spread[:, u % 2], ALU.mult).then_inc(norm_done, 1)
                dve.wait_ge(norm_done, u + 1)
                nc.vector.tensor_scalar(part(dev, half, n), part(sq, half, n), scale[:, n:n + 1], offset[:, n:n + 1],
                                        ALU.mult, ALU.add).then_inc(affine_done, 1)

        @block.gpsimd
        def _(pool):
            for u, (half, n) in enumerate(slots):
                pool.wait_ge(affine_done, u + 1)
                nc.gpsimd.tensor_tensor(part(out, half, n), part(dev, half, n), part(gate, half, n), ALU.mult).then_inc(out_done, 1)


def rwkv_layer(nc, a, X, ident, column):
    def col(n):
        return column(f"L1_xattn_{n}")

    def tokens(t, half):
        return t[:, 4 * half:4 * half + 4, :]

    with Scope(nc, "l1") as sc:
        big = [P, B, CC, L]
        before = sc.sb("before", [P, 2, B, CC])
        with Scope(nc, "l1t") as st:
            W = {n: st.sb(n, [P, CC, C]) for n in ("WkT", "WvT", "WrT", "WgT")}
            w1, w2 = st.sb("w1", [P, CC, 5 * 32]), st.sb("w2", [P, C])
            w2g = st.sb("w2g", [32, C])
            d1, d2 = st.sb("d1", [P, CC, 64]), st.sb("d2", [64, C])
            low, lowg, lowd = st.sb("low", [P, B, L]), st.sb("lowg", [32, B, L]), st.sb("lowd", [64, B, L])
            cur, diff = st.sb("cur", big), st.sb("diff", big)
            mix = [st.sb(f"mix{i}", big) for i in range(2)]
            key, value, decay, receive, gate = (st.sb(n, big) for n in ("key", "value", "decay", "receive", "gate"))
            grow = st.sb("grow", [P, 2, 4, L])
            loaded, kept = st.sem("loaded"), st.sem("kept")
            start_copies(nc, "l1w", loaded, [(before[:], a["before"]), (w1[:], by_chunks(a["L1_maa_w1"])), (w2[:], a["L1_maa_w2"][0:P, :]),
                                     (w2g[:], a["L1_maa_w2"][P:, :]), (d1[:], by_chunks(a["L1_decay_w1"])),
                                     (d2[:], a["L1_decay_w2"])] + [(W[n][:], by_chunks(a[f"L1_{n}"])) for n in W])
            layer_norm_transposed(nc, "l1a", X, 1e-5, col("ln1_w"), col("ln1_b"), ident, lambda b: (cur[:, b],), "plain")
            await_copies(nc, "l1j", (loaded, 10))
            shifted_difference(nc, "l1d", cur[:], before[:, 1], diff[:], [(col("maa_x"), mix[0])])

            def dense(weight, source):
                return lambda n, half: [(weight[:, c, n * P:(n + 1) * P], source[:, 4 * half:4 * half + 4, c, :]) for c in range(CC)]

            def keep(out, func=ACT.Copy):
                return lambda act, n, half, bank: nc.scalar.activation(out[:, 4 * half:4 * half + 4, n, :], bank, func)

            mix_and_product(nc, "l1m", product=(
                1, lambda n, half: [(w1[:, c, 0:P], mix[0][:, 4 * half:4 * half + 4, c, :]) for c in range(CC)],
                lambda act, n, half, bank: nc.scalar.activation(tokens(low, half), bank, ACT.Tanh)))
            mix_and_product(nc, "l1n", product=(
                1, lambda n, half: [(w1[:, c, P:P + 32], mix[0][:, 4 * half:4 * half + 4, c, :]) for c in range(CC)],
                lambda act, n, half, bank: nc.scalar.activation(tokens(lowg, half), bank, ACT.Tanh)))

            def mixing(f, out):
                name = "wkvrg"[f]
                if f < 4:
                    return (lambda n: w2[32 * f:32 * f + 32, n * P:(n + 1) * P], lambda half: low[32 * f:32 * f + 32, 4 * half:4 * half + 4, :],
                            col(f"maa_{name}"), diff, cur, out)
                return lambda n: w2g[:, n * P:(n + 1) * P], lambda half: tokens(lowg, half), col("maa_g"), diff, cur, out

            grown = st.sem("grown")
            grown_count = [0]

            def keep_decay(act, n, half, bank):
                g = grow[:, grown_count[0] % 2]
                grown_count[0] += 1
                nc.scalar.activation(g, bank, ACT.Exp, bias=col("time_decay")[:, n:n + 1]).then_inc(grown, 1)
                act.wait_ge(grown, grown_count[0])
                return nc.scalar.activation(decay[:, 4 * half:4 * half + 4, n, 1:L], g[:, :, 0:L - 1], ACT.Exp, scale=-1.0)

            mix_and_product(nc, "l1o", mixing(0, mix[1]))
            mix_and_product(nc, "l1p", mixing(1, mix[0]), (
                1, lambda n, half: [(d1[:, c, :], mix[1][:, 4 * half:4 * half + 4, c, :]) for c in range(CC)],
                lambda act, n, half, bank: nc.scalar.activation(tokens(lowd, half), bank, ACT.Tanh)))
            clear(nc, decay[:].rearrange("p b c l -> p (b c) l")[:, :, 0])
            mix_and_product(nc, "l1q", None, (CC, lambda n, half: [(d2[:, n * P:(n + 1) * P], tokens(lowd, half))], keep_decay))
            keep_in_dram(nc, "decay", decay, a, kept)
            mix_and_product(nc, "l1r", mixing(2, mix[1]), (CC, dense(W["WkT"], mix[0]), keep(key)))
            keep_in_dram(nc, "key", key, a, kept)
            mix_and_product(nc, "l1s", mixing(3, mix[0]), (CC, dense(W["WvT"], mix[1]), keep(value)))
            keep_in_dram(nc, "value", value, a, kept)
            mix_and_product(nc, "l1u", mixing(4, mix[1]), (CC, dense(W["WrT"], mix[0]), keep(receive)))
            keep_in_dram(nc, "receive", receive, a, kept)
            mix_and_product(nc, "l1v", None, (CC, dense(W["WgT"], mix[1]), keep(gate, ACT.Silu)))
            keep_in_dram(nc, "gate", gate, a, kept)
            await_copies(nc, "l1k", (kept, 5))
        y, gate = sc.sb("y", big), sc.sb("gate2", big)
        means = sc.sb("means", [P, P])
        W = {n: sc.sb(n, [P, CC, C]) for n in ("WoT", "fWkT", "fWrT", "fWvT")}
        later = sc.sem("later")
        with Scope(nc, "l1c") as st:
            spread, gather = st.sb("spread", [P, HD, P]), st.sb("gather", [P, HD, P])
            blocks = st.sb("blocks", [P, P])
            matrices = st.sem("matrices")
            start_copies(nc, "l1x", matrices, [(spread[:], a["spread"]), (gather[:], a["gather"]), (blocks[:], a["blocks"])])
            await_copies(nc, "l1t", (matrices, 3))
            start_copies(nc, "l1y", later, [(means[:], a["means"]), (gate[:], a["kept_gate"])] + [(W[n][:], by_chunks(a[f"L1_{n}"])) for n in W])
            recurrence(nc, a["kept_key"], a["kept_value"], a["kept_decay"], a["kept_receive"], a["first"], col("faaaa"),
                       spread, gather, blocks, y)
        with Scope(nc, "l1e") as st:
            dev, sq, z = st.sb("dev", big), st.sb("sq", big), st.sb("z", big)
            rr = st.sb("rr", [L, B, C])
            tmp = st.sb("tmp", [L, 2, C])
            await_copies(nc, "l1aw", (later, 6))
            head_norm(nc, y, dev, sq, means, col("gn_w"), col("gn_b"), gate, 1e-5, z)
            product_rows(nc, "l1z", W["WoT"], z, lambda e, b, bank: e.tensor_tensor(X[:, b, :], X[:, b, :], bank, ALU.add))
            layer_norm_transposed(nc, "l1b", X, 1e-5, col("ln2_w"), col("ln2_b"), ident, lambda b: (y[:, b],), "plain")
            shifted_difference(nc, "l1f", y[:], before[:, 0], dev[:], [(col("fmaa_k"), sq), (col("fmaa_r"), z)])
            product_rows(nc, "l1g", W["fWrT"], z, lambda e, b, bank: e.activation(rr[:, b, :], bank, ACT.Sigmoid), "scalar")
            product_transposed(nc, "l1h", W["fWkT"], sq, lambda e, n, half, bank: e.activation(dev[:, 4 * half:4 * half + 4, n, :], bank, ACT.Relu),
                               engines=("scalar",))
            square(nc, dev[:].rearrange("p b c l -> p (b c l)"))
            gated = st.sem("gated")

            def add_gated(e, b, bank):
                e.tensor_tensor(tmp[:, b % 2, :], bank, rr[:, b, :], ALU.mult).then_inc(gated, 1)
                e.wait_ge(gated, b + 1)
                e.tensor_tensor(X[:, b, :], X[:, b, :], tmp[:, b % 2, :], ALU.add)

            product_rows(nc, "l1i", W["fWvT"], dev, add_gated)


def clear(nc, t):
    with Scope(nc, "clear") as sc:
        block = sc.block()

        @block.vector
        def _(dve):
            nc.vector.memset(t, 0.0)


def square(nc, t):
    with Scope(nc, "square") as sc:
        block = sc.block()

        @block.vector
        def _(dve):
            nc.vector.tensor_tensor(t, t, t, ALU.mult)


def keep_in_dram(nc, name, t, a, kept):
    a[f"kept_{name}"] = nc.dram_tensor(f"kept_{name}", tuple(t.shape), F32).ap()
    start_copies(nc, f"keep_{name}", kept, [(a[f"kept_{name}"], t[:])])


def start_copies(nc, prefix, sem, pairs):
    with Scope(nc, prefix) as sc:
        block = sc.block()

        @block.sync
        def _(sp):
            for tile, src in pairs:
                sp.dma_start(tile, src).then_inc(sem, 16)


def await_copies(nc, prefix, *waits):
    with Scope(nc, prefix) as sc:
        block = sc.block()

        @block.sync
        def _(sp):
            for sem, count in waits:
                sp.wait_ge(sem, 16 * count)


def by_chunks(w):
    return w.rearrange("(c p) n -> p c n", p=P)


def product_transposed(nc, prefix, weight, source, store, engines=("scalar", "vector"), tiles=CC):
    with Scope(nc, prefix) as sc:
        banks = [sc.bank(f"bank{i}", [P, 4, P]) for i in range(2 * tiles)]
        full = sc.sem("full")
        block = sc.block()
        slots = [(half, n) for half in range(2) for n in range(tiles)]

        @block.tensor
        def _(pe):
            for u, (half, n) in enumerate(slots):
                for c in range(CC):
                    last = nc.tensor.matmul(banks[u][:, :, 0:L], weight[:, c, n * P:(n + 1) * P],
                                            source[:, 4 * half:4 * half + 4, c, :], start=(c == 0), stop=(c == CC - 1))
                last.then_inc(full, 1)

        def keep(name, engine, other):
            for u, (half, n) in enumerate(slots):
                if engines[u % len(engines)] == name:
                    other.wait_ge(full, u + 1)
                    store(engine, n, half, banks[u][:, :, 0:L])

        @block.scalar
        def _(act):
            keep("scalar", nc.scalar, act)

        @block.vector
        def _(dve):
            keep("vector", nc.vector, dve)


def product_rows(nc, prefix, weight, source, store, engine_name="vector"):
    with Scope(nc, prefix) as sc:
        banks = [sc.bank(f"bank{i}") for i in range(B)]
        full = sc.sem("full")
        block = sc.block()

        @block.tensor
        def _(pe):
            for b in range(B):
                for c in range(CC):
                    last = nc.tensor.matmul(banks[b][0:L, :], source[:, b, c, :], weight[:, c, :],
                                            start=(c == 0), stop=(c == CC - 1))
                last.then_inc(full, 1)

        if engine_name == "vector":
            @block.vector
            def _(dve):
                for b in range(B):
                    dve.wait_ge(full, b + 1)
                    store(nc.vector, b, banks[b][0:L, :])
        else:
            @block.scalar
            def _(act):
                for b in range(B):
                    act.wait_ge(full, b + 1)
                    store(nc.scalar, b, banks[b][0:L, :])


def transposed(nc, prefix, X, ident, out):
    with Scope(nc, prefix) as sc:
        banks = [sc.bank(f"bank{i}", [P, CC, P]) for i in range(B)]
        full = sc.sem("full")
        block = sc.block()

        @block.tensor
        def _(pe):
            for b in range(B):
                for c in range(CC):
                    last = nc.tensor.transpose(banks[b][:, c, 0:L], X[:, b, c * P:(c + 1) * P], ident[0:L, 0:L])
                last.then_inc(full, 1)

        @block.scalar
        def _(act):
            for b in range(0, B, 2):
                act.wait_ge(full, b + 1)
                nc.scalar.activation(out[:, b], banks[b][:, :, 0:L], ACT.Copy)

        @block.vector
        def _(dve):
            for b in range(1, B, 2):
                dve.wait_ge(full, b + 1)
                nc.vector.tensor_copy(out[:, b], banks[b][:, :, 0:L])


def store_copy(out):
    def store(engine, n, half, bank):
        dst = out[:, 4 * half:4 * half + 4, n, :]
        if hasattr(engine, "activation"):
            return engine.activation(dst, bank, ACT.Copy)
        return engine.tensor_copy(dst, bank)
    return store


def plain_attention_layer(nc, a, X, ident):
    scale = float(C) ** -0.5
    with Scope(nc, "l2") as sc:
        w = {n: sc.sb(n, [P, CC, C]) for n in ("w_qT", "w_k", "w_vT", "w_oT")}
        alpha = sc.sb("alpha", [L, 1])
        one, two = sc.sb("one", [P, B, CC, L]), sc.sb("two", [P, B, CC, L])
        query_weights, other_weights = sc.sem("query_weights"), sc.sem("other_weights")
        start_copies(nc, "l2w", query_weights, [(w[n][:], by_chunks(a[f"L2_{n}"])) for n in ("w_qT", "w_k")])
        start_copies(nc, "l2z", other_weights, [(w[n][:], by_chunks(a[f"L2_{n}"])) for n in ("w_vT", "w_oT")] + [(alpha[:], a["alpha_rows"])])
        transposed(nc, "l2x", X, ident, one)
        await_copies(nc, "l2u", (query_weights, 2))
        product_transposed(nc, "l2q", w["w_qT"], one, store_copy(two))
        product_transposed(nc, "l2k", w["w_k"], two, store_copy(one))
        with Scope(nc, "l2a") as s2:
            CB = 4
            ctxT = s2.sb("ctxT", [P, CB, CC, SP])
            ctxN = s2.sb("ctxN", [P, CB, 3, C])
            probs = s2.sb("probs", [L, 2, S])
            turned = s2.sb("turned", [P, 2, 3, L])
            top, shift = s2.sb("top", [L, B]), s2.sb("shift", [L, B])
            total, share = s2.sb("total", [L, B]), s2.sb("share", [L, B])
            score = [s2.bank(f"score{i}") for i in range(2)]
            turn = [s2.bank(f"turn{i}", [P, CC, P]) for i in range(2)]
            mixed = [s2.bank(f"mixed{i}", [P, CC, P]) for i in range(2)]
            in_t = [s2.sem(f"in_t{i}") for i in range(CB)]
            in_n = [s2.sem(f"in_n{i}") for i in range(CB)]
            (score_full, top_done, shift_done, exp_done, share_done, probs_done, turn_full, turned_done,
             mixed_full, mixed_done) = (s2.sem(n) for n in (
                 "score_full", "top_done", "shift_done", "exp_done", "share_done", "probs_done", "turn_full",
                 "turned_done", "mixed_full", "mixed_done"))
            block = s2.block()

            @block.sync
            def _(sp):
                for b in range(B):
                    if b >= CB:
                        sp.wait_ge(mixed_full, b - CB + 1)
                    sp.dma_start(ctxT[:, b % CB], a["ctxT"][b]).then_inc(in_t[b % CB], 16)
                    sp.dma_start(ctxN[:, b % CB, 0:2, :], a["ctx"][b, 0:2 * P, :].rearrange("(t p) c -> p t c", p=P)).then_inc(in_n[b % CB], 16)
                    sp.dma_start(ctxN[0:S - 2 * P, b % CB, 2, :], a["ctx"][b, 2 * P:S, :]).then_inc(in_n[b % CB], 16)

            @block.tensor
            def _(pe):
                def scores(b):
                    pe.wait_ge(in_t[b % CB], 16 * (b // CB + 1))
                    if b >= 2:
                        pe.wait_ge(exp_done, b - 1)
                    for c in range(CC):
                        last = nc.tensor.matmul(score[b % 2][0:L, 0:S], one[:, b, c, :], ctxT[:, b % CB, c, 0:S],
                                                start=(c == 0), stop=(c == CC - 1))
                    last.then_inc(score_full, 1)

                scores(0)
                for b in range(B):
                    if b + 1 < B:
                        scores(b + 1)
                    pe.wait_ge(probs_done, b + 1)
                    if b >= 2:
                        pe.wait_ge(turned_done, 2 * (b - 1))
                    for t, (s0, rows) in enumerate(STILES):
                        last = nc.tensor.transpose(turn[b % 2][0:rows, t, 0:L], probs[:, b % 2, s0:s0 + rows], ident[0:L, 0:L])
                    last.then_inc(turn_full, 1)
                    pe.wait_ge(turned_done, 2 * (b + 1))
                    pe.wait_ge(in_n[b % CB], 32 * (b // CB + 1))
                    if b >= 2:
                        pe.wait_ge(mixed_done, b - 1)
                    for c in range(CC):
                        for t, (s0, rows) in enumerate(STILES):
                            last = nc.tensor.matmul(mixed[b % 2][:, c, 0:L], ctxN[0:rows, b % CB, t, c * P:(c + 1) * P],
                                                    turned[0:rows, b % 2, t, :], start=(t == 0), stop=(t == 2))
                    last.then_inc(mixed_full, 1)

            @block.scalar
            def _(act):
                for b in range(B):
                    act.wait_ge(shift_done, b + 1)
                    if b >= 2:
                        act.wait_ge(turn_full, b - 1)
                    nc.scalar.activation(probs[:, b % 2, :], score[b % 2][0:L, 0:S], ACT.Exp, bias=shift[:, b:b + 1],
                                         scale=scale, accum_out=total[:, b:b + 1]).then_inc(exp_done, 1)
                    act.wait_ge(turn_full, b + 1)
                    if b >= 2:
                        act.wait_ge(mixed_full, b - 1)
                    nc.scalar.activation(turned[:, b % 2, 0:2, :], turn[b % 2][:, 0:2, 0:L], ACT.Copy).then_inc(turned_done, 1)
                    rows = STILES[2][1]
                    nc.scalar.activation(turned[0:rows, b % 2, 2, :], turn[b % 2][0:rows, 2, 0:L], ACT.Copy).then_inc(turned_done, 1)

            @block.vector
            def _(dve):
                def maxima(b):
                    dve.wait_ge(score_full, b + 1)
                    nc.vector.reduce_max(top[:, b:b + 1], score[b % 2][0:L, 0:S], AX_X).then_inc(top_done, 1)
                    dve.wait_ge(top_done, b + 1)
                    nc.vector.tensor_scalar(shift[:, b:b + 1], top[:, b:b + 1], -scale, None, ALU.mult).then_inc(shift_done, 1)

                maxima(0)
                for b in range(B):
                    dve.wait_ge(exp_done, b + 1)
                    nc.vector.reciprocal(share[:, b:b + 1], total[:, b:b + 1]).then_inc(share_done, 1)
                    dve.wait_ge(share_done, b + 1)
                    nc.vector.tensor_scalar(probs[:, b % 2, :], probs[:, b % 2, :], share[:, b:b + 1], None,
                                            ALU.mult).then_inc(probs_done, 1)
                    if b + 1 < B:
                        maxima(b + 1)
                    dve.wait_ge(mixed_full, b + 1)
                    nc.vector.tensor_copy(two[:, b], mixed[b % 2][:, :, 0:L]).then_inc(mixed_done, 1)

        await_copies(nc, "l2t", (other_weights, 3))
        product_transposed(nc, "l2v", w["w_vT"], two, store_copy(one))

        def add_scaled(engine, b, bank):
            engine.scalar_tensor_tensor(X[:, b, :], bank, alpha[:, 0:1], X[:, b, :], ALU.mult, ALU.add)

        product_rows(nc, "l2o", w["w_oT"], one, add_scaled)

H3, K3 = 16, 128
G3 = 4
NG3 = H3 // G3
F3 = 2048
RING = 4
W3 = G3 * K3
BH = B // 2
U_K, U_T, U_AV, U_V = 0, 4, 7, 8
UNITS = 11
FILLED = {U_AV: 9, U_V: 9, U_V + 1: 10, U_V + 2: 11}
BANK = {U_AV: 0, U_V: RING + 1, U_V + 1: 2, U_V + 2: 3}


def load_group(engine, raw, weights, m, g):
    if m < 3:
        src = weights.rearrange("(c p) n -> p c n", p=P)[:, :, bass.ds(g * W3, W3)]
    else:
        src = weights.rearrange("(h p) n -> p h n", p=P)[:, bass.ds(g * G3, G3), :]
    return engine.dma_start(raw[:, m % 2, :].rearrange("p (c n) -> p c n", c=CC), src)


def cross_attention(nc, prefix, X, highT, lowT, ctxT, weights, head_columns, value_rows, bias_rows, scratch, ident,
                    raw, craw, raw_in, ctx_in):
    scale = float(K3) ** -0.5
    W = W3
    steps = NG3 * B
    with Scope(nc, prefix) as sc:
        wh = sc.sb("wh", [P, 4, CC * W], F32R)
        wl = sc.sb("wl", [P, 4, CC * W], F32R)
        columns = sc.sb("columns", [P, H3 * 4])
        keyh, keyl = sc.sb("keyh", [P, H3], F32R), sc.sb("keyl", [P, H3], F32R)
        ch = sc.sb("ch", [P, 2, CC, SP], F32R)
        cl = sc.sb("cl", [P, 2, CC, SP], F32R)
        qh, ql = sc.sb("qh", [P, G3, HALF], F32R), sc.sb("ql", [P, G3, HALF], F32R)
        kh, kl = sc.sb("kh", [P, G3, SP], F32R), sc.sb("kl", [P, G3, SP], F32R)
        vh, vl = sc.sb("vh", [P, 3, W], F32R), sc.sb("vl", [P, 3, W], F32R)
        probs = sc.sb("probs", [L, G3, SP])
        pp = sc.sb("pp", [P, 3, 2, G3 * L], F32R)
        mid = sc.sb("mid", [P, G3, L])
        oh, ol = sc.sb("oh", [P, G3, L], F32R), sc.sb("ol", [P, G3, L], F32R)
        top, shift = sc.sb("top", [L, G3]), sc.sb("shift", [L, G3])
        total, share = sc.sb("total", [L, G3]), sc.sb("share", [L, G3])
        early = probs[:].rearrange("l h s -> l (h s)")
        bias = early[:, 0:C]
        vrow = early[0:H3, C:C + 2 * K3].rearrange("h (i k) -> h i k", k=K3)
        vdiff = early[0:H3, C + 2 * K3:C + 3 * K3]
        vdh, vdl = sc.sb("vdh", [H3, K3], F32R), sc.sb("vdl", [H3, K3], F32R)
        nothing = sc.sb("nothing", [P, 1])
        mark = sc.sb("mark", [1, 2])

        ring = [sc.bank(f"ring{i}") for i in range(RING)]
        score = [sc.bank(f"score{i}") for i in range(G3)]
        banks = ring + score

        (columns_in, rows_in, bias_in, bias_added, rows_out, extra_put, nothing_set,
         key_high, key_ready, diff_ready, diff_high, diff_split, keyx_ready,
         weight_high, weight_ready, ctx_high, ctx_ready,
         ring_full, part_kept, mid_ready, high_done, bank_free, score_full, top_done, shift_ready,
         exp_done, share_ready, probs_ready, out_full, added) = (sc.sem(n) for n in (
             "columns_in", "rows_in", "bias_in", "bias_added", "rows_out", "extra_put", "nothing_set",
             "key_high", "key_ready", "diff_ready", "diff_high", "diff_split", "keyx_ready",
             "weight_high", "weight_ready", "ctx_high", "ctx_ready",
             "ring_full", "part_kept", "mid_ready", "high_done", "bank_free", "score_full", "top_done", "shift_ready",
             "exp_done", "share_ready", "probs_ready", "out_full", "added"))
        ADDED0 = 1
        block = sc.block()

        def before(n, i):
            halves = (n - i) // BH + 1 if i else 0
            return UNITS * n + halves * G3

        def pair_parts(pair):
            bank = (banks[BANK[U_AV]], score[2])[pair]
            return bank[:, 0:4 * L].rearrange("p (h i l) -> p h i l", i=2, l=L)

        def column(i, n, h):
            return columns[:, bass.ds((n // B) * (4 * G3) + h * 4 + i, 1)]

        def steps_of(engine, step, after):
            step(0, 0)
            with engine.Fori(0, steps // BH - 1) as m:
                for i in range(1, BH + 1):
                    step(m * BH + i, i)
            for i in range(1, BH):
                step(steps - BH + i, i)
            after(steps)

        @block.sync
        def _(sp):
            sp.dma_start(columns[:], head_columns).then_inc(columns_in, 16)
            sp.dma_start(vrow, value_rows).then_inc(rows_in, 16)
            sp.dma_start(bias, bias_rows).then_inc(bias_in, 16)
            sp.wait_ge(diff_split, 2)
            sp.dma_start(scratch[0], vdh[:].bitcast(F32)).then_inc(rows_out, 16)
            sp.dma_start(scratch[1], vdl[:].bitcast(F32)).then_inc(rows_out, 16)

            def load_weights(g, m):
                sp.wait_ge(weight_ready, 4 * g + m - 1)
                load_group(sp, raw, weights[m], m, g).then_inc(raw_in[m % 2], 16)

            def load_context(n):
                sp.wait_ge(ctx_ready, n)
                sp.dma_start(craw[:], ctxT[bass.ds(n % B, 1)].rearrange("a p c s -> p (a c) s")).then_inc(ctx_in, 16)

            load_weights(0, 2)
            load_context(1)
            load_weights(0, 3)
            with sp.Fori(0, NG3 - 1) as g:
                load_context(g * B + 2)
                load_weights(g + 1, 0)
                load_weights(g + 1, 1)
                for b in (3, 4, 5, 6):
                    load_context(g * B + b)
                load_weights(g + 1, 2)
                for b in (7, 8, 9):
                    load_context(g * B + b)
                load_weights(g + 1, 3)
            for n in range(B * (NG3 - 1) + 2, steps):
                load_context(n)

        @block.gpsimd
        def _(pool):
            nc.gpsimd.memset(nothing[:], 0.0).then_inc(nothing_set, 1)
            pool.wait_ge(nothing_set, 1)
            pool.wait_ge(key_ready, 1)

            def flat(t):
                return t.rearrange("p c s -> p (c s)")

            def split_context(n, parity, wait=True, more=0):
                pool.wait_ge(ctx_in, 16 * n + 16)
                if wait:
                    pool.wait_ge(ring_full, before_any(n - 1) + more)
                nc.gpsimd.tensor_tensor(flat(ch[:, parity]), flat(craw[:]), nothing[:].broadcast_to([P, CC * SP]), ALU.add).then_inc(ctx_high, 1)
                pool.wait_ge(ctx_high, n + 1)
                nc.gpsimd.tensor_tensor(cl[:, parity], craw[:], ch[:, parity].bitcast(F32),
                                        ALU.subtract).then_inc(ctx_ready, 1)

            def before_any(n):
                return UNITS * n + ((n + BH - 1) // BH) * G3

            def split_weights(g, m):
                past = (before_any(g * B - BH) + G3, before_any(g * B - 1) + U_T, before_any(g * B), before_any(g * B + 1) + 1)
                pool.wait_ge(raw_in[m % 2], 32 * g + 16 * (m // 2) + 16)
                pool.wait_ge(ring_full, past[m])
                nc.gpsimd.tensor_tensor(wh[:, m, :], raw[:, m % 2, :], nothing[:].broadcast_to([P, CC * W]), ALU.add).then_inc(weight_high, 1)
                pool.wait_ge(weight_high, 4 * g + m + 1)
                nc.gpsimd.tensor_tensor(wl[:, m, :], raw[:, m % 2, :], wh[:, m, :].bitcast(F32),
                                        ALU.subtract).then_inc(weight_ready, 1)

            def learned_key(g):
                nc.gpsimd.tensor_copy(kh[:, :, S], keyh[:, bass.ds(g * G3, G3)].bitcast(F32)).then_inc(keyx_ready, 1)
                nc.gpsimd.tensor_copy(kl[:, :, S], keyl[:, bass.ds(g * G3, G3)].bitcast(F32)).then_inc(keyx_ready, 1)

            split_context(0, 0, False)
            pool.wait_ge(bias_in, 16)
            for b in range(B):
                nc.gpsimd.tensor_tensor(X[:, b, :], X[:, b, :], bias, ALU.add).then_inc(bias_added, 1)
            split_context(1, 1, False)
            learned_key(0)
            with pool.Fori(0, NG3 - 1) as g:
                for b in (2, 3, 4, 5):
                    split_context(g * B + b, b % 2)
                split_weights(g + 1, 0)
                for b in (6, 7, 8):
                    split_context(g * B + b, b % 2)
                split_weights(g + 1, 1)
                split_weights(g + 1, 2)
                split_context(g * B + 9, 1, more=1)
                learned_key(g + 1)
                split_weights(g + 1, 3)
            for n in range(B * (NG3 - 1) + 2, steps):
                split_context(n, n % 2)

        @block.scalar
        def _(act):
            act.wait_ge(columns_in, 16)
            for m in range(4):
                act.wait_ge(raw_in[m % 2], 16 * (m // 2) + 16)
                nc.scalar.activation(wh[:, m, :], raw[:, m % 2, :], ACT.Copy).then_inc(weight_high, 1)
                if m == 1:
                    act.wait_ge(rows_out, 32)

            def exponentials(n):
                act.wait_ge(shift_ready, n)
                for h in range(G3):
                    nc.scalar.activation(probs[:, h, :], score[h][0:L, 0:SP], ACT.Exp, bias=shift[:, h:h + 1],
                                         scale=scale, accum_out=total[:, h:h + 1]).then_inc(exp_done, 1)

            def turned_tiles(at):
                for t in range(3):
                    rows = STILES[t][1] + (t == 2)
                    act.wait_ge(ring_full, at + U_T + t + 1)
                    nc.scalar.activation(pp[0:rows, t, 0, :], ring[t][0:rows, 0:G3 * L], ACT.Copy).then_inc(high_done, 1)

            def attended(n, filled):
                act.wait_ge(ring_full, filled)
                for h in range(G3):
                    last = nc.scalar.activation(mid[:, h, :], pair_parts(h // 2)[:, h % 2, 1, :], ACT.Identity, bias=column(2, n - 1, h))
                last.then_inc(part_kept, 1)
                act.wait_ge(mid_ready, n * 2)
                nc.scalar.activation(oh[:], mid[:], ACT.Copy).then_inc(high_done, 1)

            def step(n, i):
                at = before(n, i)
                if i:
                    exponentials(n)
                else:
                    act.wait_ge(bias_added, B)
                if i % BH == 0:
                    for h in range(G3):
                        act.wait_ge(ring_full, at + h + 1)
                        nc.scalar.activation(qh[:, h, :], ring[h][:, 0:HALF], ACT.Identity, bias=column(0, n, h)).then_inc(high_done, 1)
                    at = at + G3
                for h in range(G3):
                    act.wait_ge(ring_full, at + h + 1)
                    nc.scalar.activation(kh[:, h, 0:S], ring[h][:, 0:S], ACT.Identity, bias=column(1, n, h)).then_inc(
                        high_done, 1 if i or h < G3 - 1 else 1 + U_V - U_T)
                if i:
                    turned_tiles(at)
                    attended(n, at + FILLED[U_AV])
                for t in range(3):
                    rows = STILES[t][1]
                    act.wait_ge(ring_full, at + FILLED[U_V + t])
                    nc.scalar.activation(vh[0:rows, t, :], banks[BANK[U_V + t]][0:rows, :], ACT.Copy).then_inc(high_done, 1)
                if i % BH == 0:
                    row = STILES[2][1]
                    for part, values in enumerate((vh, vl)):
                        act.dma_start(values[row:row + 1, 2, :].bitcast(F32),
                                      scratch[part:part + 1].rearrange("a h k -> a (h k)")[:, bass.ds((n // B) * W, W)]).then_inc(extra_put, 16)

            def after(n):
                at = before(n, BH) - U_T
                exponentials(n)
                turned_tiles(at)
                attended(n, at + U_AV + 1)

            steps_of(act, step, after)

        @block.vector
        def _(dve):
            nc.vector.memset(mark[:, 0:1], 0.0).then_inc(added, ADDED0)
            dve.wait_ge(columns_in, 16)
            bias_k = columns[:].rearrange("p (h i) -> p h i", i=4)[:, :, 3]
            nc.vector.tensor_copy(keyh[:], bias_k).then_inc(key_high, 1)
            dve.wait_ge(key_high, 1)
            nc.vector.tensor_tensor(keyl[:], bias_k, keyh[:].bitcast(F32), ALU.subtract).then_inc(key_ready, 1)
            dve.wait_ge(rows_in, 16)
            nc.vector.tensor_tensor(vdiff, vrow[:, 0, :], vrow[:, 1, :], ALU.subtract).then_inc(diff_ready, 1)
            dve.wait_ge(diff_ready, 1)
            nc.vector.tensor_copy(vdh[:], vdiff).then_inc(diff_split, 1)
            dve.wait_ge(diff_split, 1)
            nc.vector.tensor_tensor(vdl[:], vdiff, vdh[:].bitcast(F32), ALU.subtract).then_inc(diff_split, 1)
            for m in range(4):
                dve.wait_ge(weight_high, m + 1)
                nc.vector.tensor_tensor(wl[:, m, :], raw[:, m % 2, :], wh[:, m, :].bitcast(F32), ALU.subtract).then_inc(weight_ready, 1)

            def shares(n):
                dve.wait_ge(exp_done, G3 * n)
                nc.vector.reciprocal(share[:], total[:]).then_inc(share_ready, 1)
                dve.wait_ge(share_ready, n)
                for h in range(G3):
                    nc.vector.tensor_scalar(probs[:, h, :], probs[:, h, :], share[:, h:h + 1], None, ALU.mult).then_inc(probs_ready, 1)

            def turned_tiles(at):
                for t in range(3):
                    rows = STILES[t][1] + (t == 2)
                    dve.wait_ge(high_done, at + U_T + t + 1)
                    nc.vector.tensor_tensor(pp[0:rows, t, 1, :], ring[t][0:rows, 0:G3 * L], pp[0:rows, t, 0, :].bitcast(F32),
                                            ALU.subtract).then_inc(bank_free, 1)

            def attended(n, at):
                dve.wait_ge(part_kept, n)
                for pair in range(2):
                    both = slice(2 * pair, 2 * pair + 2)
                    nc.vector.tensor_tensor(mid[:, both, :], mid[:, both, :], pair_parts(pair)[:, :, 0, :], ALU.add).then_inc(mid_ready, 1)
                dve.wait_ge(high_done, at + U_AV + 1)
                nc.vector.tensor_tensor(ol[:], mid[:], oh[:].bitcast(F32), ALU.subtract).then_inc(bank_free, 1)

            def add_output(n):
                dve.wait_ge(out_full, n)
                xb = X[:, bass.ds((n - 1) % B, 1), :].rearrange("p a c -> p (a c)")
                nc.vector.tensor_tensor(xb, xb, ring[0][0:L, :], ALU.add).then_inc(added, 1)

            def step(n, i):
                at = before(n, i)
                if i:
                    shares(n)
                else:
                    dve.wait_ge(bias_added, B)
                if i % BH == 0:
                    for h in range(G3):
                        dve.wait_ge(high_done, at + h + 1)
                        nc.vector.scalar_tensor_tensor(ql[:, h, :], ring[h][:, 0:HALF], column(0, n, h), qh[:, h, :].bitcast(F32),
                                                       ALU.add, ALU.subtract).then_inc(bank_free, 1)
                    at = at + G3
                for h in range(G3):
                    dve.wait_ge(high_done, at + h + 1)
                    nc.vector.scalar_tensor_tensor(kl[:, h, 0:S], ring[h][:, 0:S], column(1, n, h), kh[:, h, 0:S].bitcast(F32),
                                                   ALU.add, ALU.subtract).then_inc(bank_free, 1 if i or h < G3 - 1 else 1 + U_V - U_T)
                if i:
                    turned_tiles(at)
                    attended(n, at)
                for t in range(3):
                    rows = STILES[t][1]
                    dve.wait_ge(high_done, at + U_V + t + 1)
                    nc.vector.tensor_tensor(vl[0:rows, t, :], banks[BANK[U_V + t]][0:rows, :], vh[0:rows, t, :].bitcast(F32),
                                            ALU.subtract).then_inc(bank_free, 1)
                if i:
                    add_output(n)
                for h in range(G3):
                    dve.wait_ge(score_full, G3 * n + h + 1)
                    nc.vector.reduce_max(top[:, h:h + 1], score[h][0:L, 0:SP], AX_X).then_inc(top_done, 1)
                dve.wait_ge(top_done, G3 * n + G3)
                nc.vector.tensor_scalar(shift[:], top[:], -scale, None, ALU.mult).then_inc(shift_ready, 1)

            def after(n):
                at = before(n, BH) - U_T
                shares(n)
                turned_tiles(at)
                attended(n, at)
                add_output(n)

            steps_of(dve, step, after)

        @block.tensor
        def _(pe):
            def products(out, terms):
                count = 3 * len(terms)
                k = 0
                for (ah, al), (bh, bl) in terms:
                    for a, b in ((al, bh), (ah, bl), (ah, bh)):
                        last = nc.tensor.matmul(out, a, b, start=(k == 0), stop=(k == count - 1))
                        k += 1
                return last

            def weights_there(n, m):
                pe.wait_ge(weight_ready, (n // B) * 4 + m + 1)

            def queries(n, at):
                weights_there(n, 0)
                b0 = n % B
                for h in range(G3):
                    products(ring[h][:, 0:HALF].rearrange("p (b l) -> p b l", l=L), [
                        ((wh[:, 0, c * W + h * K3:c * W + (h + 1) * K3], wl[:, 0, c * W + h * K3:c * W + (h + 1) * K3]),
                         (highT[:, bass.ds(b0, BH), c, :], lowT[:, bass.ds(b0, BH), c, :])) for c in range(CC)]).then_inc(ring_full, 1)

            def turned_tiles(n, at):
                pe.wait_ge(probs_ready, G3 * n)
                for t in range(3):
                    pe.wait_ge(bank_free, at + t + 1)
                    s0 = STILES[t][0]
                    rows = STILES[t][1] + (t == 2)
                    for h in range(G3):
                        last = nc.tensor.transpose(ring[t][0:rows, h * L:(h + 1) * L],
                                                   probs[:, h, s0:s0 + rows], ident[0:L, 0:L])
                    last.then_inc(ring_full, 1)

            def attended(at, halves):
                pe.wait_ge(bank_free, at + U_AV)
                pe.wait_ge(extra_put, 32 * halves)
                for h in range(G3):
                    parts = pair_parts(h // 2)[:, h % 2]
                    for t, rows in ((0, P), (1, P), (2, STILES[2][1] + 1)):
                        nc.tensor.matmul(parts, vh[0:rows, t, h * K3:(h + 1) * K3], pp[0:rows, t, :, h * L:(h + 1) * L],
                                         start=(t == 0), stop=False)
                        last = nc.tensor.matmul(parts[:, 0, :], vl[0:rows, t, h * K3:(h + 1) * K3], pp[0:rows, t, 0, h * L:(h + 1) * L],
                                                start=False, stop=(t == 2))
                last.then_inc(ring_full, 1)

            def output(n, at):
                pe.wait_ge(bank_free, at + U_AV + 1)
                weights_there(n - 1, 3)
                products(ring[0][0:L, :], [
                    ((oh[:, h, :], ol[:, h, :]), (wh[:, 3, h * C:(h + 1) * C], wl[:, 3, h * C:(h + 1) * C]))
                    for h in range(G3)]).then_inc(out_full, 1)

            def step(n, i):
                parity = i % 2
                at = before(n, i)
                last_use = (at - 3, at - 3, at - 1, at)
                if i:
                    pe.wait_ge(added, n - 1 + ADDED0)
                if i % BH == 0:
                    if i:
                        pe.wait_ge(bank_free, at)
                    queries(n, at)
                    last_use = (at + 1, at + 2, at + 3, at + 4)
                    at = at + G3
                weights_there(n, 1)
                pe.wait_ge(ctx_ready, n + 1)
                for h in range(G3):
                    if i or i % BH == 0:
                        pe.wait_ge(bank_free, last_use[h])
                    products(ring[h][:, 0:SP], [
                        ((wh[:, 1, c * W + h * K3:c * W + (h + 1) * K3], wl[:, 1, c * W + h * K3:c * W + (h + 1) * K3]),
                         (ch[:, parity, c, :], cl[:, parity, c, :])) for c in range(CC)]).then_inc(
                             ring_full, 1 if i or h < G3 - 1 else 1 + U_V - U_T - 1)

                def value_tile(t, count=1):
                    if t == 1:
                        pe.wait_ge(bank_free, at + (U_T + 3 if i else 3))
                    if t == 2:
                        pe.wait_ge(bank_free, at + 4)
                    s0, rows = STILES[t]
                    products(banks[BANK[U_V + t]][0:rows, :], [
                        ((ch[:, parity, c, s0:s0 + rows], cl[:, parity, c, s0:s0 + rows]),
                         (wh[:, 2, c * W:(c + 1) * W], wl[:, 2, c * W:(c + 1) * W])) for c in range(CC)]).then_inc(ring_full, count)

                if i:
                    turned_tiles(n, at)
                weights_there(n, 2)
                value_tile(0, 1 if i else 2)
                if i:
                    attended(at, (n - i) // BH + 1)
                value_tile(1)
                value_tile(2)
                if i:
                    output(n, at)
                pe.wait_ge(keyx_ready, (n // B) * 2 + 2)
                j = i % BH
                pe.wait_ge(bank_free, at + U_V + 1)
                for h in range(G3):
                    products(score[h][0:L, 0:SP], [((qh[:, h, j * L:(j + 1) * L], ql[:, h, j * L:(j + 1) * L]),
                                                    (kh[:, h, :], kl[:, h, :]))]).then_inc(score_full, 1)

            def after(n):
                at = before(n, BH)
                pe.wait_ge(bank_free, at)
                turned_tiles(n, at - U_T)
                attended(at - U_T, steps // BH)
                output(n, at - U_T)

            steps_of(pe, step, after)


def add_row(nc, prefix, X, row):
    with Scope(nc, prefix) as sc:
        bias = sc.sb("bias", [L, C])
        bias_in, done = sc.sem("bias_in"), sc.sem("done")
        block = sc.block()

        @block.sync
        def _(sp):
            sp.dma_start(bias[:], row).then_inc(bias_in, 16)

        @block.vector
        def _(dve):
            dve.wait_ge(bias_in, 16)
            for b in range(B):
                nc.vector.tensor_tensor(X[:, b, :], X[:, b, :], bias[:], ALU.add).then_inc(done, 1)
            dve.wait_ge(done, B)


def mlp(nc, a, X, ident, column):
    FH = F3 // 2
    FT = FH // P
    PARTS = 2
    with Scope(nc, "mlp") as sc:
        highT = sc.sb("highT", [P, B, CC, L], F32R)
        lowT = sc.sb("lowT", [P, B, CC, L], F32R)
        raw = [sc.sb(f"raw{i}", [P, CC * FH]) for i in range(2)]
        raw_in = [sc.sem(f"raw_in{i}") for i in range(2)]
        fc1 = a["L3_xattn_w_fc1"].rearrange("(c p) n -> p c n", p=P)
        fc2 = a["L3_xattn_w_fc2"].rearrange("(c p) n -> p c n", p=P)

        def loads(part):
            return [(raw[0][:].rearrange("p (c n) -> p c n", c=CC), fc1[:, :, part * FH:(part + 1) * FH]),
                    (raw[1][:].rearrange("p (c n) -> p c n", c=FT), fc2[:, part * FT:(part + 1) * FT, :])]

        bias = sc.sb("bias", [P, PARTS * FT])
        row = sc.sb("row", [L, C])
        small_in = sc.sem("small_in")
        start_copies(nc, "mlpa", raw_in[0], loads(0)[0:1])
        start_copies(nc, "mlpb", raw_in[1], loads(0)[1:2])
        start_copies(nc, "mlpc", small_in, [(bias[:], a["fc1_columns"]), (row[:], a["fc2_rows"])])
        layer_norm_transposed(nc, "lnm", X, 1e-5, column("L3_xattn_ln_mlp_scale"), column("L3_xattn_ln_mlp_offset"),
                              ident, lambda b: (highT[:, b], lowT[:, b]), "split")
        wh = [sc.sb(f"wh{i}", [P, CC * FH], F32R) for i in range(2)]
        wl = [sc.sb(f"wl{i}", [P, CC * FH], F32R) for i in range(2)]
        act32 = sc.sb("act32", [P, 2, HALF])
        fh, fl = sc.sb("fh", [P, 2 * FT, HALF], F32R), sc.sb("fl", [P, 2 * FT, HALF], F32R)
        ring = [sc.bank(f"ring{i}") for i in range(RING)]
        outs = [sc.bank(f"outs{i}") for i in range(2)]
        (high_w, weight_ready, full, gelu_done, high_done, low_done, out_full, row_added, added) = (
            sc.sem(n) for n in ("high_w", "weight_ready", "full", "gelu_done", "high_done", "low_done", "out_full",
                                "row_added", "added"))
        HIDDEN = 2 * FT
        PIECES = 2
        FP = FT // PIECES
        block = sc.block()

        def pieces(t, m):
            if m == 0:
                full_view = t.rearrange("p (c n) -> p c n", c=CC)
                return [full_view[:, :, i * FP * P:(i + 1) * FP * P] for i in range(PIECES)]
            return [t[:, i * FP * C:(i + 1) * FP * C] for i in range(PIECES)]

        @block.sync
        def _(sp):
            for part in range(1, PARTS):
                for m in range(2):
                    sp.wait_ge(weight_ready, PIECES * (2 * (part - 1) + m + 1))
                    sp.dma_start(*loads(part)[m]).then_inc(raw_in[m], 16)

        @block.gpsimd
        def _(pool):
            pool.wait_ge(small_in, 32)
            for b in range(B):
                nc.gpsimd.tensor_tensor(X[:, b, :], X[:, b, :], row[:], ALU.add).then_inc(row_added, 1)

        @block.scalar
        def _(act):
            def high(part, m):
                act.wait_ge(raw_in[m], 16 * part + 16)
                if part:
                    act.wait_ge((full, out_full)[m], (HIDDEN, B)[m] * part)
                for dst, src in zip(pieces(wh[m][:], m), pieces(raw[m][:], m)):
                    nc.scalar.activation(dst, src, ACT.Copy).then_inc(high_w, 1)

            act.wait_ge(small_in, 32)
            high(0, 0)
            for part in range(PARTS):
                for u in range(HIDDEN):
                    n = HIDDEN * part + u
                    act.wait_ge(full, n + 1)
                    if n >= 2:
                        act.wait_ge(low_done, n - 1)
                    f = FT * part + u % FT
                    nc.scalar.activation(act32[:, u % 2, :], ring[u % RING][:, 0:HALF], ACT.Gelu,
                                         bias=bias[:, f:f + 1]).then_inc(gelu_done, 1)
                    if u == 1:
                        high(part, 1)
                if part + 1 < PARTS:
                    high(part + 1, 0)

        @block.vector
        def _(dve):
            def low(part, m):
                for i, (dst, src, rounded) in enumerate(zip(pieces(wl[m][:], m), pieces(raw[m][:], m), pieces(wh[m][:], m))):
                    dve.wait_ge(high_w, PIECES * (2 * part + m) + i + 1)
                    nc.vector.tensor_tensor(dst, src, rounded.bitcast(F32), ALU.subtract).then_inc(weight_ready, 1)

            low(0, 0)
            for part in range(PARTS):
                for u in range(HIDDEN):
                    n = HIDDEN * part + u
                    dve.wait_ge(gelu_done, n + 1)
                    if part and u % FT == 0:
                        dve.wait_ge(out_full, B * (part - 1) + (B // 2) * (u // FT + 1))
                    nc.vector.tensor_copy(fh[:, u, :], act32[:, u % 2, :]).then_inc(high_done, 1)
                    dve.wait_ge(high_done, n + 1)
                    nc.vector.tensor_tensor(fl[:, u, :], act32[:, u % 2, :], fh[:, u, :].bitcast(F32),
                                            ALU.subtract).then_inc(low_done, 1)
                    if u == 1:
                        low(part, 1)
                if part == 0:
                    dve.wait_ge(row_added, B)
                if part + 1 < PARTS:
                    low(part + 1, 0)
                for b in range(B):
                    k = B * part + b
                    dve.wait_ge(out_full, k + 1)
                    if k >= B:
                        dve.wait_ge(added, k - B + 1)
                    nc.vector.tensor_tensor(X[:, b, :], X[:, b, :], outs[b % 2][0:L, :], ALU.add).then_inc(added, 1)

        @block.tensor
        def _(pe):
            def products(out, terms):
                k = 0
                for (ah, al), (bh, bl) in terms:
                    for x, y in ((al, bh), (ah, bl), (ah, bh)):
                        last = nc.tensor.matmul(out, x, y, start=(k == 0), stop=(k == 3 * len(terms) - 1))
                        k += 1
                return last

            for part in range(PARTS):
                for half in range(2):
                    for f in range(FT):
                        n = HIDDEN * part + FT * half + f
                        pe.wait_ge(weight_ready, PIECES * 2 * part + f // FP + 1)
                        if n >= RING:
                            pe.wait_ge(gelu_done, n - RING + 1)
                        products(ring[n % RING][:, 0:HALF].rearrange("p (b l) -> p b l", l=L), [
                            ((wh[0][:, c * FH + f * P:c * FH + (f + 1) * P], wl[0][:, c * FH + f * P:c * FH + (f + 1) * P]),
                             (highT[:, 4 * half:4 * half + 4, c, :], lowT[:, 4 * half:4 * half + 4, c, :]))
                            for c in range(CC)]).then_inc(full, 1)
                pe.wait_ge(weight_ready, PIECES * (2 * part + 2))
                for b in range(B):
                    k = B * part + b
                    half, j = b // (B // 2), b % (B // 2)
                    pe.wait_ge(low_done, HIDDEN * part + FT * (half + 1))
                    if k >= 2:
                        pe.wait_ge(added, k - 1)
                    products(outs[b % 2][0:L, :], [
                        ((fh[:, FT * half + f, j * L:(j + 1) * L], fl[:, FT * half + f, j * L:(j + 1) * L]),
                         (wh[1][:, f * C:(f + 1) * C], wl[1][:, f * C:(f + 1) * C])) for f in range(FT)]).then_inc(out_full, 1)


def load_state(nc, X, x_dram, ident, ident_dram, columns, columns_dram):
    with Scope(nc, "load") as sc:
        come = sc.sem("come")
        block = sc.block()

        @block.sync
        def _(sp):
            sp.dma_start(X[:], x_dram.rearrange("b l c -> l b c")).then_inc(come, 16)
            sp.dma_start(ident[:], ident_dram).then_inc(come, 16)
            sp.dma_start(columns[:], columns_dram).then_inc(come, 16)
            sp.wait_ge(come, 48)


def store_state(nc, X, out, gone):
    with Scope(nc, "store") as sc:
        block = sc.block()

        @block.sync
        def _(sp):
            sp.dma_start(out.rearrange("b l c -> l b c"), X[:]).then_inc(gone, 16)
            sp.wait_ge(gone, 16)


def attention_block(nc, a, X, ident, column, i):
    weights = [a[f"L3_xattn_w{w}{i}"] for w in "qkvo"]
    with Scope(nc, f"att{i}") as sc:
        highT = sc.sb("highT", [P, B, CC, L], F32R)
        lowT = sc.sb("lowT", [P, B, CC, L], F32R)
        raw = sc.sb("raw", [P, 2, CC * W3])
        craw = sc.sb("craw", [P, CC, SP])
        raw_in = [sc.sem(f"raw_in{k}") for k in range(2)]
        ctx_in = sc.sem("ctx_in")
        with Scope(nc, f"fetch{i}") as fetch:
            block = fetch.block()

            @block.sync
            def _(sp):
                load_group(sp, raw, weights[0], 0, 0).then_inc(raw_in[0], 16)
                sp.dma_start(craw[:], a["ctxT"][0]).then_inc(ctx_in, 16)
                load_group(sp, raw, weights[1], 1, 0).then_inc(raw_in[1], 16)

        layer_norm_transposed(nc, f"ln{i}", X, 1e-5, column(f"L3_xattn_ln{i}_scale"), column(f"L3_xattn_ln{i}_offset"),
                              ident, lambda b: (highT[:, b], lowT[:, b]), "split")
        cross_attention(nc, f"ca{i}", X, highT, lowT, a["ctxT"], weights, a[f"head_columns{i}"], a[f"value_rows{i}"], a[f"bo{i}_rows"],
                        nc.dram_tensor(f"value_parts{i}", (2, H3, K3), F32).ap(), ident, raw, craw, raw_in, ctx_in)


def program(nc, a, out):
    output_gone = nc.alloc_semaphore("output_gone")
    with Scope(nc, "state") as sc:
        X = sc.sb("X", [L, B, C])
        ident = sc.sb("ident", [P, P])
        columns = sc.sb("columns", [P, len(COLUMNS), CC])

        def column(name):
            return columns[:, COLUMNS.index(name), :]

        load_state(nc, X, a["x"], ident, a["ident"], columns, a["columns"])
        gqa_layer(nc, a, X, ident, column)
        clear_semaphores(nc)
        rwkv_layer(nc, a, X, ident, column)
        clear_semaphores(nc)
        plain_attention_layer(nc, a, X, ident)
        clear_semaphores(nc)
        attention_block(nc, a, X, ident, column, 1)
        clear_semaphores(nc)
        attention_block(nc, a, X, ident, column, 2)
        clear_semaphores(nc)
        mlp(nc, a, X, ident, column)
        store_state(nc, X, out, output_gone)
        Scope.retired.append(output_gone)
        clear_semaphores(nc)


COLUMNS = ["L3_xattn_ln1_scale", "L3_xattn_ln1_offset", "L3_xattn_ln2_scale", "L3_xattn_ln2_offset",
           "L3_xattn_ln_mlp_scale", "L3_xattn_ln_mlp_offset",
           "L1_xattn_ln1_w", "L1_xattn_ln1_b", "L1_xattn_ln2_w", "L1_xattn_ln2_b",
           "L1_xattn_maa_x", "L1_xattn_maa_w", "L1_xattn_maa_k", "L1_xattn_maa_v", "L1_xattn_maa_r", "L1_xattn_maa_g",
           "L1_xattn_time_decay", "L1_xattn_faaaa", "L1_xattn_gn_w", "L1_xattn_gn_b",
           "L1_xattn_fmaa_k", "L1_xattn_fmaa_r", "L0_bq"]


def lay_out(inputs):
    import numpy as np

    def rows(v):
        return np.repeat(np.asarray(v).reshape(1, -1), L, axis=0)

    f = {k: np.asarray(v) for k, v in inputs.items()}
    a = {"x": f["x"], "ident": np.eye(P, dtype=np.float32)}
    ctx = f["ctx_2048"]
    ctxT = ctx.transpose(0, 2, 1).reshape(B, CC, P, S).transpose(0, 2, 1, 3)
    a["ctxT"] = np.pad(ctxT, ((0, 0), (0, 0), (0, 0), (0, SP - S)))
    a["columns"] = np.stack([f[n if n in f else "L0_xattn_bq"].reshape(CC, P).T for n in COLUMNS], axis=1)
    for i in (1, 2):
        for w in "qkvo":
            a[f"L3_xattn_w{w}{i}"] = f[f"L3_xattn_w{w}{i}"]
        a[f"bo{i}_rows"] = rows(f[f"L3_xattn_bo{i}"])
        a[f"head_columns{i}"] = np.stack([f[f"L3_xattn_{n}{i}"].reshape(H3, K3).T for n in ("bq", "bk", "bv", "bias_k")],
                                         axis=2).reshape(P, H3 * 4)
        a[f"value_rows{i}"] = np.stack([f[f"L3_xattn_{n}{i}"].reshape(H3, K3) for n in ("bias_v", "bv")], axis=1)
    order = np.arange(C).reshape(KV0, CC, D0).transpose(1, 0, 2).reshape(C)
    a["L0_Wq"], a["L0_Wv"], a["L0_Wo"] = f["L0_xattn_Wq"][:, order], f["L0_xattn_Wv"], f["L0_xattn_Wo"][order]
    a["L0_Wk"], a["L0_bk"] = f["L0_xattn_Wk"], f["L0_xattn_bk"].reshape(P, 1)
    a["L0_bv"] = np.repeat(f["L0_xattn_bv"].reshape(1, -1), P, axis=0)
    a["columns"][:, COLUMNS.index("L0_bq")] = f["L0_xattn_bq"][order].reshape(CC, P).T
    a["heads_of"] = (np.arange(P)[:, None] // D0 == np.arange(HC)[None, :]).astype(np.float32)
    a["mask"] = f["mask_Bx1xSxS2_ff0"][:, 0]
    a["L0_bo"], a["L0_gamma"], a["L0_beta"] = (rows(f[f"L0_xattn_{n}"]) for n in ("bo", "gamma", "beta"))
    for n in ("Wk", "Wv", "Wr", "Wg", "Wo", "fWk", "fWr", "fWv"):
        a[f"L1_{n}T"] = f[f"L1_xattn_{n}"].T
    a["L1_maa_w1"], a["L1_maa_w2"] = f["L1_xattn_maa_w1"], f["L1_xattn_maa_w2"].reshape(5 * 32, C)
    a["L1_decay_w1"], a["L1_decay_w2"] = f["L1_xattn_decay_w1"], f["L1_xattn_decay_w2"]
    a["before"] = ctx[:, 0:2, :].reshape(B, 2, CC, P).transpose(3, 1, 0, 2)
    a["first"] = ctx[:, 2:2 + HD, :].reshape(B, CC, P, HD).transpose(0, 2, 3, 1)
    spread = np.zeros((P, HD, P), np.float32)
    for p in range(P):
        for j in range(HD):
            spread[p // HD * HD + j, j, p] = 1.0
    a["spread"], a["gather"] = spread, spread.transpose(2, 1, 0)
    head = np.arange(P) // HD
    a["blocks"] = (head[:, None] == head[None, :]).astype(np.float32)
    a["means"] = a["blocks"] / np.float32(HD)
    a["ctx"] = ctx
    a["L2_w_qT"], a["L2_w_k"] = f["L2_xattn_w_q"].T, f["L2_xattn_w_k"]
    a["L2_w_vT"], a["L2_w_oT"] = f["L2_xattn_w_v"].T, f["L2_xattn_w_o"].T
    a["alpha_rows"] = np.repeat(f["L2_xattn_alpha"].reshape(1, 1), L, axis=0)
    a["L3_xattn_w_fc1"], a["L3_xattn_w_fc2"] = f["L3_xattn_w_fc1"], f["L3_xattn_w_fc2"]
    a["fc1_columns"] = f["L3_xattn_b_fc1"].reshape(F3 // P, P).T
    a["fc2_rows"] = rows(f["L3_xattn_b_fc2"])
    return {k: np.ascontiguousarray(v) for k, v in a.items()}


def kernel(**inputs):
    import concourse.bacc as bacc
    from concourse.bass_utils import run_bass_kernel_spmd

    nc = bacc.Bacc("TRN2", target_bir_lowering=False, num_devices=1)
    arrays = {f"in_{k}": v for k, v in lay_out(inputs).items()}
    a = {k[3:]: nc.dram_tensor(k, v.shape, mybir.dt.from_np(v.dtype), kind="ExternalInput").ap() for k, v in arrays.items()}
    out = nc.dram_tensor("out", (B, L, C), F32, kind="ExternalOutput").ap()
    program(nc, a, out)
    r = run_bass_kernel_spmd(nc, [arrays], core_ids=[0])
    return r.results[0]["out"]
```
